# Optimizing a Trainium2 kernel written in Bass

```python
import numpy as np
import jax
import jax.numpy as jnp

def _softmax(x, axis=-1):
    return jax.nn.softmax(x, axis=axis)

def _gelu(x):
    return jax.nn.gelu(x, approximate=True)

def _silu(x):
    return jax.nn.silu(x)

def _sigmoid(x):
    return jax.nn.sigmoid(x)

def _layernorm(x, axis=-1, eps=1e-05):
    m = jnp.mean(x, axis=axis, keepdims=True)
    v = jnp.var(x, axis=axis, keepdims=True)
    return (x - m) / jnp.sqrt(v + eps)

def _scatter_add(tgt, idx, src, axis=0):
    return tgt.at[idx].add(src)

def _segment_sum(src, seg, n):
    return jax.ops.segment_sum(src, seg, n)
kernel_name = 'mk_macaron_d1_jaxref_r4_b20df0'

def setup_inputs(seed: int=0):
    np.random.seed(seed)
    _w = jnp.asarray

    def _L0_attn_setup():
        import jax, jax.numpy as jnp
        import numpy as np
        DIM = 512
        N_HEADS = 16
        HEAD_DIM = DIM // N_HEADS
        GROUP_SIZE = 128
        THRESHOLD = 0.5
        EPS = 1e-08
        B, T = (2, 512)

        def _ternary_dequant(w):
            O, I = w.shape
            g = I // GROUP_SIZE
            wg = w.reshape(O, g, GROUP_SIZE)
            scale = jnp.clip(jnp.mean(jnp.abs(wg), axis=-1, keepdims=True), EPS)
            wn = wg / scale
            q = jnp.where(wn > THRESHOLD, 1.0, jnp.where(wn < -THRESHOLD, -1.0, 0.0))
            return (q * scale).reshape(O, I)

        def _bitlinear(x, w):
            w_ste = w + jax.lax.stop_gradient(_ternary_dequant(w) - w)
            return x @ w_ste.T

        def _rope_tables(t, head_dim, base=10000.0):
            half = head_dim // 2
            inv_freq = 1.0 / base ** (jnp.arange(half, dtype=jnp.float32) / half)
            freqs = jnp.outer(jnp.arange(t, dtype=jnp.float32), inv_freq)
            return (jnp.cos(freqs), jnp.sin(freqs))

        def _apply_rope(x, cos, sin):
            d = x.shape[-1]
            x1, x2 = (x[..., :d // 2], x[..., d // 2:])
            cos = cos[None, None, :, :]
            sin = sin[None, None, :, :]
            return jnp.concatenate([x1 * cos - x2 * sin, x1 * sin + x2 * cos], axis=-1)
        key = jax.random.key(seed)
        ks = jax.random.split(key, 5)
        std = 1.0 / np.sqrt(DIM)
        return {'x': jax.random.normal(ks[0], (B, T, DIM), dtype=jnp.float32), 'w_q': jax.random.normal(ks[1], (DIM, DIM), dtype=jnp.float32) * std, 'w_k': jax.random.normal(ks[2], (DIM, DIM), dtype=jnp.float32) * std, 'w_v': jax.random.normal(ks[3], (DIM, DIM), dtype=jnp.float32) * std, 'w_o': jax.random.normal(ks[4], (DIM, DIM), dtype=jnp.float32) * std}
    _L0_attn_in = _L0_attn_setup()

    def _L0_ffn_setup():
        import jax, jax.numpy as jnp
        import numpy as np
        IN_F, OUT_F = (512, 512)
        N_EXPERTS, RANK, TOP_K = (8, 128, 2)
        key = jax.random.key(seed)
        k_x, k_r, k_a, k_b = jax.random.split(key, 4)
        hidden_states = jax.random.normal(k_x, (4, 1024, IN_F), dtype=jnp.float32)
        router_w = jax.random.normal(k_r, (IN_F, N_EXPERTS), dtype=jnp.float32) * IN_F ** (-0.5)
        Wa = jax.random.normal(k_a, (N_EXPERTS, IN_F, RANK), dtype=jnp.float32) * IN_F ** (-0.5)
        Wb = jax.random.normal(k_b, (N_EXPERTS, RANK, OUT_F), dtype=jnp.float32) * RANK ** (-0.5)
        return {'hidden_states': hidden_states, 'router_w': router_w, 'Wa': Wa, 'Wb': Wb}
    _L0_ffn_in = _L0_ffn_setup()
    _d = {'L0_attn_x': _L0_attn_in['x'], 'L0_attn_w_q': _L0_attn_in['w_q'], 'L0_attn_w_k': _L0_attn_in['w_k'], 'L0_attn_w_v': _L0_attn_in['w_v'], 'L0_attn_w_o': _L0_attn_in['w_o'], 'L0_ffn_router_w': _L0_ffn_in['router_w'], 'L0_ffn_Wa': _L0_ffn_in['Wa'], 'L0_ffn_Wb': _L0_ffn_in['Wb']}
    _x0 = _d['L0_attn_x']
    _d['L0_attn_x'] = jax.random.normal(jax.random.fold_in(jax.random.key(seed), 1), (8, 1024, 512), dtype=_x0.dtype)
    del _x0
    return _d

def reference(L0_attn_x, L0_attn_w_q, L0_attn_w_k, L0_attn_w_v, L0_attn_w_o, L0_ffn_router_w, L0_ffn_Wa, L0_ffn_Wb):

    def _L0_attn_ref(x, w_q, w_k, w_v, w_o):
        import jax, jax.numpy as jnp
        import numpy as np
        DIM = 512
        N_HEADS = 16
        HEAD_DIM = DIM // N_HEADS
        GROUP_SIZE = 128
        THRESHOLD = 0.5
        EPS = 1e-08
        B, T = (2, 512)

        def _ternary_dequant(w):
            O, I = w.shape
            g = I // GROUP_SIZE
            wg = w.reshape(O, g, GROUP_SIZE)
            scale = jnp.clip(jnp.mean(jnp.abs(wg), axis=-1, keepdims=True), EPS)
            wn = wg / scale
            q = jnp.where(wn > THRESHOLD, 1.0, jnp.where(wn < -THRESHOLD, -1.0, 0.0))
            return (q * scale).reshape(O, I)

        def _bitlinear(x, w):
            w_ste = w + jax.lax.stop_gradient(_ternary_dequant(w) - w)
            return x @ w_ste.T

        def _rope_tables(t, head_dim, base=10000.0):
            half = head_dim // 2
            inv_freq = 1.0 / base ** (jnp.arange(half, dtype=jnp.float32) / half)
            freqs = jnp.outer(jnp.arange(t, dtype=jnp.float32), inv_freq)
            return (jnp.cos(freqs), jnp.sin(freqs))

        def _apply_rope(x, cos, sin):
            d = x.shape[-1]
            x1, x2 = (x[..., :d // 2], x[..., d // 2:])
            cos = cos[None, None, :, :]
            sin = sin[None, None, :, :]
            return jnp.concatenate([x1 * cos - x2 * sin, x1 * sin + x2 * cos], axis=-1)
        b, t, c = x.shape
        scale = HEAD_DIM ** (-0.5)

        def split_heads(y):
            return y.reshape(b, t, N_HEADS, HEAD_DIM).transpose(0, 2, 1, 3)
        q = split_heads(_bitlinear(x, w_q))
        k = split_heads(_bitlinear(x, w_k))
        v = split_heads(_bitlinear(x, w_v))
        cos, sin = _rope_tables(t, HEAD_DIM)
        q = _apply_rope(q, cos, sin)
        k = _apply_rope(k, cos, sin)
        scores = jnp.einsum('bhqd,bhkd->bhqk', q, k) * scale
        causal = jnp.triu(jnp.ones((t, t), dtype=bool), k=1)
        scores = jnp.where(causal[None, None], -jnp.inf, scores)
        probs = jax.nn.softmax(scores, axis=-1)
        y = jnp.einsum('bhqk,bhkd->bhqd', probs, v)
        y = y.transpose(0, 2, 1, 3).reshape(b, t, c)
        return _bitlinear(y, w_o)

    def _L0_ffn_ref(hidden_states, router_w, Wa, Wb):
        import jax, jax.numpy as jnp
        import numpy as np
        IN_F, OUT_F = (512, 512)
        N_EXPERTS, RANK, TOP_K = (8, 128, 2)
        B, S, D = hidden_states.shape
        x = hidden_states.reshape(-1, D)
        norm = jnp.maximum(jnp.linalg.norm(x, axis=-1, keepdims=True), 1e-12)
        router_logits = x / norm @ router_w
        routing_weights = jax.nn.softmax(router_logits.astype(jnp.float32), axis=-1)
        rw, selected_experts = jax.lax.top_k(routing_weights, TOP_K)
        rw = rw / jnp.sum(rw, axis=-1, keepdims=True)
        rw = rw.astype(hidden_states.dtype)
        combine = jnp.sum(jax.nn.one_hot(selected_experts, N_EXPERTS, dtype=rw.dtype) * rw[..., None], axis=1)
        out = jnp.zeros((x.shape[0], OUT_F), dtype=hidden_states.dtype)
        for e in range(N_EXPERTS):
            out = out + combine[:, e, None] * (x @ Wa[e] @ Wb[e])
        return out.reshape(B, S, OUT_F)
    x = L0_attn_x
    x = x + 0.5 * _L0_ffn_ref(_layernorm(x, axis=-1), L0_ffn_router_w, L0_ffn_Wa, L0_ffn_Wb)
    x = x + _L0_attn_ref(_layernorm(x, axis=-1), L0_attn_w_q, L0_attn_w_k, L0_attn_w_v, L0_attn_w_o)
    x = x + 0.5 * _L0_ffn_ref(_layernorm(x, axis=-1), L0_ffn_router_w, L0_ffn_Wa, L0_ffn_Wb)
    return x

_drawn_inputs = setup_inputs


def setup_inputs(seed=0):
    import zlib

    import numpy as np

    out = dict(_drawn_inputs(seed))
    spreads = {}
    factors = {}
    for name, (base, spread) in spreads.items():
        noise = np.random.default_rng([zlib.crc32(name.encode()), seed]).standard_normal(out[name].shape)
        drawn = base * np.exp(spread * noise) if base else spread * noise
        out[name] = jnp.asarray(drawn.astype(out[name].dtype))
    for name, factor in factors.items():
        out[name] = (out[name] * factor).astype(out[name].dtype)
    return out
```

```python
from contextlib import ExitStack

import numpy as np
import concourse.bass as bass
from concourse import mybir

ALU = mybir.AluOpType
ACT = mybir.ActivationFunctionType
AX = mybir.AxisListType
F32 = mybir.dt.float32
F32R = mybir.dt.float32r
BF16 = mybir.dt.bfloat16

P = 128
D = 512
KT = D // P
NE = 8
RANK = 128
TB = 512
TT = TB // P
LN_EPS = 1e-5
NORM_MIN = 1e-12
BIG = 1e30


class Block2:

    def __init__(self, pair, parity):
        self.pair, self.parity = pair, parity

    def at(self, k, c):
        return self.pair * (2 * k) + (self.parity * k + c)

    def next(self):
        return Block2(self.pair, 1) if self.parity == 0 else Block2(self.pair + 1, 0)

    def index(self):
        return self.pair * 2 + self.parity


def each_block(engine, nblocks, body):
    last = nblocks // 2 - 1
    with engine.Fori(0, last) as pair:
        body(Block2(pair, 0), True, True)
        body(Block2(pair, 1), True, True)
    body(Block2(last, 0), True, False)
    body(Block2(last, 1), False, False)


def ffn_phase(nc, psum, tag, nblocks, x_src, x_dst, w_router, w_a, w_b, moments_dst=None, y_src=None, w_o=None):
    with_o = y_src is not None
    HS = 2
    STAGES = 1 if with_o else 4
    STORES = 16 * (1 if moments_dst is None else 2)
    LAG = 1 if with_o else 0
    with ExitStack() as ctx:
        def sb(name, shape, dt):
            return ctx.enter_context(nc.sbuf_tensor(f"{tag}_{name}", shape, dt))

        def sem(name):
            return ctx.enter_context(nc.semaphore(f"{tag}_{name}"))

        ident = sb("ident", [P, P], F32)
        eps_col = sb("eps_col", [P, 1], F32)
        zero_col = sb("zero_col", [P, 1], F32)
        wa = sb("wa", [P, KT, 2, NE * RANK], F32R)
        wb = sb("wb", [P, NE, 2, D], F32R)
        wr = sb("wr", [P, KT, 4, NE], F32R)
        wr_raw = sb("wr_raw", [P, KT, NE], F32)
        fold = sb("fold", [2 * NE, NE], F32)
        first_w = sb("first_w", [P, TT, NE], F32)
        x = sb("x", [P, 2, TT, D], F32)
        xn = sb("xn", [P, TT, D], F32)
        xh = sb("xh", [P, KT, TB], F32R)
        xl = sb("xl", [P, KT, TB], F32R)
        hs = sb("hs", [P, HS, TB], F32)
        hh = sb("hh", [P, NE, TB], F32R)
        hl = sb("hl", [P, NE, TB], F32R)
        cb = sb("cb", [P, 2, TB], F32)
        stage = sb("stage", [P, STAGES, 2 * D], F32)
        lg = sb("lg", [2 * NE, TB], F32)
        cm = sb("cm", [P, TT, P], F32R)
        own_tile = sb("own_tile", [P, TT], F32)
        rows_of = sb("rows_of", [P, 2 * NE], F32)
        spread = sb("spread", [P, NE, P], F32R)
        stats = sb("stats", [P, TT, 6], F32)
        mv = sb("mv", [P, TT, 2], F32)
        root = sb("root", [P, 2, TT], F32)
        inv0 = sb("inv0", [P, TT], F32)
        newton = sb("newton", [P, TT], F32)
        rstd = sb("rstd", [P, TT], F32)
        norm = sb("norm", [P, TT], F32)
        inv_norm = sb("inv_norm", [P, TT], F32)
        logit = sb("logit", [P, TT, NE], F32)
        hit = sb("hit", [P, TT, NE], F32)
        score = sb("score", [P, TT, NE], F32)
        top = [sb(f"top{i}", [P, TT, NE], F32) for i in range(2)]
        peak = sb("peak", [P, 2, TT], F32)
        who = sb("who", [P, TT], F32)
        gap = sb("gap", [P, TT], F32)
        ratio = sb("ratio", [P, TT], F32)
        gate = sb("gate", [P, 2, TT], F32)
        total = sb("total", [P, TT], F32)
        comb = sb("comb", [P, NE, TT], F32)
        comb_parts = sb("comb_parts", [P, 4, NE, TT], F32R)
        if moments_dst is not None:
            out_stats = sb("out_stats", [P, 2, TT, 6], F32)
        if with_o:
            wo = sb("wo", [P, KT, 2, D], F32R)
            yt = sb("yt", [P, KT, TB], F32)
            yh = sb("yh", [P, KT, TB], F32R)
            yl = sb("yl", [P, KT, TB], F32R)

        banks = [psum[:, i] for i in range(8)]
        t_bank, h_bank, o_bank, m_bank = banks[0:2], banks[2:5], banks[5:7], banks[7]

        zeroed = sem("zeroed")
        consts_ready = sem("consts_ready")
        w_loaded = [sem(f"w_loaded{s}") for s in range(STAGES)]
        w_hi = sem("w_hi")
        w_lo = sem("w_lo")
        wr_loaded = sem("wr_loaded")
        wr_step = sem("wr_step")
        x_loaded = [sem("x_loaded0"), sem("x_loaded1")]
        x_stored = [sem("x_stored0"), sem("x_stored1")]
        dve_step = sem("dve_step")
        stats_ready = sem("stats_ready")
        var_ready = sem("var_ready")
        root_ready = sem("root_ready")
        xn_ready = sem("xn_ready")
        t_filled = sem("t_filled")
        xh_ready = sem("xh_ready")
        xl_ready = sem("xl_ready")
        lg_filled = sem("lg_filled")
        lg_copied = sem("lg_copied")
        lt_filled = sem("lt_filled")
        gap_ready = sem("gap_ready")
        ratio_ready = sem("ratio_ready")
        comb_ready = sem("comb_ready")
        ct_filled = sem("ct_filled")
        cm_ready = sem("cm_ready")
        cb_filled = sem("cb_filled")
        cb_ready = sem("cb_ready")
        h_filled = sem("h_filled")
        h_scaled = sem("h_scaled")
        hh_ready = sem("hh_ready")
        hl_ready = sem("hl_ready")
        o_filled = sem("o_filled")
        o_added = sem("o_added")
        y_loaded = sem("y_loaded")
        yh_ready = sem("yh_ready")
        yl_ready = sem("yl_ready")
        res_filled = sem("res_filled")
        res_added = sem("res_added")
        out_stats_ready = sem("out_stats_ready")

        pieces = []
        if with_o:
            wo_v = w_o.rearrange("(c p) n -> p c n", p=P)
            for c in range(0, KT, 2):
                pieces.append((wo_v[:, c:c + 2], wo[:, c:c + 2, 0], wo[:, c:c + 2, 1], 2))
        for k in range(KT):
            pieces.append((w_a[:, k * P:(k + 1) * P, :].rearrange("e p r -> p e r"),
                           wa[:, k, 0].rearrange("p (e r) -> p e r", e=NE),
                           wa[:, k, 1].rearrange("p (e r) -> p e r", e=NE), NE))
        for e in range(0, NE, 2):
            pieces.append((w_b[e:e + 2].rearrange("e p n -> p e n"), wb[:, e:e + 2, 0], wb[:, e:e + 2, 1], 2))
        n_pieces = len(pieces)
        n_first = n_pieces - NE // 2

        def staged(c, parts):
            return stage[:, c % STAGES].rearrange("p (a n) -> p a n", a=parts)

        x_in = x_src.rearrange("(n j p) d -> n p j d", p=P, j=TT)
        x_out = x_dst.rearrange("(n j p) d -> n p j d", p=P, j=TT)
        y_in = y_src.rearrange("(c p) (n t) -> n p c t", p=P, t=TB) if with_o else None
        first, second = Block2(0, 0), Block2(0, 1)

        block = ctx.enter_context(nc.Block())

        @block.sync
        def _(sp):
            def load_x(m):
                sp.dma_start(x[:, m.parity], x_in[m.index()]).then_inc(x_loaded[m.parity], 16)

            def load_y(m):
                sp.wait_ge(yl_ready, m.at(KT, 0))
                sp.dma_start(yt[:], y_in[m.index()]).then_inc(y_loaded, 16)

            def body(n, look, look2):
                if look2 and with_o:
                    load_y(n.next().next())
                sp.wait_ge(o_added, n.at(TT, TT))
                sp.dma_start(x_out[n.index()], x[:, n.parity]).then_inc(x_stored[n.parity], 16)
                if moments_dst is not None:
                    sp.wait_ge(out_stats_ready, n.at(1, 1))
                    sp.dma_start(moments_dst[n.index()], out_stats[:, n.parity]).then_inc(x_stored[n.parity], 16)
                if look2:
                    sp.wait_ge(x_stored[n.parity], (n.pair + 1) * STORES)
                    load_x(n.next().next())

            load_x(first)
            sp.dma_start(wr_raw[:], w_router.rearrange("(k p) e -> p k e", p=P)).then_inc(wr_loaded, 16)
            if with_o:
                load_y(first)
            for c, (src, _, _, parts) in enumerate(pieces):
                if c >= STAGES:
                    sp.wait_ge(w_lo, c - STAGES + 1)
                sp.dma_start(staged(c, parts), src).then_inc(w_loaded[c % STAGES], 16)
            load_x(second)
            if with_o:
                load_y(second)
            each_block(sp, nblocks, body)
            for parity in range(2):
                sp.wait_ge(x_stored[parity], STORES * (nblocks // 2))

        @block.gpsimd
        def _(pool):
            nc.gpsimd.memset(ident[:], 0.0).then_inc(zeroed, 1)
            nc.gpsimd.memset(fold[:], 0.0).then_inc(zeroed, 1)
            nc.gpsimd.memset(eps_col[:], LN_EPS).then_inc(consts_ready, 1)
            nc.gpsimd.memset(zero_col[:], 0.0).then_inc(consts_ready, 1)
            nc.gpsimd.iota(first_w[:], pattern=[[0, TT], [-1, NE]], base=NE, channel_multiplier=0,
                           allow_small_or_imprecise_dtypes=True).then_inc(consts_ready, 1)
            pool.wait_ge(zeroed, 2)
            nc.gpsimd.affine_select(out=ident[:], in_=ident[:], compare_op=ALU.not_equal, fill=1.0, base=0,
                                    pattern=[[-1, P]], channel_multiplier=1).then_inc(consts_ready, 1)
            nc.gpsimd.affine_select(out=fold[:], in_=fold[:], compare_op=ALU.not_equal, fill=1.0, base=0,
                                    pattern=[[-1, NE]], channel_multiplier=1).then_inc(zeroed, 1)
            pool.wait_ge(zeroed, 3)
            nc.gpsimd.affine_select(out=fold[:], in_=fold[:], compare_op=ALU.not_equal, fill=1.0, base=-NE,
                                    pattern=[[-1, NE]], channel_multiplier=1).then_inc(consts_ready, 1)
            nc.gpsimd.memset(own_tile[:], 0.0).then_inc(zeroed, 1)
            nc.gpsimd.memset(rows_of[:], 0.0).then_inc(zeroed, 1)
            pool.wait_ge(zeroed, 5)
            for a in range(2 * NE):
                nc.gpsimd.affine_select(out=own_tile[:], in_=own_tile[:], compare_op=ALU.not_equal, fill=1.0,
                                        base=-TT * a, pattern=[[-1, TT]], channel_multiplier=1).then_inc(zeroed, 1)
                pool.wait_ge(zeroed, 6 + a)
            nc.gpsimd.memset(rows_of[0:2 * NE * TT], 1.0).then_inc(zeroed, 1)
            pool.wait_ge(zeroed, 22)
            nc.gpsimd.affine_select(out=rows_of[:], in_=rows_of[:], compare_op=ALU.is_ge, fill=0.0, base=0,
                                    pattern=[[-TT, 2 * NE]], channel_multiplier=1).then_inc(zeroed, 1)
            pool.wait_ge(zeroed, 23)
            nc.gpsimd.affine_select(out=rows_of[:], in_=rows_of[:], compare_op=ALU.is_ge, fill=0.0, base=TT - 1,
                                    pattern=[[TT, 2 * NE]], channel_multiplier=-1).then_inc(consts_ready, 1)

            def split_y(m):
                for k in range(KT):
                    pool.wait_ge(yh_ready, m.at(KT, k + 1))
                    nc.gpsimd.tensor_tensor(yl[:, k], yt[:, k], yh[:, k].bitcast(F32),
                                            ALU.subtract).then_inc(yl_ready, 1)

            def body(n, look, look2):
                for e in range(NE):
                    pool.wait_ge(hh_ready, n.at(NE, e + 1))
                    nc.gpsimd.tensor_tensor(hl[:, e], hs[:, e % HS], hh[:, e].bitcast(F32),
                                            ALU.subtract).then_inc(hl_ready, 1)
                    if e == 3 and look2 and with_o:
                        split_y(n.next().next())

            if with_o:
                split_y(first)
                split_y(second)
            each_block(pool, nblocks, body)

        @block.scalar
        def _(act):
            def roots(m):
                act.wait_ge(var_ready, m.at(1, 1))
                nc.scalar.activation(root[:, 0], mv[:, :, 1], ACT.Sqrt, bias=eps_col[:])
                nc.scalar.activation(root[:, 1], mv[:, :, 1], ACT.Sqrt, bias=zero_col[:],
                                     scale=float(D)).then_inc(root_ready, 1)

            def x_hi(m):
                for k in range(KT):
                    act.wait_ge(t_filled, m.at(KT, k + 1))
                    nc.scalar.copy(xh[:, k], t_bank[k % 2][:]).then_inc(xh_ready, 1)

            def logits_copy(m):
                act.wait_ge(lg_filled, m.at(1, 1))
                nc.scalar.copy(lg[:], m_bank[0:2 * NE, :]).then_inc(lg_copied, 1)

            def gap_exp(m):
                act.wait_ge(gap_ready, m.at(1, 1))
                nc.scalar.activation(ratio[:], gap[:], ACT.Exp, bias=zero_col[:]).then_inc(ratio_ready, 1)

            def cb_copy(n, e):
                act.wait_ge(cb_filled, n.at(NE, e + 1))
                if e >= 2:
                    act.wait_ge(h_scaled, n.at(NE, e - 1))
                nc.scalar.copy(cb[:, e % 2], m_bank[:]).then_inc(cb_ready, 1)

            def y_hi(m):
                act.wait_ge(y_loaded, m.at(16, 16))
                act.wait_ge(res_filled, m.at(TT, 0))
                for k in range(KT):
                    nc.scalar.copy(yh[:, k], yt[:, k]).then_inc(yh_ready, 1)

            def body(n, look, look2):
                cb_copy(n, 0)
                for e in range(NE):
                    if e + 1 < NE:
                        cb_copy(n, e + 1)
                    act.wait_ge(h_scaled, n.at(NE, e + 1))
                    nc.scalar.copy(hh[:, e], hs[:, e % HS]).then_inc(hh_ready, 1)
                    if e == 3 and look2 and with_o:
                        y_hi(n.next().next())
                    if e == 3 + LAG and look:
                        roots(n.next())
                if look:
                    x_hi(n.next())
                    logits_copy(n.next())
                    gap_exp(n.next())

            act.wait_ge(consts_ready, 6)
            if with_o:
                y_hi(first)
            for c, (_, hi, _, parts) in enumerate(pieces):
                act.wait_ge(w_loaded[c % STAGES], 16 * (c // STAGES + 1))
                nc.scalar.copy(hi, staged(c, parts)).then_inc(w_hi, 1)
            if with_o:
                y_hi(second)
            roots(first)
            x_hi(first)
            logits_copy(first)
            gap_exp(first)
            each_block(act, nblocks, body)

        @block.vector
        def _(dve):
            LINKS = 26
            taken = [0]

            def link(m, ins):
                taken[0] += 1
                ins.then_inc(dve_step, 1)
                dve.wait_ge(dve_step, m.at(LINKS, taken[0]))

            def wide(col):
                return col.unsqueeze(2).to_broadcast([P, TT, NE])

            def x_ready(m):
                dve.wait_ge(x_loaded[m.parity], m.pair * 16 + 16)
                if with_o:
                    for j in range(TT):
                        dve.wait_ge(res_filled, m.at(TT, j + 1))
                        nc.vector.tensor_tensor(x[:, m.parity, j], o_bank[j % 2][:], x[:, m.parity, j],
                                                ALU.add).then_inc(res_added, 1)
                    dve.wait_ge(res_added, m.at(TT, TT))

            def moments(m, j):
                nc.vector.bn_stats(stats[:, j], x[:, m.parity, j]).then_inc(stats_ready, 1)

            def aggregate(m):
                for i in range(TT):
                    ins = nc.vector.bn_aggr(mv[:, i], stats[:, i])
                ins.then_inc(var_ready, 1)

            def scales(m):
                dve.wait_ge(root_ready, m.at(1, 1))
                link(m, nc.vector.reciprocal(inv0[:], root[:, 0]))
                link(m, nc.vector.tensor_tensor(newton[:], inv0[:], inv0[:], ALU.mult))
                link(m, nc.vector.scalar_tensor_tensor(newton[:], mv[:, :, 1], LN_EPS, newton[:], ALU.add, ALU.mult))
                link(m, nc.vector.tensor_scalar(newton[:], newton[:], -0.5, 1.5, ALU.mult, ALU.add))
                link(m, nc.vector.tensor_tensor(rstd[:], inv0[:], newton[:], ALU.mult))
                link(m, nc.vector.tensor_tensor(norm[:], root[:, 1], rstd[:], ALU.mult))
                link(m, nc.vector.tensor_scalar(norm[:], norm[:], NORM_MIN, None, ALU.max))
                link(m, nc.vector.reciprocal(inv_norm[:], norm[:]))

            def normalise(m):
                dve.wait_ge(t_filled, m.at(KT, 0))
                for j in range(TT):
                    ins = nc.vector.tensor_scalar(xn[:, j], x[:, m.parity, j], mv[:, j, 0:1], rstd[:, j:j + 1],
                                                  ALU.subtract, ALU.mult)
                ins.then_inc(xn_ready, 1)

            def x_lo(m):
                for k in range(KT):
                    dve.wait_ge(xh_ready, m.at(KT, k + 1))
                    nc.vector.tensor_tensor(xl[:, k], t_bank[k % 2][:], xh[:, k].bitcast(F32),
                                            ALU.subtract).then_inc(xl_ready, 1)

            def pick(m, i):
                link(m, nc.vector.tensor_reduce(peak[:, i], logit[:], AX.X, ALU.max))
                link(m, nc.vector.tensor_tensor(hit[:], logit[:], wide(peak[:, i]), ALU.is_equal))
                link(m, nc.vector.tensor_tensor(score[:], hit[:], first_w[:], ALU.mult))
                link(m, nc.vector.tensor_reduce(who[:], score[:], AX.X, ALU.max))
                link(m, nc.vector.tensor_tensor(top[i][:], score[:], wide(who[:]), ALU.is_equal))

            def route(m):
                dve.wait_ge(lt_filled, m.at(1, 1))
                link(m, nc.vector.tensor_tensor(logit[:], m_bank[:, 0:TT * NE].rearrange("p (j e) -> p j e", e=NE),
                                                wide(inv_norm[:]), ALU.mult))
                pick(m, 0)
                link(m, nc.vector.scalar_tensor_tensor(logit[:], top[0][:], -BIG, logit[:], ALU.mult, ALU.add))
                pick(m, 1)
                nc.vector.tensor_tensor(gap[:], peak[:, 1], peak[:, 0], ALU.subtract).then_inc(gap_ready, 1)
                dve.wait_ge(ratio_ready, m.at(1, 1))
                link(m, nc.vector.tensor_scalar(total[:], ratio[:], 1.0, None, ALU.add))
                link(m, nc.vector.reciprocal(gate[:, 0], total[:]))
                link(m, nc.vector.tensor_tensor(gate[:, 1], ratio[:], gate[:, 0], ALU.mult))
                nc.vector.tensor_tensor(score[:], top[0][:], wide(gate[:, 0]), ALU.mult)
                link(m, nc.vector.tensor_tensor(hit[:], top[1][:], wide(gate[:, 1]), ALU.mult))
                link(m, nc.vector.tensor_tensor(comb[:].rearrange("p e j -> p j e"), score[:], hit[:], ALU.add))
                dve.wait_ge(ct_filled, m.at(1, 0))
                link(m, nc.vector.tensor_copy(comb_parts[:, 0], comb[:]))
                nc.vector.tensor_tensor(comb_parts[:, 1], comb[:], comb_parts[:, 0].bitcast(F32),
                                        ALU.subtract).then_inc(comb_ready, 1)
                assert taken[0] == LINKS

            def mask_combine(m):
                dve.wait_ge(cb_filled, m.at(NE, 0))
                dve.wait_ge(ct_filled, m.at(1, 1))
                nc.vector.tensor_tensor(cm[:], m_bank[:, 0:P].unsqueeze(1).to_broadcast([P, TT, P]),
                                        own_tile[:].unsqueeze(2).to_broadcast([P, TT, P]),
                                        ALU.mult).then_inc(cm_ready, 1)

            def add_out(n, j):
                dve.wait_ge(o_filled, n.at(TT, j + 1))
                nc.vector.scalar_tensor_tensor(x[:, n.parity, j], o_bank[j % 2][:], 0.5, x[:, n.parity, j],
                                               ALU.mult, ALU.add).then_inc(o_added, 1)

            def out_moments(n):
                dve.wait_ge(o_added, n.at(TT, TT))
                for j in range(TT):
                    ins = nc.vector.bn_stats(out_stats[:, n.parity, j], x[:, n.parity, j])
                ins.then_inc(out_stats_ready, 1)

            def body(n, look, look2):
                m = n.next()
                taken[0] = 0
                for e in range(NE):
                    dve.wait_ge(cb_ready, n.at(NE, e + 1))
                    dve.wait_ge(h_filled, n.at(NE, e + 1))
                    if e >= HS:
                        dve.wait_ge(hl_ready, n.at(NE, e - HS + 1))
                    if look and e == 2 + LAG:
                        dve.wait_ge(stats_ready, m.at(TT, TT))
                    nc.vector.tensor_tensor(hs[:, e % HS], h_bank[e % 3][:], cb[:, e % 2], ALU.mult).then_inc(h_scaled, 1)
                    if not look:
                        continue
                    if e == LAG:
                        x_ready(m)
                    if e in (LAG, LAG + 1):
                        moments(m, 2 * (e - LAG))
                        moments(m, 2 * (e - LAG) + 1)
                    if e == 2 + LAG:
                        aggregate(m)
                    if e == 4 + LAG:
                        scales(m)
                    if e == 5 + LAG:
                        normalise(m)
                if look:
                    x_lo(m)
                add_out(n, 0)
                add_out(n, 1)
                if look:
                    route(m)
                add_out(n, 2)
                if look:
                    mask_combine(m)
                add_out(n, 3)
                if moments_dst is not None:
                    out_moments(n)

            dve.wait_ge(consts_ready, 6)
            dve.wait_ge(wr_loaded, 16)
            nc.vector.memset(wr[:, :, 3].bitcast(F32), 0.0)
            nc.vector.tensor_copy(wr[:, :, 0], wr_raw[:])
            nc.vector.tensor_copy(wr[:, :, 2], wr_raw[:]).then_inc(wr_step, 1)
            dve.wait_ge(wr_step, 1)
            nc.vector.tensor_tensor(wr[:, :, 1], wr_raw[:], wr[:, :, 0].bitcast(F32), ALU.subtract).then_inc(wr_step, 1)
            nc.vector.memset(comb_parts[:, 2:4].bitcast(F32), 0.0)
            for e in range(NE):
                nc.vector.tensor_tensor(spread[:, e], rows_of[:, e:e + 1].to_broadcast([P, P]),
                                        rows_of[:, NE + e:NE + e + 1].to_broadcast([P, P]),
                                        ALU.add).then_inc(wr_step, 1)
            for c, (_, hi, lo, parts) in enumerate(pieces):
                dve.wait_ge(w_hi, c + 1)
                nc.vector.tensor_tensor(lo, staged(c, parts), hi.bitcast(F32), ALU.subtract).then_inc(w_lo, 1)
            x_ready(first)
            for j in range(TT):
                moments(first, j)
            dve.wait_ge(stats_ready, TT)
            aggregate(first)
            scales(first)
            normalise(first)
            x_lo(first)
            route(first)
            mask_combine(first)
            each_block(dve, nblocks, body)

        @block.tensor
        def _(pe):
            def residual(m):
                pe.wait_ge(yl_ready, m.at(KT, KT))
                for j in range(TT):
                    if j >= 2:
                        pe.wait_ge(res_added, m.at(TT, j - 1))
                    t = slice(j * P, (j + 1) * P)
                    for k in range(KT):
                        nc.tensor.matmul(o_bank[j % 2][:], yh[:, k, t], wo[:, k, 0], start=k == 0, stop=False)
                        nc.tensor.matmul(o_bank[j % 2][:], yh[:, k, t], wo[:, k, 1], start=False, stop=False)
                        mm = nc.tensor.matmul(o_bank[j % 2][:], yl[:, k, t], wo[:, k, 0], start=False, stop=k == KT - 1)
                    mm.then_inc(res_filled, 1)

            def hidden(n, e):
                if e == 0:
                    pe.wait_ge(xl_ready, n.at(KT, KT))
                if e >= 3:
                    pe.wait_ge(h_scaled, n.at(NE, e - 2))
                r = slice(e * RANK, (e + 1) * RANK)
                for k in range(KT):
                    nc.tensor.matmul(h_bank[e % 3][:], wa[:, k, 0, r], xh[:, k], start=k == 0, stop=False)
                    nc.tensor.matmul(h_bank[e % 3][:], wa[:, k, 0, r], xl[:, k], start=False, stop=False)
                    mm = nc.tensor.matmul(h_bank[e % 3][:], wa[:, k, 1, r], xh[:, k], start=False, stop=k == KT - 1)
                mm.then_inc(h_filled, 1)

            def output(n, j, look):
                if j < 2:
                    if with_o and look:
                        pe.wait_ge(res_added, n.at(TT, 2 * TT))
                else:
                    pe.wait_ge(o_added, n.at(TT, j - 1))
                t = slice(j * P, (j + 1) * P)
                for e in range(NE):
                    if j == 0:
                        pe.wait_ge(hl_ready, n.at(NE, e + 1))
                    nc.tensor.matmul(o_bank[j % 2][:], hh[:, e, t], wb[:, e, 0], start=e == 0, stop=False)
                    nc.tensor.matmul(o_bank[j % 2][:], hh[:, e, t], wb[:, e, 1], start=False, stop=False)
                    mm = nc.tensor.matmul(o_bank[j % 2][:], hl[:, e, t], wb[:, e, 0], start=False, stop=e == NE - 1)
                mm.then_inc(o_filled, 1)

            def turn_x(m, k):
                pe.wait_ge(xn_ready, m.at(1, 1))
                pe.wait_ge(xl_ready, m.at(KT, max(k - 1, 0)))
                for j in range(TT):
                    mm = nc.tensor.transpose(t_bank[k % 2][:, j * P:(j + 1) * P], xn[:, j, k * P:(k + 1) * P], ident[:])
                mm.then_inc(t_filled, 1)

            def logits(m):
                pe.wait_ge(xl_ready, m.at(KT, KT))
                pe.wait_ge(cb_ready, m.at(NE, 0))
                for k in range(KT):
                    nc.tensor.matmul(m_bank[0:2 * NE, :], wr[:, k, 0:2].rearrange("p a e -> p (a e)"), xh[:, k],
                                     start=k == 0, stop=False)
                    mm = nc.tensor.matmul(m_bank[0:2 * NE, :], wr[:, k, 2:4].rearrange("p a e -> p (a e)"), xl[:, k],
                                          start=False, stop=k == KT - 1)
                mm.then_inc(lg_filled, 1)

            def turn_logits(m):
                pe.wait_ge(lg_copied, m.at(1, 1))
                for j in range(TT):
                    mm = nc.tensor.matmul(m_bank[:, j * NE:(j + 1) * NE], lg[:, j * P:(j + 1) * P], fold[:],
                                          start=True, stop=True)
                mm.then_inc(lt_filled, 1)

            def turn_combine(m):
                pe.wait_ge(comb_ready, m.at(1, 1))
                nc.tensor.transpose(m_bank[:, 0:P], comb_parts[:].rearrange("p a e j -> p (a e j)").bitcast(F32),
                                    ident[:]).then_inc(ct_filled, 1)

            def spread_combine(n, e):
                if e == 0:
                    pe.wait_ge(cm_ready, n.at(1, 1))
                else:
                    pe.wait_ge(cb_ready, n.at(NE, e))
                nc.tensor.matmul(m_bank[:], spread[:, e], cm[:].rearrange("p j t -> p (j t)"),
                                 start=True, stop=True).then_inc(cb_filled, 1)

            def body(n, look, look2):
                m = n.next()
                for e in range(NE):
                    hidden(n, e)
                    spread_combine(n, e)
                    if e == 1 and look and with_o:
                        pe.wait_ge(h_scaled, n.at(NE, 1))
                        residual(m)
                if look:
                    turn_x(m, 0)
                    turn_x(m, 1)
                output(n, 0, look)
                if look:
                    turn_x(m, 2)
                    turn_x(m, 3)
                output(n, 1, look)
                if look:
                    logits(m)
                output(n, 2, look)
                if look:
                    turn_logits(m)
                output(n, 3, look)
                if look:
                    turn_combine(m)

            pe.wait_ge(consts_ready, 6)
            if with_o:
                pe.wait_ge(w_lo, KT // 2)
                residual(first)
            for k in range(KT):
                turn_x(first, k)
            pe.wait_ge(wr_step, 2 + NE)
            logits(first)
            turn_logits(first)
            turn_combine(first)
            pe.wait_ge(w_lo, n_pieces)
            each_block(pe, nblocks, body)



HEADS = 16
HD = D // HEADS
HALF = HD // 2
GH = 4
NG = HEADS // GH
SEQ = 1024
XR = 2
QB = 512
ST = SEQ // P
SCALE = HD ** -0.5
GROUP = 128
Q_EPS = 1e-8
STEPS = [(qb, kt) for qb in range(SEQ // QB) for kt in reversed(range((qb + 1) * QB // P))]
NS = len(STEPS)
PIECES = [(i, k, min(k + QB, (i + 1) * P)) for i in range(ST) for k in range(0, (i + 1) * P, QB)]
NP = GH * len(PIECES)


def prepare_weights(nc, psum, w_q, w_k, w_v, w_o, wqk_dst, wv_dst, wo_dst):
    with ExitStack() as ctx:
        def sb(name, shape, dt):
            return ctx.enter_context(nc.sbuf_tensor(f"prep_{name}", shape, dt))

        def sem(name):
            return ctx.enter_context(nc.semaphore(f"prep_{name}"))

        NW = 4
        G = D // GROUP
        ident = sb("ident", [P, P], F32)
        w = sb("w", [P, NW, KT * G, GROUP], F32)
        sums = sb("sums", [P, NW, KT * G], F32)
        scale = sb("scale", [P, NW, KT * G], F32)
        half = sb("half", [P, NW, 2, KT * G], F32)
        pos = sb("pos", [P, KT * G, GROUP], F32)
        neg = sb("neg", [P, KT * G, GROUP], F32)
        qk_t = sb("qk_t", [P, KT, 2, NG, 2, 2, GH * HALF], F32R)
        v_t = sb("v_t", [P, 2, KT, D], F32R)
        o_t = sb("o_t", [P, KT, D], F32)

        zeroed = sem("zeroed")
        ident_ready = sem("ident_ready")
        w_loaded = [sem(f"w_loaded{i}") for i in range(NW)]
        step = sem("step")
        w_ready = sem("w_ready")
        turned = sem("turned")
        hi_ready = sem("hi_ready")
        lo_ready = sem("lo_ready")
        stored = sem("stored")

        block = ctx.enter_context(nc.Block())

        @block.sync
        def _(sp):
            for i, src in enumerate((w_q, w_k, w_v, w_o)):
                sp.dma_start(w[:, i].rearrange("p (o g) c -> p o (g c)", g=G),
                             src.rearrange("(o p) c -> p o c", p=P)).then_inc(w_loaded[i], 16)
            sp.wait_ge(lo_ready, 2 * KT)
            for k in range(KT):
                for part in range(2):
                    sp.dma_start(wqk_dst[:, part, k].rearrange("g p c -> p g c"),
                                 qk_t[:, k, part].rearrange("p g f w c -> p g (f w c)").bitcast(F32)).then_inc(stored, 16)
            sp.wait_ge(lo_ready, 3 * KT)
            sp.dma_start(wv_dst.rearrange("a (k p) n -> p (a k) n", p=P), v_t[:].rearrange("p a k n -> p (a k) n").bitcast(F32)).then_inc(stored, 16)
            sp.wait_ge(hi_ready, 4 * KT)
            sp.dma_start(wo_dst.rearrange("(k p) n -> p k n", p=P), o_t[:]).then_inc(stored, 16)
            sp.wait_ge(stored, 16 * (2 * KT + 2))

        @block.gpsimd
        def _(pool):
            nc.gpsimd.memset(ident[:], 0.0).then_inc(zeroed, 1)
            pool.wait_ge(zeroed, 1)
            nc.gpsimd.affine_select(out=ident[:], in_=ident[:], compare_op=ALU.not_equal, fill=1.0, base=0,
                                    pattern=[[-1, P]], channel_multiplier=1).then_inc(ident_ready, 1)

        @block.vector
        def _(dve):
            count = [0]

            def link(ins):
                count[0] += 1
                ins.then_inc(step, 1)
                dve.wait_ge(step, count[0])

            def wide(t):
                return t.unsqueeze(2).to_broadcast([P, KT * G, GROUP])

            def quantise(i):
                dve.wait_ge(w_loaded[i], 16)
                link(nc.vector.tensor_reduce(sums[:, i], w[:, i], AX.X, ALU.add, apply_absolute_value=True))
                link(nc.vector.tensor_scalar(scale[:, i], sums[:, i], 1.0 / GROUP, Q_EPS, ALU.mult, ALU.max))
                nc.vector.tensor_scalar(half[:, i, 0], scale[:, i], 0.5, None, ALU.mult)
                link(nc.vector.tensor_scalar(half[:, i, 1], scale[:, i], -0.5, None, ALU.mult))
                nc.vector.tensor_tensor(pos[:], w[:, i], wide(half[:, i, 0]), ALU.is_gt)
                link(nc.vector.tensor_tensor(neg[:], w[:, i], wide(half[:, i, 1]), ALU.is_lt))
                link(nc.vector.tensor_tensor(pos[:], pos[:], neg[:], ALU.subtract))
                link(nc.vector.tensor_tensor(pos[:], pos[:], wide(scale[:, i]), ALU.mult))
                link(nc.vector.tensor_tensor(pos[:], pos[:], w[:, i], ALU.subtract))
                nc.vector.tensor_tensor(w[:, i], w[:, i], pos[:], ALU.add).then_inc(w_ready, 1)
                dve.wait_ge(w_ready, i + 1)

            def lo(i, k):
                b = i * KT + k
                dve.wait_ge(hi_ready, b + 1)
                if i < 2:
                    src = psum[:, b % 8].rearrange("p (g h f d) -> p f g h d", g=NG, f=2, d=HALF)
                    for f in range(2):
                        ins = nc.vector.tensor_tensor(qk_t[:, k, 1, :, f, i].rearrange("p g (h d) -> p g h d", d=HALF), src[:, f],
                                                      qk_t[:, k, 0, :, f, i].rearrange("p g (h d) -> p g h d", d=HALF).bitcast(F32),
                                                      ALU.subtract)
                    ins.then_inc(lo_ready, 1)
                else:
                    nc.vector.tensor_tensor(v_t[:, 1, k], psum[:, b % 8], v_t[:, 0, k].bitcast(F32),
                                            ALU.subtract).then_inc(lo_ready, 1)

            for i in range(NW):
                quantise(i)
                if 1 <= i < 3:
                    for k in range(KT):
                        lo(i - 1, k)
            for k in range(KT):
                lo(2, k)

        @block.scalar
        def _(act):
            for i in range(NW):
                for k in range(KT):
                    b = i * KT + k
                    act.wait_ge(turned, b + 1)
                    if i < 2:
                        src = psum[:, b % 8].rearrange("p (g h f d) -> p f g h d", g=NG, f=2, d=HALF)
                        for f in range(2):
                            ins = nc.scalar.copy(qk_t[:, k, 0, :, f, i].rearrange("p g (h d) -> p g h d", d=HALF), src[:, f])
                        ins.then_inc(hi_ready, 1)
                    elif i == 2:
                        nc.scalar.copy(v_t[:, 0, k], psum[:, b % 8]).then_inc(hi_ready, 1)
                    else:
                        nc.scalar.copy(o_t[:, k], psum[:, b % 8]).then_inc(hi_ready, 1)

        @block.tensor
        def _(pe):
            pe.wait_ge(ident_ready, 1)
            for i in range(NW):
                pe.wait_ge(w_ready, i + 1)
                for k in range(KT):
                    if i >= 2:
                        pe.wait_ge(lo_ready, (i - 2) * KT + k + 1)
                    for o in range(KT):
                        mm = nc.tensor.transpose(psum[:, (i * KT + k) % 8, o * P:(o + 1) * P], w[:, i, o * G + k], ident[:])
                    mm.then_inc(turned, 1)


class Unit:

    def __init__(self, b, g):
        self.b, self.g = b, g

    def plus(self, n):
        return Unit(self.b + (self.g + n) // NG, (self.g + n) % NG)

    def at(self, k, c):
        return self.b * (NG * k) + (self.g * k + c)

    def ring(self, k, c):
        return self.b * (NG // 2 * k) + (self.g // 2 * k + c)


def attention_phase(nc, psum, nbatch, x_src, moments_src, wqk_src, wv_src, cos_src, sin_src, y_dst, rope_tmp, mrow_tmp):
    with ExitStack() as ctx:
        def sb(name, shape, dt):
            return ctx.enter_context(nc.sbuf_tensor(f"att_{name}", shape, dt))

        def sem(name):
            return ctx.enter_context(nc.semaphore(f"att_{name}"))

        ident = sb("ident", [P, P], F32)
        ident_b = sb("ident_b", [P, P], BF16)
        hide_k = sb("hide_k", [P, P], BF16)
        hide_q = sb("hide_q", [P, P], BF16)
        ones = sb("ones", [P, HD], F32)
        cos = sb("cos", [P, SEQ], F32)
        sin = sb("sin", [P, SEQ], F32)
        wqk = sb("wqk", [P, 2, 2, KT, 2, P], F32R)
        wv = sb("wv", [P, 2, KT, D], F32R)
        mv = sb("mv", [P, nbatch * ST, 2], F32)
        root = sb("root", [P, nbatch * ST], F32)
        newton = sb("newton", [P, nbatch * ST], F32)
        rstd = sb("rstd", [P, nbatch * ST], F32)
        eps_col = sb("eps_col", [P, 1], F32)
        xt = sb("xt", [P, XR, D], F32)
        xh = sb("xh", [P, KT, SEQ], F32R)
        xl = sb("xl", [P, KT, SEQ], F32R)
        v = sb("v", [P, ST, D], F32)
        qs = sb("qs", [P, 2, GH, SEQ], F32R)
        ks = sb("ks", [P, 2, GH, SEQ], F32R)
        ra = sb("ra", [P, 2, 2, QB], F32)
        rb = sb("rb", [P, 2, 2, QB], F32)
        turned_qk = sb("turned_qk", [P, 2, 2, QB], F32R)
        mxp = sb("mxp", [P, GH, len(PIECES)], F32)
        mneg = sb("mneg", [P, GH, ST], F32)
        mrow = sb("mrow", [GH * ST, P], F32R)
        probs = sb("probs", [P, 2, GH, QB], F32)
        acc = sb("acc", [P, 2, QB], F32)
        den = sb("den", [P, 2, QB], F32)

        stats = acc[:].rearrange("p j t -> p (j t)")[:, 0:nbatch * ST * 6].rearrange("p (i c) -> p i c", c=6)

        s_bank = [psum[:, 0:2], psum[:, 2:4]]
        w_bank = [psum[:, 4], psum[:, 5]]
        pv_bank, den_bank = psum[:, 6], psum[:, 7]

        def t_bank(i):
            return (w_bank + [psum[:, 0], psum[:, 1]])[i % 4]

        def qk_bank(f):
            return (w_bank[0], w_bank[1]) if f == 0 else (psum[:, 2], psum[:, 3])

        zeroed = sem("zeroed")
        consts_ready = sem("consts_ready")
        tables_loaded = sem("tables_loaded")
        wv_loaded = sem("wv_loaded")
        wqk_loaded = [sem(f"wqk_loaded{i}") for i in range(2)]
        stats_loaded = sem("stats_loaded")
        mv_ready = sem("mv_ready")
        root_ready = sem("root_ready")
        rstd_step = sem("rstd_step")
        xt_loaded = [sem(f"xt_loaded{i}") for i in range(XR)]
        xt_ready = sem("xt_ready")
        xt_turned = sem("xt_turned")
        xh_ready = sem("xh_ready")
        xl_ready = sem("xl_ready")
        v_filled = sem("v_filled")
        v_ready = sem("v_ready")
        qk_filled = sem("qk_filled")
        qk_read = sem("qk_read")
        rope_ready = sem("rope_ready")
        rope_hi = sem("rope_hi")
        rope_lo = sem("rope_lo")
        rope_stored = sem("rope_stored")
        placed = sem("placed")
        mx_filled = sem("mx_filled")
        mx_read = sem("mx_read")
        mneg_ready = sem("mneg_ready")
        mrow_turned = sem("mrow_turned")
        mrow_copied = sem("mrow_copied")
        mrow_stored = sem("mrow_stored")
        mrow_placed = sem("mrow_placed")
        s_filled = sem("s_filled")
        exp_done = sem("exp_done")
        pv_done = sem("pv_done")
        acc_copied = sem("acc_copied")
        den_copied = sem("den_copied")
        inv_ready = sem("inv_ready")
        y_ready = sem("y_ready")
        y_stored = [sem("y_stored0"), sem("y_stored1")]

        U0 = Unit(0, 0)

        def exists(u):
            return not (isinstance(u.b, int) and u.b >= nbatch)

        def each_batch(engine, body):
            with engine.Fori(0, nbatch - 1) as b:
                for g in range(NG):
                    body(Unit(b, g))
            for g in range(NG):
                body(Unit(nbatch - 1, g))

        x_in = x_src.rearrange("(b t p) d -> b t p d", p=P, t=ST)
        y_out = y_dst.rearrange("(g p) (b j t) -> g b j p t", p=P, j=2, t=QB)

        block = ctx.enter_context(nc.Block())

        @block.sync
        def _(sp):
            def wqk_load(u, used):
                sp.wait_ge(qk_filled, used)
                sp.dma_start(wqk[:, u.g % 2].rearrange("p a k f c -> p (a k) (f c)").bitcast(F32),
                             wqk_src[u.g].rearrange("a k p c -> p (a k) c")).then_inc(wqk_loaded[u.g % 2], 16)

            def load_xt(b, i, used):
                sp.wait_ge(xt_turned, used)
                sp.dma_start(xt[:, i % XR], x_in[b, i]).then_inc(xt_loaded[i % XR], 16)

            def load_batch_head(b, used):
                for i in range(XR):
                    load_xt(b, i, used)

            def store_rope(u):
                for f in range(2):
                    for part, made in enumerate((rope_hi, rope_lo)):
                        sp.wait_ge(made, u.at(4, 2 * f + 2))
                        sp.dma_start(rope_tmp[u.g % 2, part].rearrange("(p r) t -> p r t", r=2)[:, :, f * QB:(f + 1) * QB],
                                     turned_qk[:, part].bitcast(F32)).then_inc(rope_stored, 16)

            def place(u, free):
                if free is not None:
                    sp.wait_ge(pv_done, free)
                src = rope_tmp[u.g % 2].rearrange("a (w h r) t -> a w r h t", w=2, h=GH)
                for slot, (which, parts) in enumerate(((0, (0, 0, 1)), (1, (0, 1, 0)))):
                    dst = (qs, ks)[slot]
                    for row, part in enumerate(parts):
                        sp.dma_start(dst[row * HD:(row + 1) * HD, u.g % 2].bitcast(F32), src[part, which]).then_inc(placed, 16)

            def place_mrow(u):
                sp.wait_ge(mrow_copied, u.at(1, 1))
                sp.dma_start(mrow_tmp[:], mrow[:].bitcast(F32)).then_inc(mrow_stored, 16)
                sp.wait_ge(mrow_stored, u.at(16, 16))
                sp.dma_start(qs[3 * HD:3 * HD + 1, u.g % 2].rearrange("o h t -> o (h t)").bitcast(F32),
                             mrow_tmp.rearrange("(o r) t -> o (r t)", o=1)).then_inc(mrow_placed, 16)

            def store_y(u, j):
                sp.wait_ge(y_ready, u.at(2, j + 1))
                sp.dma_start(y_out[u.g, u.b, j], acc[:, j]).then_inc(y_stored[j], 16)

            def body(u):
                if exists(u.plus(3)):
                    wqk_load(u.plus(3), u.plus(2).at(4, 0))
                if u.g == 0 and exists(u.plus(NG)):
                    load_batch_head(u.b + 1, u.b * ST + ST)
                if exists(u.plus(2)):
                    store_rope(u.plus(2))
                store_y(u, 0)
                if exists(u.plus(1)):
                    place_mrow(u.plus(1))
                if exists(u.plus(2)):
                    place(u.plus(2), u.at(NS, NS))
                if u.g == 0 and exists(u.plus(NG)):
                    for i in range(XR, ST):
                        load_xt(u.b + 1, i, u.b * ST + (ST + i - XR + 1))
                store_y(u, 1)

            sp.dma_start(cos[:], cos_src).then_inc(tables_loaded, 16)
            sp.dma_start(sin[:], sin_src).then_inc(tables_loaded, 16)
            sp.dma_start(stats[:], moments_src).then_inc(stats_loaded, 16)
            load_batch_head(0, 0)
            sp.dma_start(wv[:].rearrange("p a k n -> p (a k) n").bitcast(F32), wv_src.rearrange("a (k p) n -> p (a k) n", p=P)).then_inc(wv_loaded, 16)
            wqk_load(U0, 0)
            wqk_load(U0.plus(1), 0)
            for i in range(XR, ST):
                load_xt(0, i, i - XR + 1)
            store_rope(U0)
            sp.wait_ge(rope_stored, 64)
            place(U0, None)
            wqk_load(U0.plus(2), 4)
            store_rope(U0.plus(1))
            sp.wait_ge(rope_stored, 128)
            place(U0.plus(1), None)
            place_mrow(U0)
            each_batch(sp, body)
            sp.wait_ge(y_stored[0], 16 * NG * nbatch + 1)
            sp.wait_ge(y_stored[1], 16 * NG * nbatch + 1)

        @block.gpsimd
        def _(pool):
            nc.gpsimd.memset(ident[:], 0.0).then_inc(zeroed, 1)
            nc.gpsimd.memset(ident_b[:], 0.0).then_inc(zeroed, 1)
            nc.gpsimd.memset(hide_k[:], 0.0).then_inc(zeroed, 1)
            nc.gpsimd.memset(hide_q[:], 0.0).then_inc(zeroed, 1)
            nc.gpsimd.memset(ones[:], 1.0).then_inc(y_stored[0], 1)
            nc.gpsimd.memset(eps_col[:], LN_EPS).then_inc(y_stored[1], 1)
            pool.wait_ge(zeroed, 4)
            for tile in (ident, ident_b):
                nc.gpsimd.affine_select(out=tile[:], in_=tile[:], compare_op=ALU.not_equal, fill=1.0, base=0,
                                        pattern=[[-1, P]], channel_multiplier=1).then_inc(consts_ready, 1)
            nc.gpsimd.affine_select(out=hide_k[:], in_=hide_k[:], compare_op=ALU.is_ge, fill=-BIG, base=0,
                                    pattern=[[-1, P]], channel_multiplier=1).then_inc(consts_ready, 1)
            nc.gpsimd.affine_select(out=hide_q[:], in_=hide_q[:], compare_op=ALU.is_ge, fill=-BIG, base=0,
                                    pattern=[[1, P]], channel_multiplier=-1).then_inc(consts_ready, 1)

            def mix(u):
                for f in range(2):
                    pool.wait_ge(qk_read, u.at(2, f + 1))
                    nc.gpsimd.tensor_tensor(ra[:, f, 0], ra[:, f, 0], rb[:, f, 0], ALU.subtract).then_inc(rope_ready, 1)
                    nc.gpsimd.tensor_tensor(ra[:, f, 1], ra[:, f, 1], rb[:, f, 1], ALU.add).then_inc(rope_ready, 1)

            def rope_los(u):
                for f in range(2):
                    for r in range(2):
                        pool.wait_ge(rope_hi, u.at(4, 2 * f + r + 1))
                        nc.gpsimd.tensor_tensor(turned_qk[:, 1, r], ra[:, f, r], turned_qk[:, 0, r].bitcast(F32),
                                                ALU.subtract).then_inc(rope_lo, 1)

            def normalise_y(u, j):
                pool.wait_ge(inv_ready, u.at(2, j + 1))
                pool.wait_ge(acc_copied, u.at(2, j + 1))
                nc.gpsimd.tensor_tensor(acc[:, j], acc[:, j], den[:, j], ALU.mult).then_inc(y_ready, 1)

            def body(u):
                if exists(u.plus(2)):
                    rope_los(u.plus(2))
                normalise_y(u, 0)
                normalise_y(u, 1)
                if exists(u.plus(3)):
                    mix(u.plus(3))

            mix(U0)
            rope_los(U0)
            mix(U0.plus(1))
            rope_los(U0.plus(1))
            mix(U0.plus(2))
            each_batch(pool, body)

        @block.scalar
        def _(act):
            def x_hi(b, i):
                bank = t_bank(i)
                act.wait_ge(xt_turned, b * ST + (i + 1))
                nc.scalar.copy(xh[:, :, i * P:(i + 1) * P], bank.rearrange("p (k t) -> p k t", k=KT)).then_inc(xh_ready, 1)

            def v_copy(b, i):
                act.wait_ge(v_filled, b * ST + (i + 1))
                nc.scalar.copy(v[:, i], w_bank[i % 2]).then_inc(v_ready, 1)

            def rope_his(u, f, before=None):
                if before is not None:
                    act.wait_ge(placed, before)
                act.wait_ge(rope_stored, u.at(64, 32 * f))
                for r in range(2):
                    act.wait_ge(rope_ready, u.at(4, 2 * f + r + 1))
                    nc.scalar.copy(turned_qk[:, 0, r], ra[:, f, r]).then_inc(rope_hi, 1)

            def mrow_copy(u):
                act.wait_ge(mrow_turned, u.at(1, 1))
                act.wait_ge(mrow_stored, u.at(16, 0))
                nc.scalar.copy(mrow[:], s_bank[0][0:GH * ST, 0, 0:P]).then_inc(mrow_copied, 1)

            def exps(u, t):
                first = (STEPS[t][1] * P - STEPS[t][0] * QB) if STEPS[t][1] * P > STEPS[t][0] * QB else 0
                for hp in range(2):
                    act.wait_ge(s_filled, u.at(2 * NS, 2 * t + hp + 1))
                    if hp == 0 and t >= 2:
                        act.wait_ge(pv_done, u.at(NS, t - 1))
                    nc.scalar.activation(probs[:, t % 2, 2 * hp:2 * hp + 2, first:QB], s_bank[hp][:, :, first:QB],
                                         ACT.Exp, scale=SCALE).then_inc(exp_done, 1)

            def sums_copy(u, j):
                act.wait_ge(pv_done, u.at(NS, 4 if j == 0 else NS))
                act.wait_ge(y_stored[j], u.at(16, 1))
                nc.scalar.copy(den[:, j], den_bank).then_inc(den_copied, 1)
                nc.scalar.copy(acc[:, j], pv_bank).then_inc(acc_copied, 1)

            def body(u):
                for t in range(NS):
                    exps(u, t)
                    if t in (1, 4) and exists(u.plus(2)):
                        rope_his(u.plus(2), t // 4, u.plus(1).at(96, 0) if t == 1 else None)
                    if t == 4:
                        sums_copy(u, 0)
                sums_copy(u, 1)
                if exists(u.plus(2)):
                    act.wait_ge(rope_stored, u.plus(2).at(64, 64))
                if exists(u.plus(1)):
                    mrow_copy(u.plus(1))
                if u.g == 0 and exists(u.plus(NG)):
                    for i in range(ST):
                        x_hi(u.b + 1, i)
                if u.g == NG - 1 and exists(u.plus(NG)):
                    for i in range(ST):
                        v_copy(u.b + 1, i)

            act.wait_ge(consts_ready, 5)
            act.wait_ge(mv_ready, 1)
            nc.scalar.activation(root[:], mv[:, :, 1], ACT.Sqrt, bias=eps_col[:]).then_inc(root_ready, 1)
            for i in range(ST):
                x_hi(0, i)
            for i in range(ST):
                v_copy(0, i)
            for u in (U0, U0.plus(1)):
                rope_his(u, 0)
                rope_his(u, 1)
            mrow_copy(U0)
            each_batch(act, body)

        @block.vector
        def _(dve):
            def normalise(b, i):
                dve.wait_ge(xt_loaded[i % XR], b * (ST // XR * 16) + (i // XR * 16 + 16))
                nc.vector.tensor_scalar(xt[:, i % XR], xt[:, i % XR], mv[:, bass.ds(b * ST + i, 1), 0], rstd[:, bass.ds(b * ST + i, 1)],
                                        ALU.subtract, ALU.mult).then_inc(xt_ready, 1)

            def x_lo(b, i):
                dve.wait_ge(xh_ready, b * ST + (i + 1))
                t = slice(i * P, (i + 1) * P)
                nc.vector.tensor_tensor(xl[:, :, t], t_bank(i).rearrange("p (k t) -> p k t", k=KT),
                                        xh[:, :, t].bitcast(F32), ALU.subtract).then_inc(xl_ready, 1)

            def turn(b, i0, i1):
                for i in range(i0, i1):
                    if i >= XR:
                        normalise(b, i)
                    x_lo(b, i)

            def rope(u, reused):
                for f in range(2):
                    a, c = qk_bank(f)
                    p = slice(f * QB, (f + 1) * QB)
                    dve.wait_ge(qk_filled, u.at(4, 2 * f + 2))
                    if reused:
                        dve.wait_ge(rope_lo, u.at(4, 2 * f - 2))
                    nc.vector.tensor_tensor(ra[:, f, 0], a, cos[:, p], ALU.mult)
                    nc.vector.tensor_tensor(ra[:, f, 1], a, sin[:, p], ALU.mult)
                    nc.vector.tensor_tensor(rb[:, f, 0], c, sin[:, p], ALU.mult)
                    nc.vector.tensor_tensor(rb[:, f, 1], c, cos[:, p], ALU.mult).then_inc(qk_read, 1)

            def piece_max(u, c):
                h, (i, k0, k1) = c // len(PIECES), PIECES[c % len(PIECES)]
                dve.wait_ge(mx_filled, u.at(NP, c + 1))
                nc.vector.tensor_reduce(mxp[:, h, c % len(PIECES):c % len(PIECES) + 1], w_bank[c % 2][:, 0:k1 - k0], AX.X,
                                        ALU.max).then_inc(mx_read, 1)

            def row_max(u):
                dve.wait_ge(mx_read, u.at(NP, NP))
                dve.wait_ge(mrow_turned, u.at(1, 0))
                n1 = QB // P
                nc.vector.tensor_scalar(mneg[:, :, 0:n1], mxp[:, :, 0:n1], -1.0, None, ALU.mult)
                nc.vector.tensor_reduce(mneg[:, :, n1:ST], mxp[:, :, n1:].rearrange("p h (i c) -> p h i c", c=2), AX.X,
                                        ALU.max, negate=True).then_inc(mneg_ready, 1)

            def invert(u, j):
                dve.wait_ge(den_copied, u.at(2, j + 1))
                nc.vector.reciprocal(den[:, j], den[:, j]).then_inc(inv_ready, 1)

            def body(u):
                for t in range(NS):
                    if exists(u.plus(1)):
                        for c in range(4 * t, 4 * t + 4):
                            piece_max(u.plus(1), c)
                    if u.g == 0 and t < XR and exists(u.plus(NG)):
                        normalise(u.b + 1, t)
                    if t == 5:
                        invert(u, 0)
                if exists(u.plus(1)):
                    row_max(u.plus(1))
                invert(u, 1)
                if exists(u.plus(3)):
                    rope(u.plus(3), True)
                if u.g == 0 and exists(u.plus(NG)):
                    turn(u.b + 1, 0, ST)

            nc.vector.memset(ks[3 * HD:3 * HD + 1].bitcast(F32), 1.0).then_inc(consts_ready, 1)
            dve.wait_ge(stats_loaded, 16)
            for i in range(nbatch * ST):
                ins = nc.vector.bn_aggr(mv[:, i], stats[:, i])
            ins.then_inc(mv_ready, 1)
            dve.wait_ge(root_ready, 1)
            nc.vector.reciprocal(rstd[:], root[:]).then_inc(rstd_step, 1)
            dve.wait_ge(rstd_step, 1)
            nc.vector.tensor_tensor(newton[:], rstd[:], rstd[:], ALU.mult).then_inc(rstd_step, 1)
            dve.wait_ge(rstd_step, 2)
            nc.vector.scalar_tensor_tensor(newton[:], mv[:, :, 1], LN_EPS, newton[:], ALU.add, ALU.mult).then_inc(rstd_step, 1)
            dve.wait_ge(rstd_step, 3)
            nc.vector.tensor_scalar(newton[:], newton[:], -0.5, 1.5, ALU.mult, ALU.add).then_inc(rstd_step, 1)
            dve.wait_ge(rstd_step, 4)
            nc.vector.tensor_tensor(rstd[:], rstd[:], newton[:], ALU.mult).then_inc(rstd_step, 1)
            dve.wait_ge(rstd_step, 5)
            for i in range(XR):
                normalise(0, i)
            turn(0, 0, ST)
            dve.wait_ge(tables_loaded, 32)
            rope(U0, False)
            rope(U0.plus(1), True)
            for c in range(NP):
                piece_max(U0, c)
            row_max(U0)
            rope(U0.plus(2), True)
            each_batch(dve, body)

        @block.tensor
        def _(pe):
            def turn(b, i):
                pe.wait_ge(xt_ready, b * ST + (i + 1))
                if i >= 4:
                    pe.wait_ge(xl_ready, b * ST + (i - 3))
                for k in range(KT):
                    mm = nc.tensor.transpose(t_bank(i)[:, k * P:(k + 1) * P], xt[:, i % XR, k * P:(k + 1) * P], ident[:])
                mm.then_inc(xt_turned, 1)

            def project_v(b, i):
                if i >= 2:
                    pe.wait_ge(v_ready, b * ST + (i - 1))
                t = slice(i * P, (i + 1) * P)
                for k in range(KT):
                    nc.tensor.matmul(w_bank[i % 2], xh[:, k, t], wv[:, 0, k], start=k == 0, stop=False)
                    nc.tensor.matmul(w_bank[i % 2], xh[:, k, t], wv[:, 1, k], start=False, stop=False)
                    mm = nc.tensor.matmul(w_bank[i % 2], xl[:, k, t], wv[:, 0, k], start=False, stop=k == KT - 1)
                mm.then_inc(v_filled, 1)

            def project_qk(u, f, r):
                pe.wait_ge(wqk_loaded[u.g % 2], u.ring(16, 16))
                pe.wait_ge(xl_ready, u.b * ST + ST)
                t = slice(f * QB, (f + 1) * QB)
                bank = qk_bank(f)[r]
                w = wqk[:, u.g % 2]
                for k in range(KT):
                    nc.tensor.matmul(bank, w[:, 0, k, r], xh[:, k, t], start=k == 0, stop=False)
                    nc.tensor.matmul(bank, w[:, 0, k, r], xl[:, k, t], start=False, stop=False)
                    mm = nc.tensor.matmul(bank, w[:, 1, k, r], xh[:, k, t], start=False, stop=k == KT - 1)
                mm.then_inc(qk_filled, 1)

            def piece(u, c):
                h, (i, k0, k1) = c // len(PIECES), PIECES[c % len(PIECES)]
                if c == 0:
                    pe.wait_ge(placed, u.at(96, 96))
                if c >= 2:
                    pe.wait_ge(mx_read, u.at(NP, c - 1))
                diag = k1 == (i + 1) * P
                bank = w_bank[c % 2]
                if diag:
                    nc.tensor.matmul(bank[:, k1 - k0 - P:k1 - k0], ident_b[:], hide_k[:], start=True, stop=False,
                                     skip_group_check=True)
                nc.tensor.matmul(bank[:, 0:k1 - k0], qs[0:3 * HD, u.g % 2, h, i * P:(i + 1) * P],
                                 ks[0:3 * HD, u.g % 2, h, k0:k1], start=not diag, stop=True,
                                 skip_group_check=True).then_inc(mx_filled, 1)

            def turn_mrow(u):
                pe.wait_ge(mneg_ready, u.at(1, 1))
                nc.tensor.transpose(s_bank[0][0:GH * ST, 0, 0:P], mneg[:].rearrange("p h i -> p (h i)"),
                                    ident[:]).then_inc(mrow_turned, 1)

            def scores(u, t):
                qb, kt = STEPS[t]
                first = max(kt * P - qb * QB, 0)
                for hp in range(2):
                    if t == 0 and hp == 0:
                        pe.wait_ge(mrow_placed, u.at(16, 16))
                    if t == 0 and hp == 1 and exists(u.plus(2)):
                        pe.wait_ge(qk_read, u.plus(2).at(2, 2))
                    if t > 0:
                        pe.wait_ge(exp_done, u.at(2 * NS, 2 * t + hp - 1))
                    for h in (2 * hp, 2 * hp + 1):
                        diag = kt * P >= qb * QB
                        bank = s_bank[hp][:, h % 2]
                        if diag:
                            nc.tensor.matmul(bank[:, first:first + P], ident_b[:], hide_q[:], start=True, stop=False,
                                             skip_group_check=True)
                        mm = nc.tensor.matmul(bank[:, first:QB], ks[0:3 * HD + 1, u.g % 2, h, kt * P:(kt + 1) * P],
                                              qs[0:3 * HD + 1, u.g % 2, h, qb * QB + first:(qb + 1) * QB],
                                              start=not diag, stop=True, skip_group_check=True)
                    mm.then_inc(s_filled, 1)

            def weigh(u, t):
                qb, kt = STEPS[t]
                first = max(kt * P - qb * QB, 0)
                opening = kt == (qb + 1) * QB // P - 1
                pe.wait_ge(exp_done, u.at(2 * NS, 2 * t + 2))
                if opening and qb > 0:
                    pe.wait_ge(acc_copied, u.at(2, qb))
                    pe.wait_ge(den_copied, u.at(2, qb))
                for h in range(GH):
                    rows = slice(h * HD, (h + 1) * HD)
                    nc.tensor.matmul(pv_bank[rows, first:QB], v[:, kt, u.g * P + h * HD:u.g * P + (h + 1) * HD],
                                     probs[:, t % 2, h, first:QB], start=opening, stop=kt == 0, skip_group_check=True)
                for h in range(GH):
                    rows = slice(h * HD, (h + 1) * HD)
                    mm = nc.tensor.matmul(den_bank[rows, first:QB], ones[:], probs[:, t % 2, h, first:QB],
                                          start=opening, stop=kt == 0, skip_group_check=True)
                mm.then_inc(pv_done, 1)

            def body(u):
                if u.g == 0:
                    pe.wait_ge(v_ready, u.b * ST + ST)
                if u.g == 1 and exists(u.plus(NG)):
                    pe.wait_ge(xl_ready, u.b * ST + 2 * ST)
                scores(u, 0)
                for t in range(NS):
                    if t + 1 < NS:
                        scores(u, t + 1)
                    if exists(u.plus(1)):
                        for c in range(4 * t, 4 * t + 4):
                            if c == 0 and exists(u.plus(2)):
                                pe.wait_ge(qk_read, u.plus(2).at(2, 1))
                            piece(u.plus(1), c)
                    weigh(u, t)
                if exists(u.plus(3)):
                    pe.wait_ge(mx_read, u.plus(1).at(NP, NP))
                    project_qk(u.plus(3), 0, 0)
                if exists(u.plus(1)):
                    turn_mrow(u.plus(1))
                if exists(u.plus(3)):
                    project_qk(u.plus(3), 0, 1)
                    project_qk(u.plus(3), 1, 0)
                    project_qk(u.plus(3), 1, 1)
                if u.g == 0 and exists(u.plus(NG)):
                    pe.wait_ge(qk_read, u.plus(3).at(2, 1))
                    pe.wait_ge(mrow_copied, u.plus(1).at(1, 1))
                    for i in range(ST):
                        turn(u.b + 1, i)
                if u.g == NG - 1 and exists(u.plus(NG)):
                    pe.wait_ge(qk_read, u.plus(3).at(2, 1))
                    for i in range(ST):
                        project_v(u.b + 1, i)

            pe.wait_ge(consts_ready, 5)
            for i in range(ST):
                turn(0, i)
            pe.wait_ge(wv_loaded, 16)
            pe.wait_ge(xl_ready, ST)
            for i in range(ST):
                project_v(0, i)
            pe.wait_ge(v_ready, ST)
            for n in range(2):
                for f in range(2):
                    if n:
                        pe.wait_ge(qk_read, f + 1)
                    project_qk(U0.plus(n), f, 0)
                    project_qk(U0.plus(n), f, 1)
            pe.wait_ge(qk_read, 4)
            for c in range(NP):
                piece(U0, c)
            turn_mrow(U0)
            pe.wait_ge(mx_read, NP)
            for f in range(2):
                project_qk(U0.plus(2), f, 0)
                project_qk(U0.plus(2), f, 1)
            each_batch(pe, body)


def rope_tables():
    inv = 1.0 / np.power(np.float32(10000.0), np.arange(HALF, dtype=np.float32) / np.float32(HALF), dtype=np.float32)
    angle = np.outer(np.arange(SEQ, dtype=np.float32), inv.astype(np.float32)).astype(np.float32)
    return [np.ascontiguousarray(np.tile(f(angle).astype(np.float32).T, (P // HALF, 1))) for f in (np.cos, np.sin)]


def build(nc, a, out):
    x = a["x"].rearrange("b t d -> (b t) d")
    y = out.rearrange("b t d -> (b t) d")
    tokens = x.shape[0]
    nblocks, nbatch = tokens // TB, tokens // SEQ

    def scratch(name, shape, dt):
        return nc.dram_tensor(name, shape, dt, kind="Internal").ap()

    x1 = scratch("x1", [tokens, D], F32)
    moments = scratch("moments", [nblocks, P, TT, 6], F32)
    att = scratch("att", [D, tokens], F32)
    wqk = scratch("wqk_parts", [NG, 2, KT, P, 2 * P], F32)
    wv = scratch("wv_parts", [2, D, D], F32)
    wo = scratch("wo_turned", [D, D], F32)
    rope_tmp = scratch("rope_tmp", [2, 2, 2 * P, SEQ], F32)
    mrow_tmp = scratch("mrow_tmp", [GH * ST, P], F32)
    with nc.psum_tensor("banks", [P, 8, D], F32) as psum:
        prepare_weights(nc, psum, a["w_q"], a["w_k"], a["w_v"], a["w_o"], wqk, wv, wo)
        ffn_phase(nc, psum, "ffn1", nblocks, x, x1, a["router_w"], a["w_a"], a["w_b"], moments_dst=moments)
        attention_phase(nc, psum, nbatch, x1, moments.rearrange("n p j c -> p n (j c)"), wqk, wv, a["cos"], a["sin"],
                        att, rope_tmp, mrow_tmp)
        ffn_phase(nc, psum, "ffn2", nblocks, x1, y, a["router_w"], a["w_a"], a["w_b"], y_src=att, w_o=wo)


def kernel(L0_attn_x, L0_attn_w_q, L0_attn_w_k, L0_attn_w_v, L0_attn_w_o, L0_ffn_router_w, L0_ffn_Wa, L0_ffn_Wb):
    import concourse.bacc as bacc
    from concourse.bass_utils import run_bass_kernel_spmd

    cos, sin = rope_tables()
    arrays = {"x": L0_attn_x, "w_q": L0_attn_w_q, "w_k": L0_attn_w_k, "w_v": L0_attn_w_v, "w_o": L0_attn_w_o,
              "router_w": L0_ffn_router_w, "w_a": L0_ffn_Wa, "w_b": L0_ffn_Wb, "cos": cos, "sin": sin}
    arrays = {k: np.ascontiguousarray(v) for k, v in arrays.items()}
    nc = bacc.Bacc("TRN2", target_bir_lowering=False, num_devices=1)
    a = {k: nc.dram_tensor(k, v.shape, mybir.dt.from_np(v.dtype), kind="ExternalInput").ap() for k, v in arrays.items()}
    out = nc.dram_tensor("out", arrays["x"].shape, F32, kind="ExternalOutput").ap()
    build(nc, a, out)
    result = run_bass_kernel_spmd(nc, [arrays], core_ids=[0])
    return result.results[0]["out"]
```

```python
from contextlib import ExitStack

import numpy as np
import concourse.bass as bass
from concourse import mybir

ALU = mybir.AluOpType
ACT = mybir.ActivationFunctionType
AX = mybir.AxisListType
F32 = mybir.dt.float32
F32R = mybir.dt.float32r
BF16 = mybir.dt.bfloat16

P = 128
D = 512
KT = D // P
NE = 8
RANK = 128
TB = 512
TT = TB // P
LN_EPS = 1e-5
NORM_MIN = 1e-12
BIG = 1e30


class Block2:

    def __init__(self, pair, parity):
        self.pair, self.parity = pair, parity

    def at(self, k, c):
        return self.pair * (2 * k) + (self.parity * k + c)

    def next(self):
        return Block2(self.pair, 1) if self.parity == 0 else Block2(self.pair + 1, 0)

    def index(self):
        return self.pair * 2 + self.parity


def each_block(engine, nblocks, body):
    last = nblocks // 2 - 1
    with engine.Fori(0, last) as pair:
        body(Block2(pair, 0), True, True)
        body(Block2(pair, 1), True, True)
    body(Block2(last, 0), True, False)
    body(Block2(last, 1), False, False)


def ffn_phase(nc, psum, tag, nblocks, x_src, x_dst, w_router, w_a, w_b, moments_dst=None, y_src=None, w_o=None):
    with_o = y_src is not None
    HS = 2
    STAGES = 4
    STORES = 16 * (1 if moments_dst is None else 2)
    LAG = 1 if with_o else 0
    with ExitStack() as ctx:
        def sb(name, shape, dt):
            return ctx.enter_context(nc.sbuf_tensor(f"{tag}_{name}", shape, dt))

        def sem(name):
            return ctx.enter_context(nc.semaphore(f"{tag}_{name}"))

        ident = sb("ident", [P, P], F32)
        eps_col = sb("eps_col", [P, 1], F32)
        zero_col = sb("zero_col", [P, 1], F32)
        wa = sb("wa", [P, KT, 2, NE * RANK], F32R)
        wb = sb("wb", [P, NE, 2, D], F32R)
        wr = sb("wr", [P, KT, 4, NE], F32R)
        wr_raw = sb("wr_raw", [P, KT, NE], F32)
        fold = sb("fold", [2 * NE, NE], F32)
        first_w = sb("first_w", [P, TT, NE], F32)
        x = sb("x", [P, 2, TT, D], F32)
        xn = sb("xn", [P, TT, D], F32)
        xh = sb("xh", [P, KT, TB], F32R)
        xl = sb("xl", [P, KT, TB], F32R)
        hs = sb("hs", [P, HS, TB], F32)
        hh = sb("hh", [P, NE, TB], F32R)
        hl = sb("hl", [P, NE, TB], F32R)
        cb = sb("cb", [P, 2, TB], F32)
        stages = [x[:, 1, 0:2], x[:, 1, 2:4], hs[:], cb[:]]
        lg = sb("lg", [2 * NE, TB], F32)
        cm = sb("cm", [P, TT, P], F32R)
        own_tile = sb("own_tile", [P, TT], F32)
        rows_of = sb("rows_of", [P, 2 * NE], F32)
        spread = sb("spread", [P, NE, P], F32R)
        stats = sb("stats", [P, TT, 6], F32)
        mv = sb("mv", [P, TT, 2], F32)
        root = sb("root", [P, 2, TT], F32)
        inv0 = sb("inv0", [P, TT], F32)
        newton = sb("newton", [P, TT], F32)
        rstd = sb("rstd", [P, TT], F32)
        norm = sb("norm", [P, TT], F32)
        inv_norm = sb("inv_norm", [P, TT], F32)
        logit = sb("logit", [P, TT, NE], F32)
        hit = sb("hit", [P, TT, NE], F32)
        score = sb("score", [P, TT, NE], F32)
        top = [sb(f"top{i}", [P, TT, NE], F32) for i in range(2)]
        peak = sb("peak", [P, 2, TT], F32)
        who = sb("who", [P, TT], F32)
        gap = sb("gap", [P, TT], F32)
        ratio = sb("ratio", [P, TT], F32)
        gate = sb("gate", [P, 2, TT], F32)
        total = sb("total", [P, TT], F32)
        comb = sb("comb", [P, NE, TT], F32)
        comb_parts = sb("comb_parts", [P, 4, NE, TT], F32R)
        if moments_dst is not None:
            out_stats = sb("out_stats", [P, 2, TT, 6], F32)
        if with_o:
            wo = sb("wo", [P, KT, 2, D], F32R)
            yt = sb("yt", [P, KT, TB], F32)
            yh = sb("yh", [P, KT, TB], F32R)
            yl = sb("yl", [P, KT, TB], F32R)

        banks = [psum[:, i] for i in range(8)]
        t_bank, h_bank, o_bank, m_bank = banks[0:2], banks[2:5], banks[5:7], banks[7]

        zeroed = sem("zeroed")
        cols_ready = sem("cols_ready")
        ident_ready = sem("ident_ready")
        consts_ready = sem("consts_ready")
        w_loaded = [sem(f"w_loaded{s}") for s in range(STAGES)]
        w_hi = sem("w_hi")
        w_lo = sem("w_lo")
        wr_loaded = sem("wr_loaded")
        wr_step = sem("wr_step")
        x_loaded = [sem("x_loaded0"), sem("x_loaded1")]
        x_stored = [sem("x_stored0"), sem("x_stored1")]
        dve_step = sem("dve_step")
        stats_ready = sem("stats_ready")
        var_ready = sem("var_ready")
        root_ready = sem("root_ready")
        xn_ready = sem("xn_ready")
        t_filled = sem("t_filled")
        xh_ready = sem("xh_ready")
        xl_ready = sem("xl_ready")
        lg_filled = sem("lg_filled")
        lg_copied = sem("lg_copied")
        lt_filled = sem("lt_filled")
        gap_ready = sem("gap_ready")
        ratio_ready = sem("ratio_ready")
        comb_ready = sem("comb_ready")
        ct_filled = sem("ct_filled")
        cm_ready = sem("cm_ready")
        cb_filled = sem("cb_filled")
        cb_ready = sem("cb_ready")
        h_filled = sem("h_filled")
        h_scaled = sem("h_scaled")
        hh_ready = sem("hh_ready")
        hl_ready = sem("hl_ready")
        o_filled = sem("o_filled")
        o_added = sem("o_added")
        y_loaded = sem("y_loaded")
        yh_ready = sem("yh_ready")
        yl_ready = sem("yl_ready")
        res_filled = sem("res_filled")
        res_added = sem("res_added")
        out_stats_ready = sem("out_stats_ready")

        pieces = []
        if with_o:
            wo_v = w_o.rearrange("(c p) n -> p c n", p=P)
            for c in range(0, KT, 2):
                pieces.append((wo_v[:, c:c + 2], wo[:, c:c + 2, 0], wo[:, c:c + 2, 1], 2))
        for k in range(KT):
            pieces.append((w_a[:, k * P:(k + 1) * P, :].rearrange("e p r -> p e r"),
                           wa[:, k, 0].rearrange("p (e r) -> p e r", e=NE),
                           wa[:, k, 1].rearrange("p (e r) -> p e r", e=NE), NE))
        for e in range(0, NE, 2):
            pieces.append((w_b[e:e + 2].rearrange("e p n -> p e n"), wb[:, e:e + 2, 0], wb[:, e:e + 2, 1], 2))
        n_pieces = len(pieces)

        def staged(c, parts):
            flat = stages[c % STAGES].rearrange("p j d -> p (j d)")
            return flat.rearrange("p (a n) -> p a n", a=parts)

        x_in = x_src.rearrange("(n j p) d -> n p j d", p=P, j=TT)
        x_out = x_dst.rearrange("(n j p) d -> n p j d", p=P, j=TT)
        y_in = y_src.rearrange("(c p) (n t) -> n p c t", p=P, t=TB) if with_o else None
        first, second = Block2(0, 0), Block2(0, 1)

        block = ctx.enter_context(nc.Block())

        @block.sync
        def _(sp):
            def load_x(m):
                sp.dma_start(x[:, m.parity], x_in[m.index()]).then_inc(x_loaded[m.parity], 16)

            def load_y(m):
                sp.wait_ge(yl_ready, m.at(KT, 0))
                sp.dma_start(yt[:], y_in[m.index()]).then_inc(y_loaded, 16)

            def body(n, look, look2):
                if look2 and with_o:
                    load_y(n.next().next())
                sp.wait_ge(o_added, n.at(TT, TT))
                sp.dma_start(x_out[n.index()], x[:, n.parity]).then_inc(x_stored[n.parity], 16)
                if moments_dst is not None:
                    sp.wait_ge(out_stats_ready, n.at(1, 1))
                    sp.dma_start(moments_dst[n.index()], out_stats[:, n.parity]).then_inc(x_stored[n.parity], 16)
                if look2:
                    sp.wait_ge(x_stored[n.parity], (n.pair + 1) * STORES)
                    load_x(n.next().next())

            load_x(first)
            sp.dma_start(wr_raw[:], w_router.rearrange("(k p) e -> p k e", p=P)).then_inc(wr_loaded, 16)
            if with_o:
                load_y(first)
            for c, (src, _, _, parts) in enumerate(pieces):
                if c >= STAGES:
                    sp.wait_ge(w_lo, c - STAGES + 1)
                sp.dma_start(staged(c, parts), src).then_inc(w_loaded[c % STAGES], 16)
            sp.wait_ge(w_lo, n_pieces)
            load_x(second)
            if with_o:
                load_y(second)
            each_block(sp, nblocks, body)
            for parity in range(2):
                sp.wait_ge(x_stored[parity], STORES * (nblocks // 2))

        @block.gpsimd
        def _(pool):
            nc.gpsimd.memset(eps_col[:], LN_EPS).then_inc(cols_ready, 1)
            nc.gpsimd.memset(zero_col[:], 0.0).then_inc(cols_ready, 1)
            nc.gpsimd.memset(ident[:], 0.0).then_inc(zeroed, 1)
            pool.wait_ge(zeroed, 1)
            nc.gpsimd.affine_select(out=ident[:], in_=ident[:], compare_op=ALU.not_equal, fill=1.0, base=0,
                                    pattern=[[-1, P]], channel_multiplier=1).then_inc(ident_ready, 1)
            nc.gpsimd.memset(fold[:], 0.0).then_inc(zeroed, 1)
            nc.gpsimd.iota(first_w[:], pattern=[[0, TT], [-1, NE]], base=NE, channel_multiplier=0,
                           allow_small_or_imprecise_dtypes=True).then_inc(consts_ready, 1)
            pool.wait_ge(zeroed, 2)
            nc.gpsimd.affine_select(out=fold[:], in_=fold[:], compare_op=ALU.not_equal, fill=1.0, base=0,
                                    pattern=[[-1, NE]], channel_multiplier=1).then_inc(zeroed, 1)
            pool.wait_ge(zeroed, 3)
            nc.gpsimd.affine_select(out=fold[:], in_=fold[:], compare_op=ALU.not_equal, fill=1.0, base=-NE,
                                    pattern=[[-1, NE]], channel_multiplier=1).then_inc(consts_ready, 1)
            nc.gpsimd.memset(own_tile[:], 0.0).then_inc(zeroed, 1)
            nc.gpsimd.memset(rows_of[:], 0.0).then_inc(zeroed, 1)
            pool.wait_ge(zeroed, 5)
            for a in range(2 * NE):
                nc.gpsimd.affine_select(out=own_tile[:], in_=own_tile[:], compare_op=ALU.not_equal, fill=1.0,
                                        base=-TT * a, pattern=[[-1, TT]], channel_multiplier=1).then_inc(zeroed, 1)
                pool.wait_ge(zeroed, 6 + a)
            nc.gpsimd.memset(rows_of[0:2 * NE * TT], 1.0).then_inc(zeroed, 1)
            pool.wait_ge(zeroed, 22)
            nc.gpsimd.affine_select(out=rows_of[:], in_=rows_of[:], compare_op=ALU.is_ge, fill=0.0, base=0,
                                    pattern=[[-TT, 2 * NE]], channel_multiplier=1).then_inc(zeroed, 1)
            pool.wait_ge(zeroed, 23)
            nc.gpsimd.affine_select(out=rows_of[:], in_=rows_of[:], compare_op=ALU.is_ge, fill=0.0, base=TT - 1,
                                    pattern=[[TT, 2 * NE]], channel_multiplier=-1).then_inc(consts_ready, 1)

            def split_y(m):
                for k in range(KT):
                    pool.wait_ge(yh_ready, m.at(KT, k + 1))
                    nc.gpsimd.tensor_tensor(yl[:, k], yt[:, k], yh[:, k].bitcast(F32),
                                            ALU.subtract).then_inc(yl_ready, 1)

            def body(n, look, look2):
                for e in range(NE):
                    pool.wait_ge(hh_ready, n.at(NE, e + 1))
                    nc.gpsimd.tensor_tensor(hl[:, e], hs[:, e % HS], hh[:, e].bitcast(F32),
                                            ALU.subtract).then_inc(hl_ready, 1)
                    if e == 3 and look2 and with_o:
                        split_y(n.next().next())

            if with_o:
                split_y(first)
                split_y(second)
            each_block(pool, nblocks, body)

        @block.scalar
        def _(act):
            def roots(m):
                act.wait_ge(var_ready, m.at(1, 1))
                nc.scalar.activation(root[:, 0], mv[:, :, 1], ACT.Sqrt, bias=eps_col[:])
                nc.scalar.activation(root[:, 1], mv[:, :, 1], ACT.Sqrt, bias=zero_col[:],
                                     scale=float(D)).then_inc(root_ready, 1)

            def x_hi(m):
                for k in range(KT):
                    act.wait_ge(t_filled, m.at(KT, k + 1))
                    nc.scalar.copy(xh[:, k], t_bank[k % 2][:]).then_inc(xh_ready, 1)

            def logits_copy(m):
                act.wait_ge(lg_filled, m.at(1, 1))
                nc.scalar.copy(lg[:], m_bank[0:2 * NE, :]).then_inc(lg_copied, 1)

            def gap_exp(m):
                act.wait_ge(gap_ready, m.at(1, 1))
                nc.scalar.activation(ratio[:], gap[:], ACT.Exp, bias=zero_col[:]).then_inc(ratio_ready, 1)

            def cb_copy(n, e):
                act.wait_ge(cb_filled, n.at(NE, e + 1))
                if e >= 2:
                    act.wait_ge(h_scaled, n.at(NE, e - 1))
                nc.scalar.copy(cb[:, e % 2], m_bank[:]).then_inc(cb_ready, 1)

            def y_hi(m):
                act.wait_ge(y_loaded, m.at(16, 16))
                act.wait_ge(res_filled, m.at(TT, 0))
                for k in range(KT):
                    nc.scalar.copy(yh[:, k], yt[:, k]).then_inc(yh_ready, 1)

            def body(n, look, look2):
                cb_copy(n, 0)
                for e in range(NE):
                    if e + 1 < NE:
                        cb_copy(n, e + 1)
                    act.wait_ge(h_scaled, n.at(NE, e + 1))
                    nc.scalar.copy(hh[:, e], hs[:, e % HS]).then_inc(hh_ready, 1)
                    if e == 3 and look2 and with_o:
                        y_hi(n.next().next())
                    if e == 3 + LAG and look:
                        roots(n.next())
                if look:
                    x_hi(n.next())
                    logits_copy(n.next())
                    gap_exp(n.next())

            act.wait_ge(cols_ready, 2)
            if with_o:
                y_hi(first)
            if not with_o:
                roots(first)
            for c, (_, hi, _, parts) in enumerate(pieces):
                act.wait_ge(w_loaded[c % STAGES], 16 * (c // STAGES + 1))
                nc.scalar.copy(hi, staged(c, parts)).then_inc(w_hi, 1)
            if with_o:
                y_hi(second)
                roots(first)
            x_hi(first)
            logits_copy(first)
            gap_exp(first)
            each_block(act, nblocks, body)

        @block.vector
        def _(dve):
            LINKS = 26
            taken = [0]

            def link(m, ins):
                taken[0] += 1
                ins.then_inc(dve_step, 1)
                dve.wait_ge(dve_step, m.at(LINKS, taken[0]))

            def wide(col):
                return col.unsqueeze(2).to_broadcast([P, TT, NE])

            def x_ready(m):
                dve.wait_ge(x_loaded[m.parity], m.pair * 16 + 16)
                if with_o:
                    for j in range(TT):
                        dve.wait_ge(res_filled, m.at(TT, j + 1))
                        nc.vector.tensor_tensor(x[:, m.parity, j], o_bank[j % 2][:], x[:, m.parity, j],
                                                ALU.add).then_inc(res_added, 1)
                    dve.wait_ge(res_added, m.at(TT, TT))

            def moments(m, j):
                nc.vector.bn_stats(stats[:, j], x[:, m.parity, j]).then_inc(stats_ready, 1)

            def aggregate(m):
                for i in range(TT):
                    ins = nc.vector.bn_aggr(mv[:, i], stats[:, i])
                ins.then_inc(var_ready, 1)

            def scales(m):
                dve.wait_ge(root_ready, m.at(1, 1))
                link(m, nc.vector.reciprocal(inv0[:], root[:, 0]))
                link(m, nc.vector.tensor_tensor(newton[:], inv0[:], inv0[:], ALU.mult))
                link(m, nc.vector.scalar_tensor_tensor(newton[:], mv[:, :, 1], LN_EPS, newton[:], ALU.add, ALU.mult))
                link(m, nc.vector.tensor_scalar(newton[:], newton[:], -0.5, 1.5, ALU.mult, ALU.add))
                link(m, nc.vector.tensor_tensor(rstd[:], inv0[:], newton[:], ALU.mult))
                link(m, nc.vector.tensor_tensor(norm[:], root[:, 1], rstd[:], ALU.mult))
                link(m, nc.vector.tensor_scalar(norm[:], norm[:], NORM_MIN, None, ALU.max))
                link(m, nc.vector.reciprocal(inv_norm[:], norm[:]))

            def normalise(m):
                dve.wait_ge(t_filled, m.at(KT, 0))
                for j in range(TT):
                    ins = nc.vector.tensor_scalar(xn[:, j], x[:, m.parity, j], mv[:, j, 0:1], rstd[:, j:j + 1],
                                                  ALU.subtract, ALU.mult)
                ins.then_inc(xn_ready, 1)

            def x_lo(m):
                for k in range(KT):
                    dve.wait_ge(xh_ready, m.at(KT, k + 1))
                    nc.vector.tensor_tensor(xl[:, k], t_bank[k % 2][:], xh[:, k].bitcast(F32),
                                            ALU.subtract).then_inc(xl_ready, 1)

            def pick(m, i):
                link(m, nc.vector.tensor_reduce(peak[:, i], logit[:], AX.X, ALU.max))
                link(m, nc.vector.tensor_tensor(hit[:], logit[:], wide(peak[:, i]), ALU.is_equal))
                link(m, nc.vector.tensor_tensor(score[:], hit[:], first_w[:], ALU.mult))
                link(m, nc.vector.tensor_reduce(who[:], score[:], AX.X, ALU.max))
                link(m, nc.vector.tensor_tensor(top[i][:], score[:], wide(who[:]), ALU.is_equal))

            def route(m):
                dve.wait_ge(lt_filled, m.at(1, 1))
                link(m, nc.vector.tensor_tensor(logit[:], m_bank[:, 0:TT * NE].rearrange("p (j e) -> p j e", e=NE),
                                                wide(inv_norm[:]), ALU.mult))
                pick(m, 0)
                link(m, nc.vector.scalar_tensor_tensor(logit[:], top[0][:], -BIG, logit[:], ALU.mult, ALU.add))
                pick(m, 1)
                nc.vector.tensor_tensor(gap[:], peak[:, 1], peak[:, 0], ALU.subtract).then_inc(gap_ready, 1)
                dve.wait_ge(ratio_ready, m.at(1, 1))
                link(m, nc.vector.tensor_scalar(total[:], ratio[:], 1.0, None, ALU.add))
                link(m, nc.vector.reciprocal(gate[:, 0], total[:]))
                link(m, nc.vector.tensor_tensor(gate[:, 1], ratio[:], gate[:, 0], ALU.mult))
                nc.vector.tensor_tensor(score[:], top[0][:], wide(gate[:, 0]), ALU.mult)
                link(m, nc.vector.tensor_tensor(hit[:], top[1][:], wide(gate[:, 1]), ALU.mult))
                link(m, nc.vector.tensor_tensor(comb[:].rearrange("p e j -> p j e"), score[:], hit[:], ALU.add))
                dve.wait_ge(ct_filled, m.at(1, 0))
                link(m, nc.vector.tensor_copy(comb_parts[:, 0], comb[:]))
                nc.vector.tensor_tensor(comb_parts[:, 1], comb[:], comb_parts[:, 0].bitcast(F32),
                                        ALU.subtract).then_inc(comb_ready, 1)
                assert taken[0] == LINKS

            def mask_combine(m):
                dve.wait_ge(cb_filled, m.at(NE, 0))
                dve.wait_ge(ct_filled, m.at(1, 1))
                nc.vector.tensor_tensor(cm[:], m_bank[:, 0:P].unsqueeze(1).to_broadcast([P, TT, P]),
                                        own_tile[:].unsqueeze(2).to_broadcast([P, TT, P]),
                                        ALU.mult).then_inc(cm_ready, 1)

            def add_out(n, j):
                dve.wait_ge(o_filled, n.at(TT, j + 1))
                nc.vector.scalar_tensor_tensor(x[:, n.parity, j], o_bank[j % 2][:], 0.5, x[:, n.parity, j],
                                               ALU.mult, ALU.add).then_inc(o_added, 1)

            def out_moments(n):
                dve.wait_ge(o_added, n.at(TT, TT))
                for j in range(TT):
                    ins = nc.vector.bn_stats(out_stats[:, n.parity, j], x[:, n.parity, j])
                ins.then_inc(out_stats_ready, 1)

            def body(n, look, look2):
                m = n.next()
                taken[0] = 0
                for e in range(NE):
                    dve.wait_ge(cb_ready, n.at(NE, e + 1))
                    dve.wait_ge(h_filled, n.at(NE, e + 1))
                    if e >= HS:
                        dve.wait_ge(hl_ready, n.at(NE, e - HS + 1))
                    if look and e == 2 + LAG:
                        dve.wait_ge(stats_ready, m.at(TT, TT))
                    nc.vector.tensor_tensor(hs[:, e % HS], h_bank[e % 3][:], cb[:, e % 2], ALU.mult).then_inc(h_scaled, 1)
                    if not look:
                        continue
                    if e == LAG:
                        x_ready(m)
                    if e in (LAG, LAG + 1):
                        moments(m, 2 * (e - LAG))
                        moments(m, 2 * (e - LAG) + 1)
                    if e == 2 + LAG:
                        aggregate(m)
                    if e == 4 + LAG:
                        scales(m)
                    if e == 5 + LAG:
                        normalise(m)
                if look:
                    x_lo(m)
                add_out(n, 0)
                add_out(n, 1)
                if look:
                    route(m)
                add_out(n, 2)
                if look:
                    mask_combine(m)
                add_out(n, 3)
                if moments_dst is not None:
                    out_moments(n)

            dve.wait_ge(wr_loaded, 16)
            nc.vector.memset(wr[:, :, 3].bitcast(F32), 0.0)
            nc.vector.tensor_copy(wr[:, :, 0], wr_raw[:])
            nc.vector.tensor_copy(wr[:, :, 2], wr_raw[:]).then_inc(wr_step, 1)
            dve.wait_ge(wr_step, 1)
            nc.vector.tensor_tensor(wr[:, :, 1], wr_raw[:], wr[:, :, 0].bitcast(F32), ALU.subtract).then_inc(wr_step, 1)
            nc.vector.memset(comb_parts[:, 2:4].bitcast(F32), 0.0)
            def first_tokens():
                x_ready(first)
                for j in range(TT):
                    moments(first, j)
                dve.wait_ge(stats_ready, TT)
                aggregate(first)
                scales(first)
                normalise(first)

            if not with_o:
                first_tokens()
            for c, (_, hi, lo, parts) in enumerate(pieces):
                dve.wait_ge(w_hi, c + 1)
                nc.vector.tensor_tensor(lo, staged(c, parts), hi.bitcast(F32), ALU.subtract).then_inc(w_lo, 1)
            if with_o:
                first_tokens()
            x_lo(first)
            dve.wait_ge(consts_ready, 3)
            for e in range(NE):
                nc.vector.tensor_tensor(spread[:, e], rows_of[:, e:e + 1].to_broadcast([P, P]),
                                        rows_of[:, NE + e:NE + e + 1].to_broadcast([P, P]),
                                        ALU.add).then_inc(wr_step, 1)
            route(first)
            mask_combine(first)
            each_block(dve, nblocks, body)

        @block.tensor
        def _(pe):
            def residual(m):
                pe.wait_ge(yl_ready, m.at(KT, KT))
                for j in range(TT):
                    if j >= 2:
                        pe.wait_ge(res_added, m.at(TT, j - 1))
                    t = slice(j * P, (j + 1) * P)
                    for k in range(KT):
                        nc.tensor.matmul(o_bank[j % 2][:], yh[:, k, t], wo[:, k, 0], start=k == 0, stop=False)
                        nc.tensor.matmul(o_bank[j % 2][:], yh[:, k, t], wo[:, k, 1], start=False, stop=False)
                        mm = nc.tensor.matmul(o_bank[j % 2][:], yl[:, k, t], wo[:, k, 0], start=False, stop=k == KT - 1)
                    mm.then_inc(res_filled, 1)

            def hidden(n, e):
                if e == 0:
                    pe.wait_ge(xl_ready, n.at(KT, KT))
                if e >= 3:
                    pe.wait_ge(h_scaled, n.at(NE, e - 2))
                r = slice(e * RANK, (e + 1) * RANK)
                for k in range(KT):
                    nc.tensor.matmul(h_bank[e % 3][:], wa[:, k, 0, r], xh[:, k], start=k == 0, stop=False)
                    nc.tensor.matmul(h_bank[e % 3][:], wa[:, k, 0, r], xl[:, k], start=False, stop=False)
                    mm = nc.tensor.matmul(h_bank[e % 3][:], wa[:, k, 1, r], xh[:, k], start=False, stop=k == KT - 1)
                mm.then_inc(h_filled, 1)

            def output(n, j, look, half):
                if half == 1:
                    pass
                elif j < 2:
                    if with_o and look:
                        pe.wait_ge(res_added, n.at(TT, 2 * TT))
                else:
                    pe.wait_ge(o_added, n.at(TT, j - 1))
                t = slice(j * P, (j + 1) * P)
                for e in range(NE // 2 * half, NE // 2 * (half + 1)):
                    if j == 0:
                        pe.wait_ge(hl_ready, n.at(NE, e + 1))
                    nc.tensor.matmul(o_bank[j % 2][:], hh[:, e, t], wb[:, e, 0], start=e == 0, stop=False)
                    nc.tensor.matmul(o_bank[j % 2][:], hh[:, e, t], wb[:, e, 1], start=False, stop=False)
                    mm = nc.tensor.matmul(o_bank[j % 2][:], hl[:, e, t], wb[:, e, 0], start=False, stop=e == NE - 1)
                if half == 1:
                    mm.then_inc(o_filled, 1)

            def turn_x(m, k):
                pe.wait_ge(xn_ready, m.at(1, 1))
                pe.wait_ge(xl_ready, m.at(KT, max(k - 1, 0)))
                for j in range(TT):
                    mm = nc.tensor.transpose(t_bank[k % 2][:, j * P:(j + 1) * P], xn[:, j, k * P:(k + 1) * P], ident[:])
                mm.then_inc(t_filled, 1)

            def logits(m):
                pe.wait_ge(xl_ready, m.at(KT, KT))
                pe.wait_ge(cb_ready, m.at(NE, 0))
                for k in range(KT):
                    nc.tensor.matmul(m_bank[0:2 * NE, :], wr[:, k, 0:2].rearrange("p a e -> p (a e)"), xh[:, k],
                                     start=k == 0, stop=False)
                    mm = nc.tensor.matmul(m_bank[0:2 * NE, :], wr[:, k, 2:4].rearrange("p a e -> p (a e)"), xl[:, k],
                                          start=False, stop=k == KT - 1)
                mm.then_inc(lg_filled, 1)

            def turn_logits(m):
                pe.wait_ge(lg_copied, m.at(1, 1))
                for j in range(TT):
                    mm = nc.tensor.matmul(m_bank[:, j * NE:(j + 1) * NE], lg[:, j * P:(j + 1) * P], fold[:],
                                          start=True, stop=True)
                mm.then_inc(lt_filled, 1)

            def turn_combine(m):
                pe.wait_ge(comb_ready, m.at(1, 1))
                nc.tensor.transpose(m_bank[:, 0:P], comb_parts[:].rearrange("p a e j -> p (a e j)").bitcast(F32),
                                    ident[:]).then_inc(ct_filled, 1)

            def spread_combine(n, e):
                if e == 0:
                    pe.wait_ge(cm_ready, n.at(1, 1))
                else:
                    pe.wait_ge(cb_ready, n.at(NE, e))
                nc.tensor.matmul(m_bank[:], spread[:, e], cm[:].rearrange("p j t -> p (j t)"),
                                 start=True, stop=True).then_inc(cb_filled, 1)

            def body(n, look, look2):
                m = n.next()
                for e in range(NE):
                    hidden(n, e)
                    spread_combine(n, e)
                    if e == 1 and look and with_o:
                        pe.wait_ge(h_scaled, n.at(NE, 1))
                        residual(m)
                between = {(0, 0): lambda: (turn_x(m, 0), turn_x(m, 1)), (0, 1): lambda: (turn_x(m, 2), turn_x(m, 3)),
                           (1, 0): lambda: logits(m), (1, 1): lambda: turn_logits(m), (3, 0): lambda: turn_combine(m)}
                for j in range(TT):
                    for half in range(2):
                        output(n, j, look, half)
                        if look and (j, half) in between:
                            between[j, half]()

            if with_o:
                pe.wait_ge(w_lo, KT // 2)
                residual(first)
            pe.wait_ge(ident_ready, 1)
            for k in range(KT):
                turn_x(first, k)
            pe.wait_ge(wr_step, 2)
            logits(first)
            pe.wait_ge(consts_ready, 3)
            turn_logits(first)
            turn_combine(first)
            pe.wait_ge(w_lo, n_pieces)
            each_block(pe, nblocks, body)



HEADS = 16
HD = D // HEADS
HALF = HD // 2
GH = 4
NG = HEADS // GH
SEQ = 1024
QB = 512
ST = SEQ // P
SCALE = HD ** -0.5
GROUP = 128
Q_EPS = 1e-8
STEPS = [(qb, kt) for qb in range(SEQ // QB) for kt in reversed(range((qb + 1) * QB // P))]
NS = len(STEPS)
PIECES = [(i, k, min(k + QB, (i + 1) * P)) for i in range(ST) for k in range(0, (i + 1) * P, QB)]
NP = GH * len(PIECES)
SLOTS = (0, 1, 2, 4, 6)


def first_query(t):
    qb, kt = STEPS[t]
    return max(kt * P - qb * QB, 0)


def slot_pieces(t, slot):
    widths = [QB - first_query(i) if i >= 2 else 0 for i in range(NS)]
    total = sum(widths) * SLOTS[-1]
    lo, hi = ((sum(widths[:t]) * SLOTS[-1] + widths[t] * s) * NP // total for s in SLOTS[slot:slot + 2])
    return range(lo, hi)


def prepare_weights(nc, psum, w_q, w_k, w_v, w_o, wqk_dst, wv_dst, wo_dst):
    with ExitStack() as ctx:
        def sb(name, shape, dt):
            return ctx.enter_context(nc.sbuf_tensor(f"prep_{name}", shape, dt))

        def sem(name):
            return ctx.enter_context(nc.semaphore(f"prep_{name}"))

        NW = 4
        G = D // GROUP
        ident = sb("ident", [P, P], F32)
        w = sb("w", [P, NW, KT * G, GROUP], F32)
        sums = sb("sums", [P, NW, KT * G], F32)
        scale = sb("scale", [P, NW, KT * G], F32)
        half = sb("half", [P, NW, 2, KT * G], F32)
        pos = sb("pos", [P, KT * G, GROUP], F32)
        neg = sb("neg", [P, KT * G, GROUP], F32)
        qk_t = sb("qk_t", [P, KT, 2, NG, 2, 2, GH * HALF], F32R)
        v_t = sb("v_t", [P, 2, KT, D], F32R)
        o_t = sb("o_t", [P, KT, D], F32)

        zeroed = sem("zeroed")
        ident_ready = sem("ident_ready")
        w_loaded = [sem(f"w_loaded{i}") for i in range(NW)]
        step = sem("step")
        w_ready = sem("w_ready")
        turned = sem("turned")
        hi_ready = sem("hi_ready")
        lo_ready = sem("lo_ready")
        stored = sem("stored")

        block = ctx.enter_context(nc.Block())

        @block.sync
        def _(sp):
            for i, src in enumerate((w_q, w_k, w_v, w_o)):
                sp.dma_start(w[:, i].rearrange("p (o g) c -> p o (g c)", g=G),
                             src.rearrange("(o p) c -> p o c", p=P)).then_inc(w_loaded[i], 16)
            sp.wait_ge(lo_ready, 2 * KT)
            for k in range(KT):
                for part in range(2):
                    sp.dma_start(wqk_dst[:, part, k].rearrange("g p c -> p g c"),
                                 qk_t[:, k, part].rearrange("p g f w c -> p g (f w c)").bitcast(F32)).then_inc(stored, 16)
            sp.wait_ge(lo_ready, 3 * KT)
            sp.dma_start(wv_dst.rearrange("a (k p) n -> p (a k) n", p=P), v_t[:].rearrange("p a k n -> p (a k) n").bitcast(F32)).then_inc(stored, 16)
            sp.wait_ge(hi_ready, 4 * KT)
            sp.dma_start(wo_dst.rearrange("(k p) n -> p k n", p=P), o_t[:]).then_inc(stored, 16)
            sp.wait_ge(stored, 16 * (2 * KT + 2))

        @block.gpsimd
        def _(pool):
            nc.gpsimd.memset(ident[:], 0.0).then_inc(zeroed, 1)
            pool.wait_ge(zeroed, 1)
            nc.gpsimd.affine_select(out=ident[:], in_=ident[:], compare_op=ALU.not_equal, fill=1.0, base=0,
                                    pattern=[[-1, P]], channel_multiplier=1).then_inc(ident_ready, 1)

        @block.vector
        def _(dve):
            count = [0]

            def link(ins):
                count[0] += 1
                ins.then_inc(step, 1)
                dve.wait_ge(step, count[0])

            def wide(t):
                return t.unsqueeze(2).to_broadcast([P, KT * G, GROUP])

            def quantise(i):
                dve.wait_ge(w_loaded[i], 16)
                link(nc.vector.tensor_reduce(sums[:, i], w[:, i], AX.X, ALU.add, apply_absolute_value=True))
                link(nc.vector.tensor_scalar(scale[:, i], sums[:, i], 1.0 / GROUP, Q_EPS, ALU.mult, ALU.max))
                nc.vector.tensor_scalar(half[:, i, 0], scale[:, i], 0.5, None, ALU.mult)
                link(nc.vector.tensor_scalar(half[:, i, 1], scale[:, i], -0.5, None, ALU.mult))
                nc.vector.tensor_tensor(pos[:], w[:, i], wide(half[:, i, 0]), ALU.is_gt)
                link(nc.vector.tensor_tensor(neg[:], w[:, i], wide(half[:, i, 1]), ALU.is_lt))
                link(nc.vector.tensor_tensor(pos[:], pos[:], neg[:], ALU.subtract))
                link(nc.vector.tensor_tensor(pos[:], pos[:], wide(scale[:, i]), ALU.mult))
                link(nc.vector.tensor_tensor(pos[:], pos[:], w[:, i], ALU.subtract))
                nc.vector.tensor_tensor(w[:, i], w[:, i], pos[:], ALU.add).then_inc(w_ready, 1)
                dve.wait_ge(w_ready, i + 1)

            def lo(i, k):
                b = i * KT + k
                dve.wait_ge(hi_ready, b + 1)
                if i < 2:
                    src = psum[:, b % 8].rearrange("p (g h f d) -> p f g h d", g=NG, f=2, d=HALF)
                    for f in range(2):
                        ins = nc.vector.tensor_tensor(qk_t[:, k, 1, :, f, i].rearrange("p g (h d) -> p g h d", d=HALF), src[:, f],
                                                      qk_t[:, k, 0, :, f, i].rearrange("p g (h d) -> p g h d", d=HALF).bitcast(F32),
                                                      ALU.subtract)
                    ins.then_inc(lo_ready, 1)
                else:
                    nc.vector.tensor_tensor(v_t[:, 1, k], psum[:, b % 8], v_t[:, 0, k].bitcast(F32),
                                            ALU.subtract).then_inc(lo_ready, 1)

            for i in range(NW):
                quantise(i)
                if 1 <= i < 3:
                    for k in range(KT):
                        lo(i - 1, k)
            for k in range(KT):
                lo(2, k)

        @block.scalar
        def _(act):
            for i in range(NW):
                for k in range(KT):
                    b = i * KT + k
                    act.wait_ge(turned, b + 1)
                    if i < 2:
                        src = psum[:, b % 8].rearrange("p (g h f d) -> p f g h d", g=NG, f=2, d=HALF)
                        for f in range(2):
                            ins = nc.scalar.copy(qk_t[:, k, 0, :, f, i].rearrange("p g (h d) -> p g h d", d=HALF), src[:, f])
                        ins.then_inc(hi_ready, 1)
                    elif i == 2:
                        nc.scalar.copy(v_t[:, 0, k], psum[:, b % 8]).then_inc(hi_ready, 1)
                    else:
                        nc.scalar.copy(o_t[:, k], psum[:, b % 8]).then_inc(hi_ready, 1)

        @block.tensor
        def _(pe):
            pe.wait_ge(ident_ready, 1)
            for i in range(NW):
                pe.wait_ge(w_ready, i + 1)
                for k in range(KT):
                    if i >= 2:
                        pe.wait_ge(lo_ready, (i - 2) * KT + k + 1)
                    for o in range(KT):
                        mm = nc.tensor.transpose(psum[:, (i * KT + k) % 8, o * P:(o + 1) * P], w[:, i, o * G + k], ident[:])
                    mm.then_inc(turned, 1)


class Unit:

    def __init__(self, b, g):
        self.b, self.g = b, g

    def plus(self, n):
        return Unit(self.b + (self.g + n) // NG, (self.g + n) % NG)

    def at(self, k, c):
        return self.b * (NG * k) + (self.g * k + c)


def attention_phase(nc, psum, nbatch, x_src, moments_src, wqk_src, wv_src, cos_src, sin_src, y_dst, rope_tmp, mrow_tmp):
    with ExitStack() as ctx:
        def sb(name, shape, dt):
            return ctx.enter_context(nc.sbuf_tensor(f"att_{name}", shape, dt))

        def sem(name):
            return ctx.enter_context(nc.semaphore(f"att_{name}"))

        ident = sb("ident", [P, P], F32)
        ident_b = sb("ident_b", [P, P], BF16)
        hide_k = sb("hide_k", [P, P], BF16)
        hide_q = sb("hide_q", [P, P], BF16)
        ones = sb("ones", [P, HD], F32)
        cos = sb("cos", [P, SEQ], F32)
        sin = sb("sin", [P, SEQ], F32)
        wqk = sb("wqk", [P, 2, KT, 2, P], F32R)
        wv = sb("wv", [P, 2, KT, D], F32R)
        mv = sb("mv", [P, nbatch * ST, 2], F32)
        root = sb("root", [P, nbatch * ST], F32)
        newton = sb("newton", [P, nbatch * ST], F32)
        rstd = sb("rstd", [P, nbatch * ST], F32)
        eps_col = sb("eps_col", [P, 1], F32)
        xt = sb("xt", [P, ST, D], F32)
        xh = sb("xh", [P, KT, SEQ], F32R)
        xl = sb("xl", [P, KT, SEQ], F32R)
        v = sb("v", [P, ST, D], F32)
        qs = sb("qs", [P, 2, GH, SEQ], F32R)
        ks = sb("ks", [P, 2, GH, SEQ], F32R)
        ra = sb("ra", [P, 2, 2, QB], F32)
        rb = sb("rb", [P, 2, 2, QB], F32)
        roped_hi = sb("roped_hi", [P, 2, QB], F32R)
        mxp = sb("mxp", [P, GH, len(PIECES)], F32)
        mneg = sb("mneg", [P, GH, ST], F32)
        mrow = sb("mrow", [GH * ST, P], F32R)
        probs = sb("probs", [P, 2, GH, QB], F32)
        acc = sb("acc", [P, 2, QB], F32)
        den = sb("den", [P, 2, QB], F32)

        stats = acc[:].rearrange("p j t -> p (j t)")[:, 0:nbatch * ST * 6].rearrange("p (i c) -> p i c", c=6)

        s_bank = [psum[:, 0:2], psum[:, 2:4]]
        w_bank = [psum[:, 4], psum[:, 5]]
        pv_bank, den_bank = psum[:, 6], psum[:, 7]

        def t_bank(i):
            return (psum[:, 2], psum[:, 3], psum[:, 0], psum[:, 1])[i % 4]

        def v_bank(i):
            return psum[:, 2 + i % 2]

        def qk_bank(f):
            return (psum[:, 2], psum[:, 3]) if f == 0 else (w_bank[0], w_bank[1])

        zeroed = sem("zeroed")
        consts_ready = sem("consts_ready")
        ks_ready = sem("ks_ready")
        tables_loaded = sem("tables_loaded")
        wv_loaded = sem("wv_loaded")
        wqk_loaded = sem("wqk_loaded")
        stats_loaded = sem("stats_loaded")
        mv_ready = sem("mv_ready")
        root_ready = sem("root_ready")
        rstd_step = sem("rstd_step")
        xt_loaded = [sem(f"xt_loaded{i}") for i in range(2)]
        xt_ready = sem("xt_ready")
        xt_turned = sem("xt_turned")
        xh_ready = sem("xh_ready")
        xl_ready = sem("xl_ready")
        v_filled = sem("v_filled")
        v_ready = sem("v_ready")
        qk_filled = sem("qk_filled")
        qk_read = sem("qk_read")
        rope_ready = sem("rope_ready")
        rope_hi = sem("rope_hi")
        rope_lo = sem("rope_lo")
        rope_stored = sem("rope_stored")
        placed = sem("placed")
        mx_filled = sem("mx_filled")
        mx_read = sem("mx_read")
        mneg_ready = sem("mneg_ready")
        mrow_turned = sem("mrow_turned")
        mrow_copied = sem("mrow_copied")
        mrow_stored = sem("mrow_stored")
        mrow_placed = sem("mrow_placed")
        s_filled = sem("s_filled")
        exp_done = sem("exp_done")
        pv_done = sem("pv_done")
        acc_copied = sem("acc_copied")
        den_copied = sem("den_copied")
        inv_ready = sem("inv_ready")
        y_ready = sem("y_ready")
        y_stored = [sem("y_stored0"), sem("y_stored1")]

        U0 = Unit(0, 0)

        def exists(u):
            return not (isinstance(u.b, int) and u.b >= nbatch)

        def each_batch(engine, body):
            with engine.Fori(0, nbatch - 1) as b:
                for g in range(NG):
                    body(Unit(b, g))
            for g in range(NG):
                body(Unit(nbatch - 1, g))

        x_in = x_src.rearrange("(b t p) d -> b p t d", p=P, t=ST)
        y_out = y_dst.rearrange("(g p) (b j t) -> g b j p t", p=P, j=2, t=QB)

        block = ctx.enter_context(nc.Block())

        @block.sync
        def _(sp):
            def wqk_load(u):
                if u.g or not isinstance(u.b, int):
                    sp.wait_ge(qk_filled, u.at(4, 0))
                sp.dma_start(wqk[:].rearrange("p a k f c -> p (a k) (f c)").bitcast(F32),
                             wqk_src[u.g].rearrange("a k p c -> p (a k) c")).then_inc(wqk_loaded, 16)

            def load_batch(b):
                if not isinstance(b, int):
                    sp.wait_ge(xt_turned, b * ST)
                for half in range(2):
                    t = slice(half * ST // 2, (half + 1) * ST // 2)
                    sp.dma_start(xt[:, t], x_in[b, :, t]).then_inc(xt_loaded[half], 16)

            def store_rope(u):
                for f in range(2):
                    for part, made in enumerate((rope_hi, rope_lo)):
                        sp.wait_ge(made, u.at(4, 2 * f + 2))
                        sp.dma_start(rope_tmp[u.g % 2, part].rearrange("(p r) t -> p r t", r=2)[:, :, f * QB:(f + 1) * QB],
                                     ra[:, f] if part else roped_hi[:].bitcast(F32)).then_inc(rope_stored, 16)

            def place(u, free):
                if free is not None:
                    sp.wait_ge(s_filled, free)
                src = rope_tmp[u.g % 2].rearrange("a (w h r) t -> a w r h t", w=2, h=GH)
                for slot, (which, parts) in enumerate(((0, (0, 0, 1)), (1, (0, 1, 0)))):
                    dst = (qs, ks)[slot]
                    for row, part in enumerate(parts):
                        sp.dma_start(dst[row * HD:(row + 1) * HD, u.g % 2].bitcast(F32), src[part, which]).then_inc(placed, 16)

            def place_mrow(u):
                sp.wait_ge(mrow_copied, u.at(1, 1))
                sp.dma_start(mrow_tmp[:], mrow[:].bitcast(F32)).then_inc(mrow_stored, 16)
                sp.wait_ge(mrow_stored, u.at(16, 16))
                sp.dma_start(qs[3 * HD:3 * HD + 1, u.g % 2].rearrange("o h t -> o (h t)").bitcast(F32),
                             mrow_tmp.rearrange("(o r) t -> o (r t)", o=1)).then_inc(mrow_placed, 16)

            def store_y(u, j):
                sp.wait_ge(y_ready, u.at(2, j + 1))
                sp.dma_start(y_out[u.g, u.b, j], acc[:, j]).then_inc(y_stored[j], 16)

            def body(u):
                if exists(u.plus(3)):
                    wqk_load(u.plus(3))
                if u.g == 0 and exists(u.plus(NG)):
                    load_batch(u.b + 1)
                if exists(u.plus(2)):
                    store_rope(u.plus(2))
                store_y(u, 0)
                if exists(u.plus(1)):
                    place_mrow(u.plus(1))
                if exists(u.plus(2)):
                    place(u.plus(2), u.at(2 * NS, 2 * NS))
                store_y(u, 1)

            sp.dma_start(stats[:], moments_src).then_inc(stats_loaded, 16)
            load_batch(0)
            wqk_load(U0)
            sp.dma_start(cos[:], cos_src).then_inc(tables_loaded, 16)
            sp.dma_start(sin[:], sin_src).then_inc(tables_loaded, 16)
            sp.dma_start(wv[:].rearrange("p a k n -> p (a k) n").bitcast(F32), wv_src.rearrange("a (k p) n -> p (a k) n", p=P)).then_inc(wv_loaded, 16)
            wqk_load(U0.plus(1))
            store_rope(U0)
            sp.wait_ge(rope_stored, 64)
            place(U0, None)
            wqk_load(U0.plus(2))
            store_rope(U0.plus(1))
            sp.wait_ge(rope_stored, 128)
            place(U0.plus(1), None)
            place_mrow(U0)
            each_batch(sp, body)
            sp.wait_ge(y_stored[0], 16 * NG * nbatch + 1)
            sp.wait_ge(y_stored[1], 16 * NG * nbatch + 1)

        @block.gpsimd
        def _(pool):
            nc.gpsimd.memset(ident[:], 0.0).then_inc(zeroed, 1)
            nc.gpsimd.memset(ident_b[:], 0.0).then_inc(zeroed, 1)
            nc.gpsimd.memset(hide_k[:], 0.0).then_inc(zeroed, 1)
            nc.gpsimd.memset(hide_q[:], 0.0).then_inc(zeroed, 1)
            nc.gpsimd.memset(ones[:], 1.0).then_inc(y_stored[0], 1)
            nc.gpsimd.memset(eps_col[:], LN_EPS).then_inc(y_stored[1], 1)
            pool.wait_ge(zeroed, 4)
            for tile in (ident, ident_b):
                nc.gpsimd.affine_select(out=tile[:], in_=tile[:], compare_op=ALU.not_equal, fill=1.0, base=0,
                                        pattern=[[-1, P]], channel_multiplier=1).then_inc(consts_ready, 1)
            nc.gpsimd.affine_select(out=hide_k[:], in_=hide_k[:], compare_op=ALU.is_ge, fill=-BIG, base=0,
                                    pattern=[[-1, P]], channel_multiplier=1).then_inc(consts_ready, 1)
            nc.gpsimd.affine_select(out=hide_q[:], in_=hide_q[:], compare_op=ALU.is_ge, fill=-BIG, base=0,
                                    pattern=[[1, P]], channel_multiplier=-1).then_inc(consts_ready, 1)

            def mix(u):
                for f in range(2):
                    pool.wait_ge(qk_read, u.at(2, f + 1))
                    nc.gpsimd.tensor_tensor(ra[:, f, 0], ra[:, f, 0], rb[:, f, 0], ALU.subtract).then_inc(rope_ready, 1)
                    nc.gpsimd.tensor_tensor(ra[:, f, 1], ra[:, f, 1], rb[:, f, 1], ALU.add).then_inc(rope_ready, 1)

            def rope_los(u):
                for f in range(2):
                    for r in range(2):
                        pool.wait_ge(rope_hi, u.at(4, 2 * f + r + 1))
                        nc.gpsimd.tensor_tensor(ra[:, f, r].bitcast(F32R), ra[:, f, r], roped_hi[:, r].bitcast(F32),
                                                ALU.subtract).then_inc(rope_lo, 1)

            def normalise_y(u, j):
                pool.wait_ge(inv_ready, u.at(2, j + 1))
                pool.wait_ge(acc_copied, u.at(2, j + 1))
                nc.gpsimd.tensor_tensor(acc[:, j], acc[:, j], den[:, j], ALU.mult).then_inc(y_ready, 1)

            def body(u):
                if exists(u.plus(2)):
                    rope_los(u.plus(2))
                normalise_y(u, 0)
                normalise_y(u, 1)
                if exists(u.plus(3)):
                    mix(u.plus(3))

            mix(U0)
            rope_los(U0)
            mix(U0.plus(1))
            rope_los(U0.plus(1))
            mix(U0.plus(2))
            each_batch(pool, body)

        @block.scalar
        def _(act):
            def x_hi(b, i):
                bank = t_bank(i)
                act.wait_ge(xt_turned, b * ST + (i + 1))
                nc.scalar.copy(xh[:, :, i * P:(i + 1) * P], bank.rearrange("p (k t) -> p k t", k=KT)).then_inc(xh_ready, 1)

            def v_copy(b, i):
                act.wait_ge(v_filled, b * ST + (i + 1))
                nc.scalar.copy(v[:, i], v_bank(i)).then_inc(v_ready, 1)

            def rope_his(u, f, before=None):
                if before is not None:
                    act.wait_ge(placed, before)
                act.wait_ge(rope_stored, u.at(64, 32 * f))
                for r in range(2):
                    act.wait_ge(rope_ready, u.at(4, 2 * f + r + 1))
                    nc.scalar.copy(roped_hi[:, r], ra[:, f, r]).then_inc(rope_hi, 1)

            def mrow_copy(u):
                act.wait_ge(mrow_turned, u.at(1, 1))
                act.wait_ge(mrow_stored, u.at(16, 0))
                nc.scalar.copy(mrow[:], s_bank[0][0:GH * ST, 0, 0:P]).then_inc(mrow_copied, 1)

            def exps(u, t):
                first = first_query(t)
                for hp in range(2):
                    act.wait_ge(s_filled, u.at(2 * NS, 2 * t + hp + 1))
                    if hp == 0 and t >= 2:
                        act.wait_ge(pv_done, u.at(NS, t - 1))
                    nc.scalar.activation(probs[:, t % 2, 2 * hp:2 * hp + 2, first:QB], s_bank[hp][:, :, first:QB],
                                         ACT.Exp, scale=SCALE).then_inc(exp_done, 1)

            def sums_copy(u, j):
                act.wait_ge(pv_done, u.at(NS, 4 if j == 0 else NS))
                act.wait_ge(y_stored[j], u.at(16, 1))
                nc.scalar.copy(den[:, j], den_bank).then_inc(den_copied, 1)
                nc.scalar.copy(acc[:, j], pv_bank).then_inc(acc_copied, 1)

            def body(u):
                for t in range(NS):
                    exps(u, t)
                    if t == 1 and exists(u.plus(2)):
                        rope_his(u.plus(2), 0, u.plus(1).at(96, 0))
                    if t == 7 and exists(u.plus(2)):
                        rope_his(u.plus(2), 1)
                    if t == 4:
                        sums_copy(u, 0)
                sums_copy(u, 1)
                if exists(u.plus(2)):
                    act.wait_ge(rope_stored, u.plus(2).at(64, 64))
                if exists(u.plus(1)):
                    mrow_copy(u.plus(1))
                if u.g == 0 and exists(u.plus(NG)):
                    for i in range(ST):
                        x_hi(u.b + 1, i)
                if u.g == NG - 1 and exists(u.plus(NG)):
                    for i in range(ST):
                        v_copy(u.b + 1, i)

            act.wait_ge(consts_ready, 4)
            act.wait_ge(mv_ready, 1)
            nc.scalar.activation(root[:], mv[:, :, 1], ACT.Sqrt, bias=eps_col[:]).then_inc(root_ready, 1)
            for i in range(ST):
                x_hi(0, i)
            for i in range(ST):
                v_copy(0, i)
                if i in (1, 3):
                    rope_his(U0, i // 2)
            rope_his(U0.plus(1), 0)
            rope_his(U0.plus(1), 1)
            mrow_copy(U0)
            each_batch(act, body)

        @block.vector
        def _(dve):
            def normalise(b, i):
                dve.wait_ge(xt_loaded[i // (ST // 2)], b * 16 + 16)
                nc.vector.tensor_scalar(xt[:, i], xt[:, i], mv[:, bass.ds(b * ST + i, 1), 0], rstd[:, bass.ds(b * ST + i, 1)],
                                        ALU.subtract, ALU.mult).then_inc(xt_ready, 1)

            def x_lo(b, i):
                dve.wait_ge(xh_ready, b * ST + (i + 1))
                t = slice(i * P, (i + 1) * P)
                nc.vector.tensor_tensor(xl[:, :, t], t_bank(i).rearrange("p (k t) -> p k t", k=KT),
                                        xh[:, :, t].bitcast(F32), ALU.subtract).then_inc(xl_ready, 1)

            def rope(u, reused):
                for f in range(2):
                    a, c = qk_bank(f)
                    p = slice(f * QB, (f + 1) * QB)
                    dve.wait_ge(qk_filled, u.at(4, 2 * f + 2))
                    if reused:
                        dve.wait_ge(rope_stored, u.at(64, 32 * f - 32))
                    nc.vector.tensor_tensor(ra[:, f, 0], a, cos[:, p], ALU.mult)
                    nc.vector.tensor_tensor(ra[:, f, 1], a, sin[:, p], ALU.mult)
                    nc.vector.tensor_tensor(rb[:, f, 0], c, sin[:, p], ALU.mult)
                    nc.vector.tensor_tensor(rb[:, f, 1], c, cos[:, p], ALU.mult).then_inc(qk_read, 1)

            def piece_max(u, c):
                h, (i, k0, k1) = c // len(PIECES), PIECES[c % len(PIECES)]
                dve.wait_ge(mx_filled, u.at(NP, c + 1))
                nc.vector.tensor_reduce(mxp[:, h, c % len(PIECES):c % len(PIECES) + 1], w_bank[c % 2][:, 0:k1 - k0], AX.X,
                                        ALU.max).then_inc(mx_read, 1)

            def row_max(u):
                dve.wait_ge(mx_read, u.at(NP, NP))
                dve.wait_ge(mrow_turned, u.at(1, 0))
                n1 = QB // P
                nc.vector.tensor_scalar(mneg[:, :, 0:n1], mxp[:, :, 0:n1], -1.0, None, ALU.mult)
                nc.vector.tensor_reduce(mneg[:, :, n1:ST], mxp[:, :, n1:].rearrange("p h (i c) -> p h i c", c=2), AX.X,
                                        ALU.max, negate=True).then_inc(mneg_ready, 1)

            def invert(u, j, quarter):
                if quarter == 0:
                    dve.wait_ge(den_copied, u.at(2, j + 1))
                q = slice(quarter * P, (quarter + 1) * P)
                ins = nc.vector.reciprocal(den[:, j, q], den[:, j, q])
                if quarter == 3:
                    ins.then_inc(inv_ready, 1)

            def body(u):
                for t in range(NS):
                    if not exists(u.plus(1)):
                        if t == 5:
                            for quarter in range(4):
                                invert(u, 0, quarter)
                    else:
                        for slot in range(len(SLOTS) - 1):
                            for c in slot_pieces(t, slot):
                                piece_max(u.plus(1), c)
                            if t == 5:
                                invert(u, 0, slot)
                    if u.g == 0 and t < ST and exists(u.plus(NG)):
                        normalise(u.b + 1, t)
                if exists(u.plus(1)):
                    row_max(u.plus(1))
                for quarter in range(4):
                    invert(u, 1, quarter)
                if exists(u.plus(3)):
                    rope(u.plus(3), True)
                if u.g == 0 and exists(u.plus(NG)):
                    for i in range(ST):
                        x_lo(u.b + 1, i)

            dve.wait_ge(stats_loaded, 16)
            for i in range(nbatch * ST):
                ins = nc.vector.bn_aggr(mv[:, i], stats[:, i])
            ins.then_inc(mv_ready, 1)
            dve.wait_ge(root_ready, 1)
            nc.vector.reciprocal(rstd[:], root[:]).then_inc(rstd_step, 1)
            dve.wait_ge(rstd_step, 1)
            nc.vector.tensor_tensor(newton[:], rstd[:], rstd[:], ALU.mult).then_inc(rstd_step, 1)
            dve.wait_ge(rstd_step, 2)
            nc.vector.scalar_tensor_tensor(newton[:], mv[:, :, 1], LN_EPS, newton[:], ALU.add, ALU.mult).then_inc(rstd_step, 1)
            dve.wait_ge(rstd_step, 3)
            nc.vector.tensor_scalar(newton[:], newton[:], -0.5, 1.5, ALU.mult, ALU.add).then_inc(rstd_step, 1)
            dve.wait_ge(rstd_step, 4)
            nc.vector.tensor_tensor(rstd[:], rstd[:], newton[:], ALU.mult).then_inc(rstd_step, 1)
            dve.wait_ge(rstd_step, 5)
            for i in range(ST):
                normalise(0, i)
            for i in range(ST):
                x_lo(0, i)
            nc.vector.memset(ks[3 * HD:3 * HD + 1].bitcast(F32), 1.0).then_inc(ks_ready, 1)
            dve.wait_ge(tables_loaded, 32)
            rope(U0, False)
            rope(U0.plus(1), True)
            for c in range(NP):
                piece_max(U0, c)
            row_max(U0)
            rope(U0.plus(2), True)
            each_batch(dve, body)

        @block.tensor
        def _(pe):
            def turn(b, i):
                pe.wait_ge(xt_ready, b * ST + (i + 1))
                if i >= 4:
                    pe.wait_ge(xl_ready, b * ST + (i - 3))
                for k in range(KT):
                    mm = nc.tensor.transpose(t_bank(i)[:, k * P:(k + 1) * P], xt[:, i, k * P:(k + 1) * P], ident[:])
                mm.then_inc(xt_turned, 1)

            def project_v(b, i):
                if i >= 2:
                    pe.wait_ge(v_ready, b * ST + (i - 1))
                elif i == 0 and isinstance(b, int):
                    pe.wait_ge(wv_loaded, 16)
                t = slice(i * P, (i + 1) * P)
                for k in range(KT):
                    nc.tensor.matmul(v_bank(i), xh[:, k, t], wv[:, 0, k], start=k == 0, stop=False)
                    nc.tensor.matmul(v_bank(i), xh[:, k, t], wv[:, 1, k], start=False, stop=False)
                    mm = nc.tensor.matmul(v_bank(i), xl[:, k, t], wv[:, 0, k], start=False, stop=k == KT - 1)
                mm.then_inc(v_filled, 1)

            def project_qk(u, f, r):
                pe.wait_ge(wqk_loaded, u.at(16, 16))
                pe.wait_ge(xl_ready, u.b * ST + ST)
                t = slice(f * QB, (f + 1) * QB)
                bank = qk_bank(f)[r]
                w = wqk
                for k in range(KT):
                    nc.tensor.matmul(bank, w[:, 0, k, r], xh[:, k, t], start=k == 0, stop=False)
                    nc.tensor.matmul(bank, w[:, 0, k, r], xl[:, k, t], start=False, stop=False)
                    mm = nc.tensor.matmul(bank, w[:, 1, k, r], xh[:, k, t], start=False, stop=k == KT - 1)
                mm.then_inc(qk_filled, 1)

            def piece(u, c):
                h, (i, k0, k1) = c // len(PIECES), PIECES[c % len(PIECES)]
                if c == 0:
                    pe.wait_ge(placed, u.at(96, 96))
                if c >= 2:
                    pe.wait_ge(mx_read, u.at(NP, c - 1))
                diag = k1 == (i + 1) * P
                bank = w_bank[c % 2]
                if diag:
                    nc.tensor.matmul(bank[:, k1 - k0 - P:k1 - k0], ident_b[:], hide_k[:], start=True, stop=False,
                                     skip_group_check=True)
                nc.tensor.matmul(bank[:, 0:k1 - k0], qs[0:3 * HD, u.g % 2, h, i * P:(i + 1) * P],
                                 ks[0:3 * HD, u.g % 2, h, k0:k1], start=not diag, stop=True,
                                 skip_group_check=True).then_inc(mx_filled, 1)

            def turn_mrow(u):
                pe.wait_ge(mneg_ready, u.at(1, 1))
                nc.tensor.transpose(s_bank[0][0:GH * ST, 0, 0:P], mneg[:].rearrange("p h i -> p (h i)"),
                                    ident[:]).then_inc(mrow_turned, 1)

            def pieces(u, t, slot):
                if not exists(u.plus(1)):
                    return
                for c in slot_pieces(t, slot):
                    if c == 0 and exists(u.plus(2)):
                        pe.wait_ge(qk_read, u.plus(2).at(2, 2))
                    piece(u.plus(1), c)

            def scores(u, t, hp):
                qb, kt = STEPS[t]
                first = first_query(t)
                if t == 0 and hp == 0:
                    pe.wait_ge(mrow_placed, u.at(16, 16))
                if t == 0 and hp == 1 and exists(u.plus(2)):
                    pe.wait_ge(qk_read, u.plus(2).at(2, 1))
                if t > 0:
                    pe.wait_ge(exp_done, u.at(2 * NS, 2 * t + hp - 1))
                diag = kt * P >= qb * QB
                if diag:
                    for i in range(2):
                        nc.tensor.matmul(s_bank[hp][:, i, first:first + P], ident_b[:], hide_q[:], start=True, stop=False,
                                         skip_group_check=True)
                for h in (2 * hp, 2 * hp + 1):
                    mm = nc.tensor.matmul(s_bank[hp][:, h % 2, first:QB], ks[0:3 * HD + 1, u.g % 2, h, kt * P:(kt + 1) * P],
                                          qs[0:3 * HD + 1, u.g % 2, h, qb * QB + first:(qb + 1) * QB],
                                          start=not diag, stop=True, skip_group_check=True)
                mm.then_inc(s_filled, 1)

            def weigh(u, t, bank):
                qb, kt = STEPS[t]
                first = first_query(t)
                opening = kt == (qb + 1) * QB // P - 1
                if bank is pv_bank:
                    pe.wait_ge(exp_done, u.at(2 * NS, 2 * t + 2))
                    if opening and qb > 0:
                        pe.wait_ge(acc_copied, u.at(2, qb))
                        pe.wait_ge(den_copied, u.at(2, qb))
                for h in range(GH):
                    rows = slice(h * HD, (h + 1) * HD)
                    w = v[:, kt, u.g * P + h * HD:u.g * P + (h + 1) * HD] if bank is pv_bank else ones[:]
                    mm = nc.tensor.matmul(bank[rows, first:QB], w, probs[:, t % 2, h, first:QB], start=opening,
                                          stop=kt == 0, skip_group_check=True)
                if bank is den_bank:
                    mm.then_inc(pv_done, 1)

            def body(u):
                if u.g == 0:
                    pe.wait_ge(v_ready, u.b * ST + ST)
                if u.g == 1 and exists(u.plus(NG)):
                    pe.wait_ge(xl_ready, u.b * ST + 2 * ST)
                scores(u, 0, 0)
                scores(u, 0, 1)
                for t in range(NS):
                    if t + 1 < NS:
                        scores(u, t + 1, 0)
                    pieces(u, t, 0)
                    if t + 1 < NS:
                        scores(u, t + 1, 1)
                    pieces(u, t, 1)
                    weigh(u, t, pv_bank)
                    pieces(u, t, 2)
                    weigh(u, t, den_bank)
                    pieces(u, t, 3)
                if exists(u.plus(3)):
                    project_qk(u.plus(3), 0, 0)
                if exists(u.plus(1)):
                    turn_mrow(u.plus(1))
                if exists(u.plus(3)):
                    project_qk(u.plus(3), 0, 1)
                    pe.wait_ge(mx_read, u.plus(1).at(NP, NP))
                    project_qk(u.plus(3), 1, 0)
                    project_qk(u.plus(3), 1, 1)
                if u.g == 0 and exists(u.plus(NG)):
                    pe.wait_ge(qk_read, u.plus(3).at(2, 1))
                    pe.wait_ge(mrow_copied, u.plus(1).at(1, 1))
                    for i in range(ST):
                        turn(u.b + 1, i)
                if u.g == NG - 1 and exists(u.plus(NG)):
                    pe.wait_ge(qk_read, u.plus(3).at(2, 1))
                    for i in range(ST):
                        project_v(u.b + 1, i)

            pe.wait_ge(consts_ready, 4)
            for i in range(ST):
                turn(0, i)
            for f in range(2):
                project_qk(U0, f, 0)
                project_qk(U0, f, 1)
            pe.wait_ge(qk_read, 1)
            for i in range(ST):
                project_v(0, i)
            pe.wait_ge(v_ready, ST)
            pe.wait_ge(qk_read, 2)
            for f in range(2):
                project_qk(U0.plus(1), f, 0)
                project_qk(U0.plus(1), f, 1)
            pe.wait_ge(qk_read, 4)
            for c in range(NP):
                piece(U0, c)
            turn_mrow(U0)
            pe.wait_ge(mx_read, NP)
            for f in range(2):
                project_qk(U0.plus(2), f, 0)
                project_qk(U0.plus(2), f, 1)
            pe.wait_ge(ks_ready, 1)
            each_batch(pe, body)


def rope_tables():
    inv = 1.0 / np.power(np.float32(10000.0), np.arange(HALF, dtype=np.float32) / np.float32(HALF), dtype=np.float32)
    angle = np.outer(np.arange(SEQ, dtype=np.float32), inv.astype(np.float32)).astype(np.float32)
    return [np.ascontiguousarray(np.tile(f(angle).astype(np.float32).T, (P // HALF, 1))) for f in (np.cos, np.sin)]


def build(nc, a, out):
    x = a["x"].rearrange("b t d -> (b t) d")
    y = out.rearrange("b t d -> (b t) d")
    tokens = x.shape[0]
    nblocks, nbatch = tokens // TB, tokens // SEQ

    def scratch(name, shape, dt):
        return nc.dram_tensor(name, shape, dt, kind="Internal").ap()

    x1 = scratch("x1", [tokens, D], F32)
    moments = scratch("moments", [nblocks, P, TT, 6], F32)
    att = scratch("att", [D, tokens], F32)
    wqk = scratch("wqk_parts", [NG, 2, KT, P, 2 * P], F32)
    wv = scratch("wv_parts", [2, D, D], F32)
    wo = scratch("wo_turned", [D, D], F32)
    rope_tmp = scratch("rope_tmp", [2, 2, 2 * P, SEQ], F32)
    mrow_tmp = scratch("mrow_tmp", [GH * ST, P], F32)
    with nc.psum_tensor("banks", [P, 8, D], F32) as psum:
        prepare_weights(nc, psum, a["w_q"], a["w_k"], a["w_v"], a["w_o"], wqk, wv, wo)
        ffn_phase(nc, psum, "ffn1", nblocks, x, x1, a["router_w"], a["w_a"], a["w_b"], moments_dst=moments)
        attention_phase(nc, psum, nbatch, x1, moments.rearrange("n p j c -> p n (j c)"), wqk, wv, a["cos"], a["sin"],
                        att, rope_tmp, mrow_tmp)
        ffn_phase(nc, psum, "ffn2", nblocks, x1, y, a["router_w"], a["w_a"], a["w_b"], y_src=att, w_o=wo)


def kernel(L0_attn_x, L0_attn_w_q, L0_attn_w_k, L0_attn_w_v, L0_attn_w_o, L0_ffn_router_w, L0_ffn_Wa, L0_ffn_Wb):
    import concourse.bacc as bacc
    from concourse.bass_utils import run_bass_kernel_spmd

    cos, sin = rope_tables()
    arrays = {"x": L0_attn_x, "w_q": L0_attn_w_q, "w_k": L0_attn_w_k, "w_v": L0_attn_w_v, "w_o": L0_attn_w_o,
              "router_w": L0_ffn_router_w, "w_a": L0_ffn_Wa, "w_b": L0_ffn_Wb, "cos": cos, "sin": sin}
    arrays = {k: np.ascontiguousarray(v) for k, v in arrays.items()}
    nc = bacc.Bacc("TRN2", target_bir_lowering=False, num_devices=1)
    a = {k: nc.dram_tensor(k, v.shape, mybir.dt.from_np(v.dtype), kind="ExternalInput").ap() for k, v in arrays.items()}
    out = nc.dram_tensor("out", arrays["x"].shape, F32, kind="ExternalOutput").ap()
    build(nc, a, out)
    result = run_bass_kernel_spmd(nc, [arrays], core_ids=[0])
    return result.results[0]["out"]
```

```python
from contextlib import ExitStack

import numpy as np
import concourse.bass as bass
from concourse import mybir

ALU = mybir.AluOpType
ACT = mybir.ActivationFunctionType
AX = mybir.AxisListType
F32 = mybir.dt.float32
F32R = mybir.dt.float32r
BF16 = mybir.dt.bfloat16

P = 128
D = 512
KT = D // P
NE = 8
RANK = 128
TB = 512
TT = TB // P
GROUP = P
Q_EPS = 1e-8
LN_EPS = 1e-5
NORM_MIN = 1e-12
BIG = 1e30


class Block2:

    def __init__(self, pair, parity):
        self.pair, self.parity = pair, parity

    def at(self, k, c):
        return self.pair * (2 * k) + (self.parity * k + c)

    def next(self):
        return Block2(self.pair, 1) if self.parity == 0 else Block2(self.pair + 1, 0)

    def index(self):
        return self.pair * 2 + self.parity


def each_block(engine, nblocks, body):
    last = nblocks // 2 - 1
    with engine.Fori(0, last) as pair:
        body(Block2(pair, 0), True, True)
        body(Block2(pair, 1), True, True)
    body(Block2(last, 0), True, False)
    body(Block2(last, 1), False, False)


def ffn_phase(nc, psum, tag, nblocks, x_src, x_dst, w_router, w_a, w_b, moments_dst=None, raw_src=None,
              parts_dst=None, y_src=None, wo_src=None):
    with_o = y_src is not None
    HS = 2
    STAGES = 4
    ternary = raw_src is not None
    assert not ternary or raw_src.shape[0] == nblocks
    STORES = 16 * (1 + (moments_dst is not None) + ternary)
    LAG = 1
    with ExitStack() as ctx:
        def sb(name, shape, dt):
            return ctx.enter_context(nc.sbuf_tensor(f"{tag}_{name}", shape, dt))

        def sem(name):
            return ctx.enter_context(nc.semaphore(f"{tag}_{name}"))

        ident = sb("ident", [P, P], F32)
        eps_col = sb("eps_col", [P, 1], F32)
        zero_col = sb("zero_col", [P, 1], F32)
        wa = sb("wa", [P, KT, 2, NE * RANK], F32R)
        wb = sb("wb", [P, NE, 2, D], F32R)
        wr = sb("wr", [P, KT, 4, NE], F32R)
        wr_raw = sb("wr_raw", [P, KT, NE], F32)
        fold = sb("fold", [2 * NE, NE], F32)
        first_w = sb("first_w", [P, TT, NE], F32)
        x = sb("x", [P, 2, TT, D], F32)
        xn = sb("xn", [P, TT, D], F32)
        xh = sb("xh", [P, KT, TB], F32R)
        xl = sb("xl", [P, KT, TB], F32R)
        hs = sb("hs", [P, HS, TB], F32)
        hh = sb("hh", [P, NE, TB], F32R)
        hl = sb("hl", [P, NE, TB], F32R)
        cb = sb("cb", [P, 2, TB], F32)
        stages = [x[:, 1, 0:2], x[:, 1, 2:4], hs[:], cb[:]]
        lg = sb("lg", [2 * NE, TB], F32)
        cm = sb("cm", [P, TT, P], F32R)
        own_tile = sb("own_tile", [P, TT], F32)
        rows_of = sb("rows_of", [P, 2 * NE], F32)
        spread = sb("spread", [P, NE, P], F32R)
        stats = sb("stats", [P, TT, 6], F32)
        mv = sb("mv", [P, TT, 2], F32)
        root = sb("root", [P, 2, TT], F32)
        inv0 = sb("inv0", [P, TT], F32)
        newton = sb("newton", [P, TT], F32)
        rstd = sb("rstd", [P, TT], F32)
        norm = sb("norm", [P, TT], F32)
        inv_norm = sb("inv_norm", [P, TT], F32)
        logit = sb("logit", [P, TT, NE], F32)
        hit = sb("hit", [P, TT, NE], F32)
        score = sb("score", [P, TT, NE], F32)
        top = [sb(f"top{i}", [P, TT, NE], F32) for i in range(2)]
        peak = sb("peak", [P, 2, TT], F32)
        who = sb("who", [P, TT], F32)
        gap = sb("gap", [P, TT], F32)
        ratio = sb("ratio", [P, TT], F32)
        gate = sb("gate", [P, 2, TT], F32)
        total = sb("total", [P, TT], F32)
        comb = sb("comb", [P, NE, TT], F32)
        comb_parts = sb("comb_parts", [P, 4, NE, TT], F32R)
        if moments_dst is not None:
            out_stats = sb("out_stats", [P, 2, TT, 6], F32)
        if ternary:
            raw = sb("raw", [P, 2, KT, P], F32)
            sums = sb("sums", [P, KT], F32)
            scale = sb("scale", [P, KT], F32)
            half = sb("half", [P, 2, KT], F32)
            pos = sb("pos", [P, KT, P], F32)
            neg = sb("neg", [P, KT, P], F32)
            parts = sb("parts", [P, 2, 2, KT, P], F32R)
        if with_o:
            wo = sb("wo", [P, KT, 2, KT, P], F32R)
            yt = sb("yt", [P, KT, TB], F32)
            yh = sb("yh", [P, KT, TB], F32R)
            yl = sb("yl", [P, KT, TB], F32R)

        banks = [psum[:, i] for i in range(8)]
        t_bank, h_bank, o_bank, m_bank = banks[0:2], banks[2:5], banks[5:7], banks[7]

        zeroed = sem("zeroed")
        cols_ready = sem("cols_ready")
        ident_ready = sem("ident_ready")
        consts_ready = sem("consts_ready")
        w_loaded = [sem(f"w_loaded{s}") for s in range(STAGES)]
        w_hi = sem("w_hi")
        w_lo = sem("w_lo")
        wr_loaded = sem("wr_loaded")
        wr_step = sem("wr_step")
        x_loaded = [sem("x_loaded0"), sem("x_loaded1")]
        x_stored = [sem("x_stored0"), sem("x_stored1")]
        dve_step = sem("dve_step")
        stats_ready = sem("stats_ready")
        var_ready = sem("var_ready")
        root_ready = sem("root_ready")
        xn_ready = sem("xn_ready")
        t_filled = sem("t_filled")
        xh_ready = sem("xh_ready")
        xl_ready = sem("xl_ready")
        lg_filled = sem("lg_filled")
        lg_copied = sem("lg_copied")
        lt_filled = sem("lt_filled")
        gap_ready = sem("gap_ready")
        ratio_ready = sem("ratio_ready")
        comb_ready = sem("comb_ready")
        ct_filled = sem("ct_filled")
        cm_ready = sem("cm_ready")
        cb_filled = sem("cb_filled")
        cb_ready = sem("cb_ready")
        h_filled = sem("h_filled")
        h_scaled = sem("h_scaled")
        hh_ready = sem("hh_ready")
        hl_ready = sem("hl_ready")
        o_filled = sem("o_filled")
        o_added = sem("o_added")
        y_loaded = sem("y_loaded")
        yh_ready = sem("yh_ready")
        yl_ready = sem("yl_ready")
        res_filled = sem("res_filled")
        res_added = sem("res_added")
        out_stats_ready = sem("out_stats_ready")
        raw_loaded = [sem("raw_loaded0"), sem("raw_loaded1")]
        raw_step = sem("raw_step")
        raw_ready = sem("raw_ready")
        raw_turned = sem("raw_turned")
        part_hi = sem("part_hi")
        part_lo = sem("part_lo")
        wo_loaded = sem("wo_loaded")

        pieces = []
        for k in range(KT):
            pieces.append((w_a[:, k * P:(k + 1) * P, :].rearrange("e p r -> p e r"),
                           wa[:, k, 0].rearrange("p (e r) -> p e r", e=NE),
                           wa[:, k, 1].rearrange("p (e r) -> p e r", e=NE), NE))
        for e in range(0, NE, 2):
            pieces.append((w_b[e:e + 2].rearrange("e p n -> p e n"), wb[:, e:e + 2, 0], wb[:, e:e + 2, 1], 2))
        n_pieces = len(pieces)
        n_before, n_between = (n_pieces, n_pieces) if with_o else (0, STAGES)

        def staged(c, rows):
            flat = stages[c % STAGES].rearrange("p j d -> p (j d)")
            return flat.rearrange("p (a n) -> p a n", a=rows)

        x_in = x_src.rearrange("(n j p) d -> n p j d", p=P, j=TT)
        x_out = x_dst.rearrange("(n j p) d -> n p j d", p=P, j=TT)
        y_in = y_src.rearrange("(c p) (n t) -> n p c t", p=P, t=TB) if with_o else None
        first, second = Block2(0, 0), Block2(0, 1)

        block = ctx.enter_context(nc.Block())

        @block.sync
        def _(sp):
            def load_x(m):
                sp.dma_start(x[:, m.parity], x_in[m.index()]).then_inc(x_loaded[m.parity], 16)

            def load_y(m):
                sp.wait_ge(yl_ready, m.at(KT, 0))
                sp.dma_start(yt[:], y_in[m.index()]).then_inc(y_loaded, 16)

            def load_raw(m):
                sp.dma_start(raw[:, m.parity], raw_src[m.index()].rearrange("p (k c) -> p k c", k=KT)
                             ).then_inc(raw_loaded[m.parity], 16)

            def body(n, look, look2):
                if look2 and with_o:
                    load_y(n.next().next())
                sp.wait_ge(o_added, n.at(TT, TT))
                sp.dma_start(x_out[n.index()], x[:, n.parity]).then_inc(x_stored[n.parity], 16)
                if moments_dst is not None:
                    sp.wait_ge(out_stats_ready, n.at(TT, TT))
                    sp.dma_start(moments_dst[n.index()], out_stats[:, n.parity]).then_inc(x_stored[n.parity], 16)
                if ternary:
                    sp.wait_ge(part_lo, n.at(1, 1))
                    sp.dma_start(parts_dst[n.index()], parts[:, n.parity].rearrange("p a k o -> p (a k o)").bitcast(F32)
                                 ).then_inc(x_stored[n.parity], 16)
                    if look2:
                        load_raw(n.next().next())
                if look2:
                    sp.wait_ge(x_stored[n.parity], (n.pair + 1) * STORES)
                    load_x(n.next().next())

            if with_o:
                load_y(first)
                sp.dma_start(wo[:].rearrange("p o a k c -> p o (a k c)").bitcast(F32),
                             wo_src.rearrange("o p x -> p o x")).then_inc(wo_loaded, 16)
            load_x(first)
            sp.dma_start(wr_raw[:], w_router.rearrange("(k p) e -> p k e", p=P)).then_inc(wr_loaded, 16)
            for c, (src, _, _, rows) in enumerate(pieces):
                if c >= STAGES:
                    sp.wait_ge(w_lo, c - STAGES + 1)
                sp.dma_start(staged(c, rows), src).then_inc(w_loaded[c % STAGES], 16)
            sp.wait_ge(w_lo, n_pieces)
            load_x(second)
            if ternary:
                load_raw(first)
                load_raw(second)
            if with_o:
                load_y(second)
            each_block(sp, nblocks, body)
            for parity in range(2):
                sp.wait_ge(x_stored[parity], STORES * (nblocks // 2))

        @block.gpsimd
        def _(pool):
            nc.gpsimd.memset(eps_col[:], LN_EPS).then_inc(cols_ready, 1)
            nc.gpsimd.memset(zero_col[:], 0.0).then_inc(cols_ready, 1)
            nc.gpsimd.memset(ident[:], 0.0).then_inc(zeroed, 1)
            pool.wait_ge(zeroed, 1)
            nc.gpsimd.affine_select(out=ident[:], in_=ident[:], compare_op=ALU.not_equal, fill=1.0, base=0,
                                    pattern=[[-1, P]], channel_multiplier=1).then_inc(ident_ready, 1)
            nc.gpsimd.memset(fold[:], 0.0).then_inc(zeroed, 1)
            nc.gpsimd.iota(first_w[:], pattern=[[0, TT], [-1, NE]], base=NE, channel_multiplier=0,
                           allow_small_or_imprecise_dtypes=True).then_inc(consts_ready, 1)
            pool.wait_ge(zeroed, 2)
            nc.gpsimd.affine_select(out=fold[:], in_=fold[:], compare_op=ALU.not_equal, fill=1.0, base=0,
                                    pattern=[[-1, NE]], channel_multiplier=1).then_inc(zeroed, 1)
            pool.wait_ge(zeroed, 3)
            nc.gpsimd.affine_select(out=fold[:], in_=fold[:], compare_op=ALU.not_equal, fill=1.0, base=-NE,
                                    pattern=[[-1, NE]], channel_multiplier=1).then_inc(consts_ready, 1)
            nc.gpsimd.memset(own_tile[:], 0.0).then_inc(zeroed, 1)
            nc.gpsimd.memset(rows_of[:], 0.0).then_inc(zeroed, 1)
            pool.wait_ge(zeroed, 5)
            for a in range(2 * NE):
                nc.gpsimd.affine_select(out=own_tile[:], in_=own_tile[:], compare_op=ALU.not_equal, fill=1.0,
                                        base=-TT * a, pattern=[[-1, TT]], channel_multiplier=1).then_inc(zeroed, 1)
                pool.wait_ge(zeroed, 6 + a)
            nc.gpsimd.memset(rows_of[0:2 * NE * TT], 1.0).then_inc(zeroed, 1)
            pool.wait_ge(zeroed, 22)
            nc.gpsimd.affine_select(out=rows_of[:], in_=rows_of[:], compare_op=ALU.is_ge, fill=0.0, base=0,
                                    pattern=[[-TT, 2 * NE]], channel_multiplier=1).then_inc(zeroed, 1)
            pool.wait_ge(zeroed, 23)
            nc.gpsimd.affine_select(out=rows_of[:], in_=rows_of[:], compare_op=ALU.is_ge, fill=0.0, base=TT - 1,
                                    pattern=[[TT, 2 * NE]], channel_multiplier=-1).then_inc(consts_ready, 1)

            def split_y(m):
                for k in range(KT):
                    pool.wait_ge(yh_ready, m.at(KT, k + 1))
                    nc.gpsimd.tensor_tensor(yl[:, k], yt[:, k], yh[:, k].bitcast(F32),
                                            ALU.subtract).then_inc(yl_ready, 1)

            def body(n, look, look2):
                for e in range(NE):
                    pool.wait_ge(hh_ready, n.at(NE, e + 1))
                    nc.gpsimd.tensor_tensor(hl[:, e], hs[:, e % HS], hh[:, e].bitcast(F32),
                                            ALU.subtract).then_inc(hl_ready, 1)
                    if e == 3 and look2 and with_o:
                        split_y(n.next().next())

            if with_o:
                split_y(first)
                split_y(second)
            each_block(pool, nblocks, body)

        @block.scalar
        def _(act):
            def roots(m):
                act.wait_ge(var_ready, m.at(1, 1))
                nc.scalar.activation(root[:, 0], mv[:, :, 1], ACT.Sqrt, bias=eps_col[:])
                nc.scalar.activation(root[:, 1], mv[:, :, 1], ACT.Sqrt, bias=zero_col[:],
                                     scale=float(D)).then_inc(root_ready, 1)

            def x_hi(m):
                for k in range(KT):
                    act.wait_ge(t_filled, m.at(KT, k + 1))
                    nc.scalar.copy(xh[:, k], t_bank[k % 2][:]).then_inc(xh_ready, 1)

            def logits_copy(m):
                act.wait_ge(lg_filled, m.at(1, 1))
                nc.scalar.copy(lg[:], m_bank[0:2 * NE, :]).then_inc(lg_copied, 1)

            def gap_exp(m):
                act.wait_ge(gap_ready, m.at(1, 1))
                nc.scalar.activation(ratio[:], gap[:], ACT.Exp, bias=zero_col[:]).then_inc(ratio_ready, 1)

            def cb_copy(n, e):
                act.wait_ge(cb_filled, n.at(NE, e + 1))
                if e >= 2:
                    act.wait_ge(h_scaled, n.at(NE, e - 1))
                nc.scalar.copy(cb[:, e % 2], m_bank[:]).then_inc(cb_ready, 1)

            def y_hi(m):
                act.wait_ge(y_loaded, m.at(16, 16))
                act.wait_ge(res_filled, m.at(TT, 0))
                for k in range(KT):
                    nc.scalar.copy(yh[:, k], yt[:, k]).then_inc(yh_ready, 1)

            def body(n, look, look2):
                cb_copy(n, 0)
                for e in range(NE):
                    if e + 1 < NE:
                        cb_copy(n, e + 1)
                    act.wait_ge(h_scaled, n.at(NE, e + 1))
                    nc.scalar.copy(hh[:, e], hs[:, e % HS]).then_inc(hh_ready, 1)
                    if e == 3 and look2 and with_o:
                        y_hi(n.next().next())
                    if e == 3 + LAG and look:
                        roots(n.next())
                if look:
                    x_hi(n.next())
                    logits_copy(n.next())
                    gap_exp(n.next())
                if ternary:
                    act.wait_ge(raw_turned, n.at(1, 1))
                    nc.scalar.copy(parts[:, n.parity, 0], t_bank[0][:].rearrange("p (k o) -> p k o", k=KT)).then_inc(part_hi, 1)

            act.wait_ge(cols_ready, 2)
            def weights_hi(start, stop):
                for c in range(start, stop):
                    _, hi, _, rows = pieces[c]
                    act.wait_ge(w_loaded[c % STAGES], 16 * (c // STAGES + 1))
                    nc.scalar.copy(hi, staged(c, rows)).then_inc(w_hi, 1)

            if with_o:
                y_hi(first)
            weights_hi(0, n_before)
            if with_o:
                y_hi(second)
            roots(first)
            x_hi(first)
            weights_hi(n_before, n_between)
            logits_copy(first)
            gap_exp(first)
            weights_hi(n_between, n_pieces)
            each_block(act, nblocks, body)

        @block.vector
        def _(dve):
            LINKS = 26
            taken = [0]

            def link(m, ins):
                taken[0] += 1
                ins.then_inc(dve_step, 1)
                dve.wait_ge(dve_step, m.at(LINKS, taken[0]))

            def wide(col):
                return col.unsqueeze(2).to_broadcast([P, TT, NE])

            def x_ready(m):
                dve.wait_ge(x_loaded[m.parity], m.pair * 16 + 16)
                if with_o:
                    for j in range(TT):
                        dve.wait_ge(res_filled, m.at(TT, j + 1))
                        nc.vector.tensor_tensor(x[:, m.parity, j], o_bank[j % 2][:], x[:, m.parity, j],
                                                ALU.add).then_inc(res_added, 1)
                    dve.wait_ge(res_added, m.at(TT, TT))

            def moments(m, j):
                nc.vector.bn_stats(stats[:, j], x[:, m.parity, j]).then_inc(stats_ready, 1)

            def aggregate(m):
                for i in range(TT):
                    ins = nc.vector.bn_aggr(mv[:, i], stats[:, i])
                ins.then_inc(var_ready, 1)

            def scales(m):
                dve.wait_ge(root_ready, m.at(1, 1))
                link(m, nc.vector.reciprocal(inv0[:], root[:, 0]))
                link(m, nc.vector.tensor_tensor(newton[:], inv0[:], inv0[:], ALU.mult))
                link(m, nc.vector.scalar_tensor_tensor(newton[:], mv[:, :, 1], LN_EPS, newton[:], ALU.add, ALU.mult))
                link(m, nc.vector.tensor_scalar(newton[:], newton[:], -0.5, 1.5, ALU.mult, ALU.add))
                link(m, nc.vector.tensor_tensor(rstd[:], inv0[:], newton[:], ALU.mult))
                link(m, nc.vector.tensor_tensor(norm[:], root[:, 1], rstd[:], ALU.mult))
                link(m, nc.vector.tensor_scalar(norm[:], norm[:], NORM_MIN, None, ALU.max))
                link(m, nc.vector.reciprocal(inv_norm[:], norm[:]))

            def normalise(m):
                dve.wait_ge(t_filled, m.at(KT, 0))
                for j in range(TT):
                    ins = nc.vector.tensor_scalar(xn[:, j], x[:, m.parity, j], mv[:, j, 0:1], rstd[:, j:j + 1],
                                                  ALU.subtract, ALU.mult)
                ins.then_inc(xn_ready, 1)

            def x_lo(m):
                for k in range(KT):
                    dve.wait_ge(xh_ready, m.at(KT, k + 1))
                    nc.vector.tensor_tensor(xl[:, k], t_bank[k % 2][:], xh[:, k].bitcast(F32),
                                            ALU.subtract).then_inc(xl_ready, 1)

            def pick(m, i):
                link(m, nc.vector.tensor_reduce(peak[:, i], logit[:], AX.X, ALU.max))
                link(m, nc.vector.tensor_tensor(hit[:], logit[:], wide(peak[:, i]), ALU.is_equal))
                link(m, nc.vector.tensor_tensor(score[:], hit[:], first_w[:], ALU.mult))
                link(m, nc.vector.tensor_reduce(who[:], score[:], AX.X, ALU.max))
                link(m, nc.vector.tensor_tensor(top[i][:], score[:], wide(who[:]), ALU.is_equal))

            def route(m):
                dve.wait_ge(lt_filled, m.at(1, 1))
                link(m, nc.vector.tensor_tensor(logit[:], m_bank[:, 0:TT * NE].rearrange("p (j e) -> p j e", e=NE),
                                                wide(inv_norm[:]), ALU.mult))
                pick(m, 0)
                link(m, nc.vector.scalar_tensor_tensor(logit[:], top[0][:], -BIG, logit[:], ALU.mult, ALU.add))
                pick(m, 1)
                nc.vector.tensor_tensor(gap[:], peak[:, 1], peak[:, 0], ALU.subtract).then_inc(gap_ready, 1)
                dve.wait_ge(ratio_ready, m.at(1, 1))
                link(m, nc.vector.tensor_scalar(total[:], ratio[:], 1.0, None, ALU.add))
                link(m, nc.vector.reciprocal(gate[:, 0], total[:]))
                link(m, nc.vector.tensor_tensor(gate[:, 1], ratio[:], gate[:, 0], ALU.mult))
                nc.vector.tensor_tensor(score[:], top[0][:], wide(gate[:, 0]), ALU.mult)
                link(m, nc.vector.tensor_tensor(hit[:], top[1][:], wide(gate[:, 1]), ALU.mult))
                link(m, nc.vector.tensor_tensor(comb[:].rearrange("p e j -> p j e"), score[:], hit[:], ALU.add))
                dve.wait_ge(ct_filled, m.at(1, 0))
                link(m, nc.vector.tensor_copy(comb_parts[:, 0], comb[:]))
                nc.vector.tensor_tensor(comb_parts[:, 1], comb[:], comb_parts[:, 0].bitcast(F32),
                                        ALU.subtract).then_inc(comb_ready, 1)
                assert taken[0] == LINKS

            def mask_combine(m):
                dve.wait_ge(cb_filled, m.at(NE, 0))
                dve.wait_ge(ct_filled, m.at(1, 1))
                nc.vector.tensor_tensor(cm[:], m_bank[:, 0:P].unsqueeze(1).to_broadcast([P, TT, P]),
                                        own_tile[:].unsqueeze(2).to_broadcast([P, TT, P]),
                                        ALU.mult).then_inc(cm_ready, 1)

            def add_out(n, j):
                dve.wait_ge(o_filled, n.at(TT, j + 1))
                nc.vector.scalar_tensor_tensor(x[:, n.parity, j], o_bank[j % 2][:], 0.5, x[:, n.parity, j],
                                               ALU.mult, ALU.add).then_inc(o_added, 1)

            def wide_group(col):
                return col.unsqueeze(2).to_broadcast([P, KT, P])

            def quantise(n, step):
                w = raw[:, n.parity]
                if step > 0:
                    dve.wait_ge(raw_step, n.at(7, step))
                if step == 0:
                    dve.wait_ge(raw_loaded[n.parity], n.pair * 16 + 16)
                    ins = nc.vector.tensor_reduce(sums[:], w, AX.X, ALU.add, apply_absolute_value=True)
                if step == 1:
                    ins = nc.vector.tensor_scalar(scale[:], sums[:], 1.0 / GROUP, Q_EPS, ALU.mult, ALU.max)
                if step == 2:
                    nc.vector.tensor_scalar(half[:, 0], scale[:], 0.5, None, ALU.mult)
                    ins = nc.vector.tensor_scalar(half[:, 1], scale[:], -0.5, None, ALU.mult)
                if step == 3:
                    nc.vector.tensor_tensor(pos[:], w, wide_group(half[:, 0]), ALU.is_gt)
                    ins = nc.vector.tensor_tensor(neg[:], w, wide_group(half[:, 1]), ALU.is_lt)
                if step == 4:
                    ins = nc.vector.tensor_tensor(pos[:], pos[:], neg[:], ALU.subtract)
                if step == 5:
                    ins = nc.vector.tensor_tensor(pos[:], pos[:], wide_group(scale[:]), ALU.mult)
                if step == 6:
                    ins = nc.vector.tensor_tensor(pos[:], pos[:], w, ALU.subtract)
                if step == 7:
                    ins = nc.vector.tensor_tensor(w, w, pos[:], ALU.add)
                ins.then_inc(raw_step if step < 7 else raw_ready, 1)

            def parts_lo(n):
                dve.wait_ge(part_hi, n.at(1, 1))
                nc.vector.tensor_tensor(parts[:, n.parity, 1], t_bank[0][:].rearrange("p (k o) -> p k o", k=KT),
                                        parts[:, n.parity, 0].bitcast(F32), ALU.subtract).then_inc(part_lo, 1)

            def out_moments(n, j):
                if moments_dst is None:
                    return
                dve.wait_ge(o_added, n.at(TT, j + 1))
                nc.vector.bn_stats(out_stats[:, n.parity, j], x[:, n.parity, j]).then_inc(out_stats_ready, 1)

            def body(n, look, look2):
                m = n.next()
                taken[0] = 0
                for e in range(NE):
                    dve.wait_ge(cb_ready, n.at(NE, e + 1))
                    dve.wait_ge(h_filled, n.at(NE, e + 1))
                    if e >= HS:
                        dve.wait_ge(hl_ready, n.at(NE, e - HS + 1))
                    if look and e == 2 + LAG:
                        dve.wait_ge(stats_ready, m.at(TT, TT))
                    nc.vector.tensor_tensor(hs[:, e % HS], h_bank[e % 3][:], cb[:, e % 2], ALU.mult).then_inc(h_scaled, 1)
                    if ternary:
                        for step in ((0,), (1, 2, 3), (), (4,), (5,), (6,), (), ())[e]:
                            quantise(n, step)
                    if not look:
                        continue
                    if e == LAG:
                        x_ready(m)
                    if e in (LAG, LAG + 1):
                        moments(m, 2 * (e - LAG))
                        moments(m, 2 * (e - LAG) + 1)
                    if e == 2 + LAG:
                        aggregate(m)
                    if e == 4 + LAG:
                        scales(m)
                    if e == 5 + LAG:
                        normalise(m)
                if look:
                    x_lo(m)
                if ternary:
                    quantise(n, 7)
                add_out(n, 0)
                add_out(n, 1)
                out_moments(n, 0)
                if look:
                    route(m)
                add_out(n, 2)
                out_moments(n, 1)
                out_moments(n, 2)
                if look:
                    mask_combine(m)
                if ternary:
                    parts_lo(n)
                add_out(n, 3)
                out_moments(n, 3)

            dve.wait_ge(wr_loaded, 16)
            nc.vector.memset(wr[:, :, 3].bitcast(F32), 0.0)
            nc.vector.tensor_copy(wr[:, :, 0], wr_raw[:])
            nc.vector.tensor_copy(wr[:, :, 2], wr_raw[:]).then_inc(wr_step, 1)
            dve.wait_ge(wr_step, 1)
            nc.vector.tensor_tensor(wr[:, :, 1], wr_raw[:], wr[:, :, 0].bitcast(F32), ALU.subtract).then_inc(wr_step, 1)
            nc.vector.memset(comb_parts[:, 2:4].bitcast(F32), 0.0)
            def weights_lo(start, stop):
                for c in range(start, stop):
                    _, hi, lo, rows = pieces[c]
                    dve.wait_ge(w_hi, c + 1)
                    nc.vector.tensor_tensor(lo, staged(c, rows), hi.bitcast(F32), ALU.subtract).then_inc(w_lo, 1)

            weights_lo(0, n_before)
            x_ready(first)
            for j in range(TT):
                moments(first, j)
            dve.wait_ge(stats_ready, TT)
            aggregate(first)
            scales(first)
            normalise(first)
            x_lo(first)
            weights_lo(n_before, n_between)
            dve.wait_ge(consts_ready, 3)
            for e in range(NE):
                nc.vector.tensor_tensor(spread[:, e], rows_of[:, e:e + 1].to_broadcast([P, P]),
                                        rows_of[:, NE + e:NE + e + 1].to_broadcast([P, P]),
                                        ALU.add).then_inc(wr_step, 1)
            route(first)
            mask_combine(first)
            weights_lo(n_between, n_pieces)
            each_block(dve, nblocks, body)

        @block.tensor
        def _(pe):
            def residual(m):
                pe.wait_ge(yl_ready, m.at(KT, KT))
                for j in range(TT):
                    if j >= 2:
                        pe.wait_ge(res_added, m.at(TT, j - 1))
                    t = slice(j * P, (j + 1) * P)
                    for k in range(KT):
                        nc.tensor.matmul(o_bank[j % 2][:], yh[:, k, t], wo[:, :, 0, k], start=k == 0, stop=False)
                        nc.tensor.matmul(o_bank[j % 2][:], yh[:, k, t], wo[:, :, 1, k], start=False, stop=False)
                        mm = nc.tensor.matmul(o_bank[j % 2][:], yl[:, k, t], wo[:, :, 0, k], start=False, stop=k == KT - 1)
                    mm.then_inc(res_filled, 1)

            def hidden(n, e):
                if e == 0:
                    pe.wait_ge(xl_ready, n.at(KT, KT))
                if e >= 3:
                    pe.wait_ge(h_scaled, n.at(NE, e - 2))
                r = slice(e * RANK, (e + 1) * RANK)
                for k in range(KT):
                    nc.tensor.matmul(h_bank[e % 3][:], wa[:, k, 0, r], xh[:, k], start=k == 0, stop=False)
                    nc.tensor.matmul(h_bank[e % 3][:], wa[:, k, 0, r], xl[:, k], start=False, stop=False)
                    mm = nc.tensor.matmul(h_bank[e % 3][:], wa[:, k, 1, r], xh[:, k], start=False, stop=k == KT - 1)
                mm.then_inc(h_filled, 1)

            def output(n, j, look, half):
                if half == 0 and j < 2 and with_o and look:
                    pe.wait_ge(res_added, n.at(TT, 2 * TT))
                if half == 0 and j >= 2:
                    pe.wait_ge(o_added, n.at(TT, j - 1))
                t = slice(j * P, (j + 1) * P)
                for e in range(NE // 2 * half, NE // 2 * (half + 1)):
                    if j == 0:
                        pe.wait_ge(hl_ready, n.at(NE, e + 1))
                    nc.tensor.matmul(o_bank[j % 2][:], hh[:, e, t], wb[:, e, 0], start=e == 0, stop=False)
                    nc.tensor.matmul(o_bank[j % 2][:], hh[:, e, t], wb[:, e, 1], start=False, stop=False)
                    mm = nc.tensor.matmul(o_bank[j % 2][:], hl[:, e, t], wb[:, e, 0], start=False, stop=e == NE - 1)
                if half == 1:
                    mm.then_inc(o_filled, 1)

            def turn_x(m, k):
                pe.wait_ge(xn_ready, m.at(1, 1))
                pe.wait_ge(xl_ready, m.at(KT, max(k - 1, 0)))
                for j in range(TT):
                    mm = nc.tensor.transpose(t_bank[k % 2][:, j * P:(j + 1) * P], xn[:, j, k * P:(k + 1) * P], ident[:])
                mm.then_inc(t_filled, 1)

            def logits(m):
                pe.wait_ge(xl_ready, m.at(KT, KT))
                pe.wait_ge(cb_ready, m.at(NE, 0))
                for k in range(KT):
                    nc.tensor.matmul(m_bank[0:2 * NE, :], wr[:, k, 0:2].rearrange("p a e -> p (a e)"), xh[:, k],
                                     start=k == 0, stop=False)
                    mm = nc.tensor.matmul(m_bank[0:2 * NE, :], wr[:, k, 2:4].rearrange("p a e -> p (a e)"), xl[:, k],
                                          start=False, stop=k == KT - 1)
                mm.then_inc(lg_filled, 1)

            def turn_logits(m):
                pe.wait_ge(lg_copied, m.at(1, 1))
                for j in range(TT):
                    mm = nc.tensor.matmul(m_bank[:, j * NE:(j + 1) * NE], lg[:, j * P:(j + 1) * P], fold[:],
                                          start=True, stop=True)
                mm.then_inc(lt_filled, 1)

            def turn_combine(m):
                pe.wait_ge(comb_ready, m.at(1, 1))
                nc.tensor.transpose(m_bank[:, 0:P], comb_parts[:].rearrange("p a e j -> p (a e j)").bitcast(F32),
                                    ident[:]).then_inc(ct_filled, 1)

            def spread_combine(n, e):
                if e == 0:
                    pe.wait_ge(cm_ready, n.at(1, 1))
                else:
                    pe.wait_ge(cb_ready, n.at(NE, e))
                nc.tensor.matmul(m_bank[:], spread[:, e], cm[:].rearrange("p j t -> p (j t)"),
                                 start=True, stop=True).then_inc(cb_filled, 1)

            def turn_raw(n):
                pe.wait_ge(raw_ready, n.at(1, 1))
                for k in range(KT):
                    mm = nc.tensor.transpose(t_bank[0][:, k * P:(k + 1) * P], raw[:, n.parity, k], ident[:])
                mm.then_inc(raw_turned, 1)

            def body(n, look, look2):
                m = n.next()
                for e in range(NE):
                    hidden(n, e)
                    spread_combine(n, e)
                    if e == 1 and look and with_o:
                        pe.wait_ge(h_scaled, n.at(NE, 1))
                        residual(m)
                output(n, 0, look, 0)
                if look:
                    turn_x(m, 0)
                    turn_x(m, 1)
                output(n, 0, look, 1)
                if look:
                    turn_x(m, 2)
                    turn_x(m, 3)
                output(n, 1, look, 0)
                if look:
                    logits(m)
                output(n, 1, look, 1)
                if look:
                    turn_logits(m)
                output(n, 2, look, 0)
                if ternary:
                    turn_raw(n)
                output(n, 2, look, 1)
                output(n, 3, look, 0)
                if look:
                    turn_combine(m)
                output(n, 3, look, 1)

            if with_o:
                pe.wait_ge(wo_loaded, 16)
                residual(first)
            pe.wait_ge(ident_ready, 1)
            for k in range(KT):
                turn_x(first, k)
            pe.wait_ge(wr_step, 2)
            logits(first)
            pe.wait_ge(consts_ready, 3)
            turn_logits(first)
            turn_combine(first)
            pe.wait_ge(w_lo, n_pieces)
            each_block(pe, nblocks, body)



HEADS = 16
HD = D // HEADS
HALF = HD // 2
GH = 4
NG = HEADS // GH
SEQ = 1024
QB = 512
ST = SEQ // P
SCALE = HD ** -0.5
STEPS = [(qb, kt) for qb in range(SEQ // QB) for kt in reversed(range((qb + 1) * QB // P))]
NS = len(STEPS)
PIECES = [(i, k, min(k + QB, (i + 1) * P)) for i in range(ST) for k in range(0, (i + 1) * P, QB)]
NP = GH * len(PIECES)
SLOTS = (0, 1, 4, 8, 12)


def first_query(t):
    qb, kt = STEPS[t]
    return max(kt * P - qb * QB, 0)


def slot_pieces(t, slot):
    widths = [QB - first_query(i) if i >= 2 else 0 for i in range(NS)]
    total = sum(widths) * SLOTS[-1]
    lo, hi = ((sum(widths[:t]) * SLOTS[-1] + widths[t] * s) * NP // total for s in SLOTS[slot:slot + 2])
    return range(lo, hi)


class Unit:

    def __init__(self, b, g):
        self.b, self.g = b, g

    def plus(self, n):
        return Unit(self.b + (self.g + n) // NG, (self.g + n) % NG)

    def at(self, k, c):
        return self.b * (NG * k) + (self.g * k + c)


def attention_phase(nc, psum, nbatch, x_src, moments_src, wqk_src, wv_src, cos_src, sin_src, y_dst, rope_tmp, mrow_tmp):
    with ExitStack() as ctx:
        def sb(name, shape, dt):
            return ctx.enter_context(nc.sbuf_tensor(f"att_{name}", shape, dt))

        def sem(name):
            return ctx.enter_context(nc.semaphore(f"att_{name}"))

        ident = sb("ident", [P, P], F32)
        ident_b = sb("ident_b", [P, P], BF16)
        hide_k = sb("hide_k", [P, P], BF16)
        hide_q = sb("hide_q", [P, P], BF16)
        ones = sb("ones", [P, HD], F32)
        cos = sb("cos", [P, SEQ], F32)
        sin = sb("sin", [P, SEQ], F32)
        wqk = sb("wqk", [P, 2, 2, KT, P], F32R)
        wv = sb("wv", [P, KT, 2, KT, P], F32R)
        mv = sb("mv", [P, nbatch * ST, 2], F32)
        root = sb("root", [P, nbatch * ST], F32)
        newton = sb("newton", [P, nbatch * ST], F32)
        rstd = sb("rstd", [P, nbatch * ST], F32)
        eps_col = sb("eps_col", [P, 1], F32)
        xt = sb("xt", [P, ST, D], F32)
        xh = sb("xh", [P, KT, SEQ], F32R)
        xl = sb("xl", [P, KT, SEQ], F32R)
        v = sb("v", [P, ST, D], F32)
        qs = sb("qs", [P, 2, GH, SEQ], F32R)
        ks = sb("ks", [P, 2, GH, SEQ], F32R)
        ra = sb("ra", [P, 2, 2, QB], F32)
        rb = sb("rb", [P, 2, 2, QB], F32)
        roped_hi = sb("roped_hi", [P, 2, QB], F32R)
        mxp = sb("mxp", [P, GH, len(PIECES)], F32)
        mneg = sb("mneg", [P, GH, ST], F32)
        mrow = sb("mrow", [GH * ST, P], F32R)
        probs = sb("probs", [P, 2, GH, QB], F32)
        acc = sb("acc", [P, 2, QB], F32)
        den = sb("den", [P, 2, QB], F32)

        stats = acc[:].rearrange("p j t -> p (j t)")[:, 0:nbatch * ST * 6].rearrange("p (i c) -> p i c", c=6)

        s_bank = [psum[:, 0:2], psum[:, 2:4]]
        w_bank = [psum[:, 4], psum[:, 5]]
        pv_bank, den_bank = psum[:, 6], psum[:, 7]

        def t_bank(i):
            return (psum[:, 2], psum[:, 3], psum[:, 0], psum[:, 1])[i % 4]

        def v_bank(i):
            return psum[:, 2 + i % 2]

        def qk_bank(f):
            return (psum[:, 2], psum[:, 3]) if f == 0 else (w_bank[0], w_bank[1])

        zeroed = sem("zeroed")
        consts_ready = sem("consts_ready")
        ks_ready = sem("ks_ready")
        tables_loaded = sem("tables_loaded")
        wv_loaded = sem("wv_loaded")
        wqk_loaded = sem("wqk_loaded")
        stats_loaded = sem("stats_loaded")
        mv_ready = sem("mv_ready")
        root_ready = sem("root_ready")
        rstd_step = sem("rstd_step")
        xt_loaded = [sem(f"xt_loaded{i}") for i in range(2)]
        xt_ready = sem("xt_ready")
        xt_turned = sem("xt_turned")
        xh_ready = sem("xh_ready")
        xl_ready = sem("xl_ready")
        v_filled = sem("v_filled")
        v_ready = sem("v_ready")
        qk_filled = sem("qk_filled")
        qk_read = sem("qk_read")
        rope_ready = sem("rope_ready")
        rope_hi = sem("rope_hi")
        rope_lo = sem("rope_lo")
        rope_stored = sem("rope_stored")
        placed = sem("placed")
        mx_filled = sem("mx_filled")
        mx_read = sem("mx_read")
        mneg_ready = sem("mneg_ready")
        mrow_turned = sem("mrow_turned")
        mrow_copied = sem("mrow_copied")
        mrow_stored = sem("mrow_stored")
        mrow_placed = sem("mrow_placed")
        s_filled = sem("s_filled")
        exp_done = sem("exp_done")
        pv_done = sem("pv_done")
        acc_copied = sem("acc_copied")
        den_copied = sem("den_copied")
        inv_ready = sem("inv_ready")
        y_ready = sem("y_ready")
        y_stored = [sem("y_stored0"), sem("y_stored1")]

        U0 = Unit(0, 0)

        def exists(u):
            return not (isinstance(u.b, int) and u.b >= nbatch)

        def each_batch(engine, body):
            with engine.Fori(0, nbatch - 1) as b:
                for g in range(NG):
                    body(Unit(b, g))
            for g in range(NG):
                body(Unit(nbatch - 1, g))

        x_in = x_src.rearrange("(b t p) d -> b p t d", p=P, t=ST)
        y_out = y_dst.rearrange("(g p) (b j t) -> g b j p t", p=P, j=2, t=QB)

        block = ctx.enter_context(nc.Block())

        @block.sync
        def _(sp):
            def wqk_load(u):
                if u.g or not isinstance(u.b, int):
                    sp.wait_ge(qk_filled, u.at(4, 0))
                sp.dma_start(wqk[:].rearrange("p f a k c -> p f (a k c)").bitcast(F32),
                             wqk_src[u.g]).then_inc(wqk_loaded, 16)

            def load_batch(b):
                if not isinstance(b, int):
                    sp.wait_ge(xt_turned, b * ST)
                for half in range(2):
                    t = slice(half * ST // 2, (half + 1) * ST // 2)
                    sp.dma_start(xt[:, t], x_in[b, :, t]).then_inc(xt_loaded[half], 16)

            def store_rope(u):
                for f in range(2):
                    for part, made in enumerate((rope_hi, rope_lo)):
                        sp.wait_ge(made, u.at(4, 2 * f + 2))
                        sp.dma_start(rope_tmp[u.g % 2, part].rearrange("(p r) t -> p r t", r=2)[:, :, f * QB:(f + 1) * QB],
                                     ra[:, f] if part else roped_hi[:].bitcast(F32)).then_inc(rope_stored, 16)

            def place(u, free):
                if free is not None:
                    sp.wait_ge(s_filled, free)
                src = rope_tmp[u.g % 2].rearrange("a (w h r) t -> a w r h t", w=2, h=GH)
                for slot, (which, parts) in enumerate(((0, (0, 0, 1)), (1, (0, 1, 0)))):
                    dst = (qs, ks)[slot]
                    for row, part in enumerate(parts):
                        sp.dma_start(dst[row * HD:(row + 1) * HD, u.g % 2].bitcast(F32), src[part, which]).then_inc(placed, 16)

            def place_mrow(u):
                sp.wait_ge(mrow_copied, u.at(1, 1))
                sp.dma_start(mrow_tmp[:], mrow[:].bitcast(F32)).then_inc(mrow_stored, 16)
                sp.wait_ge(mrow_stored, u.at(16, 16))
                sp.dma_start(qs[3 * HD:3 * HD + 1, u.g % 2].rearrange("o h t -> o (h t)").bitcast(F32),
                             mrow_tmp.rearrange("(o r) t -> o (r t)", o=1)).then_inc(mrow_placed, 16)

            def store_y(u, j):
                sp.wait_ge(y_ready, u.at(2, j + 1))
                sp.dma_start(y_out[u.g, u.b, j], acc[:, j]).then_inc(y_stored[j], 16)

            def body(u):
                if exists(u.plus(3)):
                    wqk_load(u.plus(3))
                if u.g == 0 and exists(u.plus(NG)):
                    load_batch(u.b + 1)
                if exists(u.plus(2)):
                    store_rope(u.plus(2))
                store_y(u, 0)
                if exists(u.plus(1)):
                    place_mrow(u.plus(1))
                if exists(u.plus(2)):
                    place(u.plus(2), u.at(2 * NS, 2 * NS))
                store_y(u, 1)

            sp.dma_start(stats[:], moments_src).then_inc(stats_loaded, 16)
            load_batch(0)
            wqk_load(U0)
            sp.dma_start(cos[:], cos_src).then_inc(tables_loaded, 16)
            sp.dma_start(sin[:], sin_src).then_inc(tables_loaded, 16)
            sp.dma_start(wv[:].rearrange("p o a k c -> p o (a k c)").bitcast(F32),
                         wv_src.rearrange("o p x -> p o x")).then_inc(wv_loaded, 16)
            wqk_load(U0.plus(1))
            store_rope(U0)
            sp.wait_ge(rope_stored, 64)
            place(U0, None)
            wqk_load(U0.plus(2))
            store_rope(U0.plus(1))
            sp.wait_ge(rope_stored, 128)
            place(U0.plus(1), None)
            place_mrow(U0)
            each_batch(sp, body)
            sp.wait_ge(y_stored[0], 16 * NG * nbatch + 1)
            sp.wait_ge(y_stored[1], 16 * NG * nbatch + 1)

        @block.gpsimd
        def _(pool):
            nc.gpsimd.memset(ident[:], 0.0).then_inc(zeroed, 1)
            nc.gpsimd.memset(ident_b[:], 0.0).then_inc(zeroed, 1)
            nc.gpsimd.memset(hide_k[:], 0.0).then_inc(zeroed, 1)
            nc.gpsimd.memset(hide_q[:], 0.0).then_inc(zeroed, 1)
            nc.gpsimd.memset(ones[:], 1.0).then_inc(y_stored[0], 1)
            nc.gpsimd.memset(eps_col[:], LN_EPS).then_inc(y_stored[1], 1)
            pool.wait_ge(zeroed, 4)
            for tile in (ident, ident_b):
                nc.gpsimd.affine_select(out=tile[:], in_=tile[:], compare_op=ALU.not_equal, fill=1.0, base=0,
                                        pattern=[[-1, P]], channel_multiplier=1).then_inc(consts_ready, 1)
            nc.gpsimd.affine_select(out=hide_k[:], in_=hide_k[:], compare_op=ALU.is_ge, fill=-BIG, base=0,
                                    pattern=[[-1, P]], channel_multiplier=1).then_inc(consts_ready, 1)
            nc.gpsimd.affine_select(out=hide_q[:], in_=hide_q[:], compare_op=ALU.is_ge, fill=-BIG, base=0,
                                    pattern=[[1, P]], channel_multiplier=-1).then_inc(consts_ready, 1)

            def mix(u):
                for f in range(2):
                    pool.wait_ge(qk_read, u.at(2, f + 1))
                    nc.gpsimd.tensor_tensor(ra[:, f, 0], ra[:, f, 0], rb[:, f, 0], ALU.subtract).then_inc(rope_ready, 1)
                    nc.gpsimd.tensor_tensor(ra[:, f, 1], ra[:, f, 1], rb[:, f, 1], ALU.add).then_inc(rope_ready, 1)

            def rope_los(u):
                for f in range(2):
                    for r in range(2):
                        pool.wait_ge(rope_hi, u.at(4, 2 * f + r + 1))
                        nc.gpsimd.tensor_tensor(ra[:, f, r].bitcast(F32R), ra[:, f, r], roped_hi[:, r].bitcast(F32),
                                                ALU.subtract).then_inc(rope_lo, 1)

            def normalise_y(u, j):
                pool.wait_ge(inv_ready, u.at(2, j + 1))
                pool.wait_ge(acc_copied, u.at(2, j + 1))
                nc.gpsimd.tensor_tensor(acc[:, j], acc[:, j], den[:, j], ALU.mult).then_inc(y_ready, 1)

            def body(u):
                if exists(u.plus(2)):
                    rope_los(u.plus(2))
                normalise_y(u, 0)
                normalise_y(u, 1)
                if exists(u.plus(3)):
                    mix(u.plus(3))

            mix(U0)
            rope_los(U0)
            mix(U0.plus(1))
            rope_los(U0.plus(1))
            mix(U0.plus(2))
            each_batch(pool, body)

        @block.scalar
        def _(act):
            def x_hi(b, i):
                bank = t_bank(i)
                act.wait_ge(xt_turned, b * ST + (i + 1))
                nc.scalar.copy(xh[:, :, i * P:(i + 1) * P], bank.rearrange("p (k t) -> p k t", k=KT)).then_inc(xh_ready, 1)

            def v_copy(b, i):
                act.wait_ge(v_filled, b * ST + (i + 1))
                nc.scalar.copy(v[:, i], v_bank(i)).then_inc(v_ready, 1)

            def rope_his(u, f, before=None):
                if before is not None:
                    act.wait_ge(placed, before)
                act.wait_ge(rope_stored, u.at(64, 32 * f))
                for r in range(2):
                    act.wait_ge(rope_ready, u.at(4, 2 * f + r + 1))
                    nc.scalar.copy(roped_hi[:, r], ra[:, f, r]).then_inc(rope_hi, 1)

            def mrow_copy(u):
                act.wait_ge(mrow_turned, u.at(1, 1))
                act.wait_ge(mrow_stored, u.at(16, 0))
                nc.scalar.copy(mrow[:], s_bank[0][0:GH * ST, 0, 0:P]).then_inc(mrow_copied, 1)

            def exps(u, t):
                first = first_query(t)
                for hp in range(2):
                    act.wait_ge(s_filled, u.at(2 * NS, 2 * t + hp + 1))
                    if hp == 0 and t >= 2:
                        act.wait_ge(pv_done, u.at(NS, t - 1))
                    nc.scalar.activation(probs[:, t % 2, 2 * hp:2 * hp + 2, first:QB], s_bank[hp][:, :, first:QB],
                                         ACT.Exp, scale=SCALE).then_inc(exp_done, 1)

            def sums_copy(u, j):
                act.wait_ge(pv_done, u.at(NS, 4 if j == 0 else NS))
                act.wait_ge(y_stored[j], u.at(16, 1))
                nc.scalar.copy(den[:, j], den_bank).then_inc(den_copied, 1)
                nc.scalar.copy(acc[:, j], pv_bank).then_inc(acc_copied, 1)

            def body(u):
                for t in range(NS):
                    exps(u, t)
                    if t == 1 and exists(u.plus(2)):
                        rope_his(u.plus(2), 0, u.plus(1).at(96, 0))
                    if t == 7 and exists(u.plus(2)):
                        rope_his(u.plus(2), 1)
                    if t == 4:
                        sums_copy(u, 0)
                sums_copy(u, 1)
                if exists(u.plus(2)):
                    act.wait_ge(rope_stored, u.plus(2).at(64, 64))
                if exists(u.plus(1)):
                    mrow_copy(u.plus(1))
                if u.g == 0 and exists(u.plus(NG)):
                    for i in range(ST):
                        x_hi(u.b + 1, i)
                if u.g == NG - 1 and exists(u.plus(NG)):
                    for i in range(ST):
                        v_copy(u.b + 1, i)

            act.wait_ge(consts_ready, 4)
            act.wait_ge(mv_ready, 1)
            nc.scalar.activation(root[:], mv[:, :, 1], ACT.Sqrt, bias=eps_col[:]).then_inc(root_ready, 1)
            for i in range(ST):
                x_hi(0, i)
            for i in range(ST):
                v_copy(0, i)
                if i in (1, 3):
                    rope_his(U0, i // 2)
            rope_his(U0.plus(1), 0)
            rope_his(U0.plus(1), 1)
            mrow_copy(U0)
            each_batch(act, body)

        @block.vector
        def _(dve):
            def normalise(b, i):
                dve.wait_ge(xt_loaded[i // (ST // 2)], b * 16 + 16)
                nc.vector.tensor_scalar(xt[:, i], xt[:, i], mv[:, bass.ds(b * ST + i, 1), 0], rstd[:, bass.ds(b * ST + i, 1)],
                                        ALU.subtract, ALU.mult).then_inc(xt_ready, 1)

            def x_lo(b, i):
                dve.wait_ge(xh_ready, b * ST + (i + 1))
                t = slice(i * P, (i + 1) * P)
                nc.vector.tensor_tensor(xl[:, :, t], t_bank(i).rearrange("p (k t) -> p k t", k=KT),
                                        xh[:, :, t].bitcast(F32), ALU.subtract).then_inc(xl_ready, 1)

            def rope(u, reused):
                for f in range(2):
                    a, c = qk_bank(f)
                    p = slice(f * QB, (f + 1) * QB)
                    dve.wait_ge(qk_filled, u.at(4, 2 * f + 2))
                    if reused:
                        dve.wait_ge(rope_stored, u.at(64, 32 * f - 32))
                    nc.vector.tensor_tensor(ra[:, f, 0], a, cos[:, p], ALU.mult)
                    nc.vector.tensor_tensor(ra[:, f, 1], a, sin[:, p], ALU.mult)
                    nc.vector.tensor_tensor(rb[:, f, 0], c, sin[:, p], ALU.mult)
                    nc.vector.tensor_tensor(rb[:, f, 1], c, cos[:, p], ALU.mult).then_inc(qk_read, 1)

            def piece_max(u, c):
                h, (i, k0, k1) = c // len(PIECES), PIECES[c % len(PIECES)]
                dve.wait_ge(mx_filled, u.at(NP, c + 1))
                nc.vector.tensor_reduce(mxp[:, h, c % len(PIECES):c % len(PIECES) + 1], w_bank[c % 2][:, 0:k1 - k0], AX.X,
                                        ALU.max).then_inc(mx_read, 1)

            def row_max(u):
                dve.wait_ge(mx_read, u.at(NP, NP))
                dve.wait_ge(mrow_turned, u.at(1, 0))
                n1 = QB // P
                nc.vector.tensor_scalar(mneg[:, :, 0:n1], mxp[:, :, 0:n1], -1.0, None, ALU.mult)
                nc.vector.tensor_reduce(mneg[:, :, n1:ST], mxp[:, :, n1:].rearrange("p h (i c) -> p h i c", c=2), AX.X,
                                        ALU.max, negate=True).then_inc(mneg_ready, 1)

            def invert(u, j, quarter):
                if quarter == 0:
                    dve.wait_ge(den_copied, u.at(2, j + 1))
                q = slice(quarter * P, (quarter + 1) * P)
                ins = nc.vector.reciprocal(den[:, j, q], den[:, j, q])
                if quarter == 3:
                    ins.then_inc(inv_ready, 1)

            def body(u):
                for t in range(NS):
                    if not exists(u.plus(1)):
                        if t == 5:
                            for quarter in range(4):
                                invert(u, 0, quarter)
                    else:
                        for slot in range(len(SLOTS) - 1):
                            for c in slot_pieces(t, slot):
                                piece_max(u.plus(1), c)
                            if t in (5, 6) and slot in (1, 3):
                                invert(u, 0, (t - 5) * 2 + slot // 2)
                    if u.g == 0 and t < ST and exists(u.plus(NG)):
                        normalise(u.b + 1, t)
                if exists(u.plus(1)):
                    row_max(u.plus(1))
                for quarter in range(4):
                    invert(u, 1, quarter)
                if exists(u.plus(3)):
                    rope(u.plus(3), True)
                if u.g == 0 and exists(u.plus(NG)):
                    for i in range(ST):
                        x_lo(u.b + 1, i)

            dve.wait_ge(stats_loaded, 16)
            for i in range(nbatch * ST):
                ins = nc.vector.bn_aggr(mv[:, i], stats[:, i])
            ins.then_inc(mv_ready, 1)
            dve.wait_ge(root_ready, 1)
            nc.vector.reciprocal(rstd[:], root[:]).then_inc(rstd_step, 1)
            dve.wait_ge(rstd_step, 1)
            nc.vector.tensor_tensor(newton[:], rstd[:], rstd[:], ALU.mult).then_inc(rstd_step, 1)
            dve.wait_ge(rstd_step, 2)
            nc.vector.scalar_tensor_tensor(newton[:], mv[:, :, 1], LN_EPS, newton[:], ALU.add, ALU.mult).then_inc(rstd_step, 1)
            dve.wait_ge(rstd_step, 3)
            nc.vector.tensor_scalar(newton[:], newton[:], -0.5, 1.5, ALU.mult, ALU.add).then_inc(rstd_step, 1)
            dve.wait_ge(rstd_step, 4)
            nc.vector.tensor_tensor(rstd[:], rstd[:], newton[:], ALU.mult).then_inc(rstd_step, 1)
            dve.wait_ge(rstd_step, 5)
            for i in range(ST):
                normalise(0, i)
            for i in range(ST):
                x_lo(0, i)
            nc.vector.memset(ks[3 * HD:3 * HD + 1].bitcast(F32), 1.0).then_inc(ks_ready, 1)
            dve.wait_ge(tables_loaded, 32)
            rope(U0, False)
            rope(U0.plus(1), True)
            for c in range(NP):
                piece_max(U0, c)
            row_max(U0)
            rope(U0.plus(2), True)
            each_batch(dve, body)

        @block.tensor
        def _(pe):
            def turn(b, i):
                pe.wait_ge(xt_ready, b * ST + (i + 1))
                if i >= 4:
                    pe.wait_ge(xl_ready, b * ST + (i - 3))
                for k in range(KT):
                    mm = nc.tensor.transpose(t_bank(i)[:, k * P:(k + 1) * P], xt[:, i, k * P:(k + 1) * P], ident[:])
                mm.then_inc(xt_turned, 1)

            def project_v(b, i):
                if i >= 2:
                    pe.wait_ge(v_ready, b * ST + (i - 1))
                elif i == 0 and isinstance(b, int):
                    pe.wait_ge(wv_loaded, 16)
                t = slice(i * P, (i + 1) * P)
                for k in range(KT):
                    nc.tensor.matmul(v_bank(i), xh[:, k, t], wv[:, :, 0, k], start=k == 0, stop=False)
                    nc.tensor.matmul(v_bank(i), xh[:, k, t], wv[:, :, 1, k], start=False, stop=False)
                    mm = nc.tensor.matmul(v_bank(i), xl[:, k, t], wv[:, :, 0, k], start=False, stop=k == KT - 1)
                mm.then_inc(v_filled, 1)

            def project_qk(u, f, r):
                pe.wait_ge(wqk_loaded, u.at(16, 16))
                pe.wait_ge(xl_ready, u.b * ST + ST)
                t = slice(f * QB, (f + 1) * QB)
                bank = qk_bank(f)[r]
                for k in range(KT):
                    nc.tensor.matmul(bank, wqk[:, r, 0, k], xh[:, k, t], start=k == 0, stop=False)
                    nc.tensor.matmul(bank, wqk[:, r, 0, k], xl[:, k, t], start=False, stop=False)
                    mm = nc.tensor.matmul(bank, wqk[:, r, 1, k], xh[:, k, t], start=False, stop=k == KT - 1)
                mm.then_inc(qk_filled, 1)

            def piece(u, c):
                h, (i, k0, k1) = c // len(PIECES), PIECES[c % len(PIECES)]
                if c == 0:
                    pe.wait_ge(placed, u.at(96, 96))
                if c >= 2:
                    pe.wait_ge(mx_read, u.at(NP, c - 1))
                diag = k1 == (i + 1) * P
                bank = w_bank[c % 2]
                if diag:
                    nc.tensor.matmul(bank[:, k1 - k0 - P:k1 - k0], ident_b[:], hide_k[:], start=True, stop=False,
                                     skip_group_check=True)
                nc.tensor.matmul(bank[:, 0:k1 - k0], qs[0:3 * HD, u.g % 2, h, i * P:(i + 1) * P],
                                 ks[0:3 * HD, u.g % 2, h, k0:k1], start=not diag, stop=True,
                                 skip_group_check=True).then_inc(mx_filled, 1)

            def turn_mrow(u):
                pe.wait_ge(mneg_ready, u.at(1, 1))
                nc.tensor.transpose(s_bank[0][0:GH * ST, 0, 0:P], mneg[:].rearrange("p h i -> p (h i)"),
                                    ident[:]).then_inc(mrow_turned, 1)

            def pieces(u, t, slot):
                if not exists(u.plus(1)):
                    return
                for c in slot_pieces(t, slot):
                    if c == 0 and exists(u.plus(2)):
                        pe.wait_ge(qk_read, u.plus(2).at(2, 2))
                    piece(u.plus(1), c)

            def scores(u, t, hp):
                qb, kt = STEPS[t]
                first = first_query(t)
                if t == 0 and hp == 0:
                    pe.wait_ge(mrow_placed, u.at(16, 16))
                if t == 0 and hp == 1 and exists(u.plus(2)):
                    pe.wait_ge(qk_read, u.plus(2).at(2, 1))
                if t > 0:
                    pe.wait_ge(exp_done, u.at(2 * NS, 2 * t + hp - 1))
                diag = kt * P >= qb * QB
                if diag:
                    for i in range(2):
                        nc.tensor.matmul(s_bank[hp][:, i, first:first + P], ident_b[:], hide_q[:], start=True, stop=False,
                                         skip_group_check=True)
                for h in (2 * hp, 2 * hp + 1):
                    mm = nc.tensor.matmul(s_bank[hp][:, h % 2, first:QB], ks[0:3 * HD + 1, u.g % 2, h, kt * P:(kt + 1) * P],
                                          qs[0:3 * HD + 1, u.g % 2, h, qb * QB + first:(qb + 1) * QB],
                                          start=not diag, stop=True, skip_group_check=True)
                mm.then_inc(s_filled, 1)

            def weigh(u, t, bank):
                qb, kt = STEPS[t]
                first = first_query(t)
                opening = kt == (qb + 1) * QB // P - 1
                if bank is pv_bank:
                    pe.wait_ge(exp_done, u.at(2 * NS, 2 * t + 2))
                    if opening and qb > 0:
                        pe.wait_ge(acc_copied, u.at(2, qb))
                        pe.wait_ge(den_copied, u.at(2, qb))
                for h in range(GH):
                    rows = slice(h * HD, (h + 1) * HD)
                    w = v[:, kt, u.g * P + h * HD:u.g * P + (h + 1) * HD] if bank is pv_bank else ones[:]
                    mm = nc.tensor.matmul(bank[rows, first:QB], w, probs[:, t % 2, h, first:QB], start=opening,
                                          stop=kt == 0, skip_group_check=True)
                if bank is den_bank:
                    mm.then_inc(pv_done, 1)

            def body(u):
                if u.g == 0:
                    pe.wait_ge(v_ready, u.b * ST + ST)
                if u.g == 1 and exists(u.plus(NG)):
                    pe.wait_ge(xl_ready, u.b * ST + 2 * ST)
                scores(u, 0, 0)
                scores(u, 0, 1)
                for t in range(NS):
                    if t + 1 < NS:
                        scores(u, t + 1, 0)
                    pieces(u, t, 0)
                    if t + 1 < NS:
                        scores(u, t + 1, 1)
                    pieces(u, t, 1)
                    weigh(u, t, pv_bank)
                    pieces(u, t, 2)
                    weigh(u, t, den_bank)
                    pieces(u, t, 3)
                if exists(u.plus(3)):
                    project_qk(u.plus(3), 0, 0)
                if exists(u.plus(1)):
                    turn_mrow(u.plus(1))
                if exists(u.plus(3)):
                    project_qk(u.plus(3), 0, 1)
                    pe.wait_ge(mx_read, u.plus(1).at(NP, NP))
                    project_qk(u.plus(3), 1, 0)
                    project_qk(u.plus(3), 1, 1)
                if u.g == 0 and exists(u.plus(NG)):
                    pe.wait_ge(qk_read, u.plus(3).at(2, 1))
                    pe.wait_ge(mrow_copied, u.plus(1).at(1, 1))
                    for i in range(ST):
                        turn(u.b + 1, i)
                if u.g == NG - 1 and exists(u.plus(NG)):
                    pe.wait_ge(qk_read, u.plus(3).at(2, 1))
                    for i in range(ST):
                        project_v(u.b + 1, i)

            pe.wait_ge(consts_ready, 4)
            for i in range(ST):
                turn(0, i)
            for f in range(2):
                project_qk(U0, f, 0)
                project_qk(U0, f, 1)
            pe.wait_ge(qk_read, 1)
            for i in range(ST):
                project_v(0, i)
            pe.wait_ge(v_ready, ST)
            pe.wait_ge(qk_read, 2)
            for f in range(2):
                project_qk(U0.plus(1), f, 0)
                project_qk(U0.plus(1), f, 1)
            pe.wait_ge(qk_read, 4)
            for c in range(NP):
                piece(U0, c)
            turn_mrow(U0)
            pe.wait_ge(mx_read, NP)
            for f in range(2):
                project_qk(U0.plus(2), f, 0)
                project_qk(U0.plus(2), f, 1)
            pe.wait_ge(ks_ready, 1)
            each_batch(pe, body)


def rope_tables():
    inv = 1.0 / np.power(np.float32(10000.0), np.arange(HALF, dtype=np.float32) / np.float32(HALF), dtype=np.float32)
    angle = np.outer(np.arange(SEQ, dtype=np.float32), inv.astype(np.float32)).astype(np.float32)
    return [np.ascontiguousarray(np.tile(f(angle).astype(np.float32).T, (P // HALF, 1))) for f in (np.cos, np.sin)]


def build(nc, a, out):
    x = a["x"].rearrange("b t d -> (b t) d")
    y = out.rearrange("b t d -> (b t) d")
    tokens = x.shape[0]
    nblocks, nbatch = tokens // TB, tokens // SEQ

    def scratch(name, shape, dt):
        return nc.dram_tensor(name, shape, dt, kind="Internal").ap()

    x1 = scratch("x1", [tokens, D], F32)
    moments = scratch("moments", [nblocks, P, TT, 6], F32)
    att = scratch("att", [D, tokens], F32)
    parts = scratch("weight_parts", [nblocks, P, 2 * D], F32)
    qk_parts = parts[0:2 * NG].rearrange("(g f) p x -> g p f x", f=2)
    rope_tmp = scratch("rope_tmp", [2, 2, 2 * P, SEQ], F32)
    mrow_tmp = scratch("mrow_tmp", [GH * ST, P], F32)
    with nc.psum_tensor("banks", [P, 8, D], F32) as psum:
        ffn_phase(nc, psum, "ffn1", nblocks, x, x1, a["router_w"], a["w_a"], a["w_b"], moments_dst=moments,
                  raw_src=a["w_qkvo"], parts_dst=parts)
        attention_phase(nc, psum, nbatch, x1, moments.rearrange("n p j c -> p n (j c)"), qk_parts, parts[2 * NG:3 * NG],
                        a["cos"], a["sin"], att, rope_tmp, mrow_tmp)
        ffn_phase(nc, psum, "ffn2", nblocks, x1, y, a["router_w"], a["w_a"], a["w_b"], y_src=att, wo_src=parts[3 * NG:])


def kernel(L0_attn_x, L0_attn_w_q, L0_attn_w_k, L0_attn_w_v, L0_attn_w_o, L0_ffn_router_w, L0_ffn_Wa, L0_ffn_Wb):
    import concourse.bacc as bacc
    from concourse.bass_utils import run_bass_kernel_spmd

    cos, sin = rope_tables()
    w_qk = np.stack([L0_attn_w_q, L0_attn_w_k]).reshape(2, NG, GH, 2, HALF, D).transpose(1, 3, 0, 2, 4, 5)
    w_qkvo = np.concatenate([w_qk.reshape(-1, D), L0_attn_w_v, L0_attn_w_o]).reshape(-1, P, D)
    arrays = {"x": L0_attn_x, "w_qkvo": w_qkvo,
              "router_w": L0_ffn_router_w, "w_a": L0_ffn_Wa, "w_b": L0_ffn_Wb, "cos": cos, "sin": sin}
    arrays = {k: np.ascontiguousarray(v) for k, v in arrays.items()}
    nc = bacc.Bacc("TRN2", target_bir_lowering=False, num_devices=1)
    a = {k: nc.dram_tensor(k, v.shape, mybir.dt.from_np(v.dtype), kind="ExternalInput").ap() for k, v in arrays.items()}
    out = nc.dram_tensor("out", arrays["x"].shape, F32, kind="ExternalOutput").ap()
    build(nc, a, out)
    result = run_bass_kernel_spmd(nc, [arrays], core_ids=[0])
    return result.results[0]["out"]
```
